# Optimizing a Trainium2 kernel written in Bass

```python
import numpy as np
import jax
import jax.numpy as jnp

def _softmax(x, axis=-1):
    return jax.nn.softmax(x, axis=axis)

def _gelu(x):
    return jax.nn.gelu(x, approximate=True)

def _silu(x):
    return jax.nn.silu(x)

def _sigmoid(x):
    return jax.nn.sigmoid(x)

def _layernorm(x, axis=-1, eps=1e-05):
    m = jnp.mean(x, axis=axis, keepdims=True)
    v = jnp.var(x, axis=axis, keepdims=True)
    return (x - m) / jnp.sqrt(v + eps)

def _scatter_add(tgt, idx, src, axis=0):
    return tgt.at[idx].add(src)

def _segment_sum(src, seg, n):
    return jax.ops.segment_sum(src, seg, n)
kernel_name = 'mk_gnn_resnorm_d2_gnn_r8_c3f2ab'

def setup_inputs(seed: int=0):
    np.random.seed(seed)
    _w = jnp.asarray

    def _rec_inputs():
        import jax
        import jax.numpy as jnp
        _gk = jax.random.key(seed)
        x = -0.0005121 + 1.001 * jax.random.normal(jax.random.fold_in(_gk, 1), (12500, 64), jnp.float32)
        src = jax.random.randint(jax.random.fold_in(_gk, 2), (200000,), 0, 12500, jnp.int32)
        dst = jax.random.randint(jax.random.fold_in(_gk, 3), (200000,), 0, 12500, jnp.int32)
        _o = jnp.argsort(dst, stable=True)
        src = src[_o]
        dst = dst[_o]
        edge_weight1 = 0.000614103 + 0.999867 * jax.random.normal(jax.random.fold_in(_gk, 12), (200000, 1), jnp.float32)
        return (x, src, dst, edge_weight1)
    x, src, dst, edge_weight1 = _rec_inputs()

    def _L0_gnn_setup():
        import jax, jax.numpy as jnp
        import numpy as np
        N, E, D_IN, D_H, D_OUT = (6250, 100000, 64, 64, 64)

        def _lin_params(key, d_in, d_out, bias=True, scale=0.05):
            kw, kb = jax.random.split(key)
            W = jax.random.normal(kw, (d_in, d_out), dtype=jnp.float32) * scale
            if bias:
                b = jax.random.normal(kb, (d_out,), dtype=jnp.float32) * scale
                return (W, b)
            return (W,)

        def transformer_conv(x, src, dst, edge_attr, Wq, bq, Wk, bk, Wv, bv, We, Ws, bs):
            d = Wq.shape[1]
            n = x.shape[0]
            q = x @ Wq + bq
            e = edge_attr @ We
            k = x[src] @ Wk + bk + e
            v = x[src] @ Wv + bv + e
            score = jnp.sum(q[dst] * k, axis=-1) / jnp.sqrt(jnp.asarray(d, x.dtype))
            m = jax.ops.segment_max(score, dst, num_segments=n)
            a = jnp.exp(score - m[dst])
            denom = jax.ops.segment_sum(a, dst, num_segments=n)
            alpha = a / denom[dst]
            out = jax.ops.segment_sum(alpha[:, None] * v, dst, num_segments=n)
            return out + x @ Ws + bs
        key = jax.random.key(seed)
        ks = jax.random.split(key, 12)
        x = jax.random.normal(ks[0], (N, D_IN), dtype=jnp.float32)
        edge_index = jax.random.randint(ks[1], (2, E), 0, N, dtype=jnp.int64)
        edge_attr = jax.random.normal(ks[2], (E, 1), dtype=jnp.float32)
        Wq1, bq1 = _lin_params(ks[3], D_IN, D_H)
        Wk1, bk1 = _lin_params(ks[4], D_IN, D_H)
        Wv1, bv1 = _lin_params(ks[5], D_IN, D_H)
        We1, = _lin_params(ks[6], 1, D_H, bias=False)
        Ws1, bs1 = _lin_params(ks[7], D_IN, D_H)
        Wq2, bq2 = _lin_params(ks[8], D_H, D_OUT)
        Wk2, bk2 = _lin_params(ks[9], D_H, D_OUT)
        Wv2, bv2 = _lin_params(ks[10], D_H, D_OUT)
        We2, = _lin_params(jax.random.fold_in(key, 100), 1, D_OUT, bias=False)
        Ws2, bs2 = _lin_params(ks[11], D_H, D_OUT)
        return dict(x=x, edge_index=edge_index, edge_attr=edge_attr, Wq1=Wq1, bq1=bq1, Wk1=Wk1, bk1=bk1, Wv1=Wv1, bv1=bv1, We1=We1, Ws1=Ws1, bs1=bs1, Wq2=Wq2, bq2=bq2, Wk2=Wk2, bk2=bk2, Wv2=Wv2, bv2=bv2, We2=We2, Ws2=Ws2, bs2=bs2)
    _L0_gnn_all = _L0_gnn_setup()
    _L0_gnn_in = {k: v for k, v in _L0_gnn_all.items() if k in ('Wq1', 'bq1', 'Wk1', 'bk1', 'Wv1', 'bv1', 'We1', 'Ws1', 'bs1', 'Wq2', 'bq2', 'Wk2', 'bk2', 'Wv2', 'bv2', 'We2', 'Ws2', 'bs2')}
    del _L0_gnn_all

    def _L1_gnn_setup():
        import jax, jax.numpy as jnp
        import numpy as np
        N, E, D, H = (6250, 62500, 64, 8)
        LN_EPS = 1e-05
        SM_EPS = 1e-16
        SLOPE = 0.2

        def layer_norm(x, g, b):
            mu = jnp.mean(x, axis=-1, keepdims=True)
            var = jnp.mean((x - mu) ** 2, axis=-1, keepdims=True)
            return (x - mu) * jax.lax.rsqrt(var + LN_EPS) * g + b
        key = jax.random.key(seed)
        ks = jax.random.split(key, 12)
        glorot = lambda k, shape: jax.random.normal(k, shape, jnp.float32) * np.sqrt(2.0 / (shape[0] + shape[-1]))
        return {'x': jax.random.normal(ks[0], (N, D), jnp.float32), 'edge_index': jax.random.randint(ks[1], (2, E), 0, N, jnp.int64), 'W_att': glorot(ks[2], (D, H * D)), 'att_src': glorot(ks[3], (H, D)), 'att_dst': glorot(ks[4], (H, D)), 'bias_att': jnp.zeros((D,), jnp.float32), 'W1': glorot(ks[5], (D, 2 * D)), 'b1': jnp.zeros((2 * D,), jnp.float32), 'W2': glorot(ks[6], (2 * D, D)), 'b2': jnp.zeros((D,), jnp.float32), 'ln1_g': jnp.ones((D,), jnp.float32), 'ln1_b': jnp.zeros((D,), jnp.float32), 'ln2_g': jnp.ones((D,), jnp.float32), 'ln2_b': jnp.zeros((D,), jnp.float32)}
    _L1_gnn_all = _L1_gnn_setup()
    _L1_gnn_in = {k: v for k, v in _L1_gnn_all.items() if k in ('W_att', 'att_src', 'att_dst', 'bias_att', 'W1', 'b1', 'W2', 'b2', 'ln1_g', 'ln1_b', 'ln2_g', 'ln2_b')}
    del _L1_gnn_all
    return {'x': x, 'src': src, 'dst': dst, 'edge_weight1': edge_weight1, 'L0_gnn_Wq1': _L0_gnn_in['Wq1'], 'L0_gnn_bq1': _L0_gnn_in['bq1'], 'L0_gnn_Wk1': _L0_gnn_in['Wk1'], 'L0_gnn_bk1': _L0_gnn_in['bk1'], 'L0_gnn_Wv1': _L0_gnn_in['Wv1'], 'L0_gnn_bv1': _L0_gnn_in['bv1'], 'L0_gnn_We1': _L0_gnn_in['We1'], 'L0_gnn_Ws1': _L0_gnn_in['Ws1'], 'L0_gnn_bs1': _L0_gnn_in['bs1'], 'L0_gnn_Wq2': _L0_gnn_in['Wq2'], 'L0_gnn_bq2': _L0_gnn_in['bq2'], 'L0_gnn_Wk2': _L0_gnn_in['Wk2'], 'L0_gnn_bk2': _L0_gnn_in['bk2'], 'L0_gnn_Wv2': _L0_gnn_in['Wv2'], 'L0_gnn_bv2': _L0_gnn_in['bv2'], 'L0_gnn_We2': _L0_gnn_in['We2'], 'L0_gnn_Ws2': _L0_gnn_in['Ws2'], 'L0_gnn_bs2': _L0_gnn_in['bs2'], 'L1_gnn_W_att': _L1_gnn_in['W_att'], 'L1_gnn_att_src': _L1_gnn_in['att_src'], 'L1_gnn_att_dst': _L1_gnn_in['att_dst'], 'L1_gnn_bias_att': _L1_gnn_in['bias_att'], 'L1_gnn_W1': _L1_gnn_in['W1'], 'L1_gnn_b1': _L1_gnn_in['b1'], 'L1_gnn_W2': _L1_gnn_in['W2'], 'L1_gnn_b2': _L1_gnn_in['b2'], 'L1_gnn_ln1_g': _L1_gnn_in['ln1_g'], 'L1_gnn_ln1_b': _L1_gnn_in['ln1_b'], 'L1_gnn_ln2_g': _L1_gnn_in['ln2_g'], 'L1_gnn_ln2_b': _L1_gnn_in['ln2_b']}

def reference(x, src, dst, edge_weight1, L0_gnn_Wq1, L0_gnn_bq1, L0_gnn_Wk1, L0_gnn_bk1, L0_gnn_Wv1, L0_gnn_bv1, L0_gnn_We1, L0_gnn_Ws1, L0_gnn_bs1, L0_gnn_Wq2, L0_gnn_bq2, L0_gnn_Wk2, L0_gnn_bk2, L0_gnn_Wv2, L0_gnn_bv2, L0_gnn_We2, L0_gnn_Ws2, L0_gnn_bs2, L1_gnn_W_att, L1_gnn_att_src, L1_gnn_att_dst, L1_gnn_bias_att, L1_gnn_W1, L1_gnn_b1, L1_gnn_W2, L1_gnn_b2, L1_gnn_ln1_g, L1_gnn_ln1_b, L1_gnn_ln2_g, L1_gnn_ln2_b):
    import jax
    import jax.numpy as jnp

    def _L0_gnn_ref(x, edge_index, edge_attr, Wq1, bq1, Wk1, bk1, Wv1, bv1, We1, Ws1, bs1, Wq2, bq2, Wk2, bk2, Wv2, bv2, We2, Ws2, bs2):
        import jax, jax.numpy as jnp
        import numpy as np
        N, E, D_IN, D_H, D_OUT = (6250, 100000, 64, 64, 64)

        def _lin_params(key, d_in, d_out, bias=True, scale=0.05):
            kw, kb = jax.random.split(key)
            W = jax.random.normal(kw, (d_in, d_out), dtype=jnp.float32) * scale
            if bias:
                b = jax.random.normal(kb, (d_out,), dtype=jnp.float32) * scale
                return (W, b)
            return (W,)

        def transformer_conv(x, src, dst, edge_attr, Wq, bq, Wk, bk, Wv, bv, We, Ws, bs):
            d = Wq.shape[1]
            n = x.shape[0]
            q = x @ Wq + bq
            e = edge_attr @ We
            k = x[src] @ Wk + bk + e
            v = x[src] @ Wv + bv + e
            score = jnp.sum(q[dst] * k, axis=-1) / jnp.sqrt(jnp.asarray(d, x.dtype))
            m = jax.ops.segment_max(score, dst, num_segments=n)
            a = jnp.exp(score - m[dst])
            denom = jax.ops.segment_sum(a, dst, num_segments=n)
            alpha = a / denom[dst]
            out = jax.ops.segment_sum(alpha[:, None] * v, dst, num_segments=n)
            return out + x @ Ws + bs
        src, dst = (edge_index[0], edge_index[1])
        h = transformer_conv(x, src, dst, edge_attr, Wq1, bq1, Wk1, bk1, Wv1, bv1, We1, Ws1, bs1)
        h = jax.nn.relu(h)
        out = transformer_conv(h, src, dst, edge_attr, Wq2, bq2, Wk2, bk2, Wv2, bv2, We2, Ws2, bs2)
        return out

    def _L1_gnn_ref(x, edge_index, W_att, att_src, att_dst, bias_att, W1, b1, W2, b2, ln1_g, ln1_b, ln2_g, ln2_b):
        import jax, jax.numpy as jnp
        import numpy as np
        N, E, D, H = (6250, 62500, 64, 8)
        LN_EPS = 1e-05
        SM_EPS = 1e-16
        SLOPE = 0.2

        def layer_norm(x, g, b):
            mu = jnp.mean(x, axis=-1, keepdims=True)
            var = jnp.mean((x - mu) ** 2, axis=-1, keepdims=True)
            return (x - mu) * jax.lax.rsqrt(var + LN_EPS) * g + b
        n = x.shape[0]
        h = (x @ W_att).reshape(n, H, D)
        a_src = jnp.einsum('nhc,hc->nh', h, att_src)
        a_dst = jnp.einsum('nhc,hc->nh', h, att_dst)
        loops = jnp.arange(n, dtype=edge_index.dtype)
        src = jnp.concatenate([edge_index[0], loops])
        dst = jnp.concatenate([edge_index[1], loops])
        e = a_src[src] + a_dst[dst]
        e = jnp.where(e > 0, e, SLOPE * e)
        m = jax.ops.segment_max(e, dst, num_segments=n)
        e = jnp.exp(e - m[dst])
        s = jax.ops.segment_sum(e, dst, num_segments=n)
        alpha = e / (s[dst] + SM_EPS)
        msg = alpha[:, :, None] * h[src]
        out = jax.ops.segment_sum(msg, dst, num_segments=n)
        att_out = out.mean(axis=1) + bias_att
        x1 = layer_norm(att_out + x, ln1_g, ln1_b)
        ff = jax.nn.relu(x1 @ W1 + b1) @ W2 + b2
        return layer_norm(ff + x1, ln2_g, ln2_b)
    edge_index = jnp.stack([src, dst])
    x = _layernorm(x + _L0_gnn_ref(x, edge_index, edge_weight1, L0_gnn_Wq1, L0_gnn_bq1, L0_gnn_Wk1, L0_gnn_bk1, L0_gnn_Wv1, L0_gnn_bv1, L0_gnn_We1, L0_gnn_Ws1, L0_gnn_bs1, L0_gnn_Wq2, L0_gnn_bq2, L0_gnn_Wk2, L0_gnn_bk2, L0_gnn_Wv2, L0_gnn_bv2, L0_gnn_We2, L0_gnn_Ws2, L0_gnn_bs2), axis=-1)
    x = _layernorm(x + _L1_gnn_ref(x, edge_index, L1_gnn_W_att, L1_gnn_att_src, L1_gnn_att_dst, L1_gnn_bias_att, L1_gnn_W1, L1_gnn_b1, L1_gnn_W2, L1_gnn_b2, L1_gnn_ln1_g, L1_gnn_ln1_b, L1_gnn_ln2_g, L1_gnn_ln2_b), axis=-1)
    return x

_drawn_inputs = setup_inputs


def setup_inputs(seed=0):
    import zlib

    import numpy as np

    out = dict(_drawn_inputs(seed))
    spreads = {'L1_gnn_bias_att': (0.0, 0.1),
     'L1_gnn_b1': (0.0, 0.1),
     'L1_gnn_b2': (0.0, 0.1),
     'L1_gnn_ln1_g': (1.0, 0.2),
     'L1_gnn_ln1_b': (0.0, 0.1),
     'L1_gnn_ln2_g': (1.0, 0.2),
     'L1_gnn_ln2_b': (0.0, 0.1)}
    factors = {'edge_weight1': 4.714,
     'L0_gnn_Wq1': 8.0,
     'L0_gnn_bq1': 8.0,
     'L0_gnn_Wk1': 8.0,
     'L0_gnn_bk1': 8.0,
     'L0_gnn_bv1': 3.213,
     'L0_gnn_We1': 8.0,
     'L0_gnn_bs1': 3.017,
     'L0_gnn_Wq2': 8.0,
     'L0_gnn_bq2': 8.0,
     'L0_gnn_Wk2': 8.0,
     'L0_gnn_bk2': 8.0,
     'L0_gnn_We2': 4.374,
     'L1_gnn_att_src': 4.641,
     'L1_gnn_att_dst': 8.0}
    for name, (base, spread) in spreads.items():
        noise = np.random.default_rng([zlib.crc32(name.encode()), seed]).standard_normal(out[name].shape)
        drawn = base * np.exp(spread * noise) if base else spread * noise
        out[name] = jnp.asarray(drawn.astype(out[name].dtype))
    for name, factor in factors.items():
        out[name] = (out[name] * factor).astype(out[name].dtype)
    return out
```

```python
import concourse.bass as bass
from concourse import mybir
from contextlib import ExitStack

F32 = mybir.dt.float32
I32 = mybir.dt.int32
ALU = mybir.AluOpType
ACT = mybir.ActivationFunctionType
AX = mybir.AxisListType
SP_ENGINE = mybir.EngineType.SP
PE_ENGINE = mybir.EngineType.PE

P = 128
N = 12500
E = 200000
D = 64
H = 8
DA = D + 2
NT = -(-N // P)
ET = -(-E // P)
N_PAD = NT * P
E_PAD = (ET + 1) * P
NODE_PAD = 1 << 20
STEPS = 13 * P
KC = STEPS // P
assert STEPS >= ET + NT - 1 and STEPS - NT < ET + P
GT = 7
NG = NT // GT
assert NT % GT == 0 and NG % 2 == 0
GATE_W = 3 * P + 1
BIG = 1.0e30
LN_EPS = 1e-5
SM_EPS = 1e-16
SLOPE = 0.2
WC = H * D + 2 * H


def until(engine, sem, value):
    engine.wait_ge(sem, value)
    engine.nop(nofuse=True)


class Tools:

    def __init__(self, nc, ctx, part):
        self.nc, self.ctx, self.part, self.sems = nc, ctx, part, []
        ctx.callback(self.clear)

    def clear(self):
        if self.sems:
            self.nc.clear_and_free_semaphores(self.sems)
            self.nc.all_engine_barrier()

    def sb(self, name, shape, dt=F32):
        return self.ctx.enter_context(self.nc.sbuf_tensor(f"{self.part}_{name}", shape, dt))

    def ps(self, name, shape, dt=F32):
        return self.ctx.enter_context(self.nc.psum_tensor(f"{self.part}_{name}", shape, dt))

    def sem(self, name):
        self.sems.append(self.nc.alloc_semaphore(f"{self.part}_{name}"))
        return self.sems[-1]


def build_schedule(nc, K, src_d, dst_d, w_d, dram):
    with ExitStack() as ctx:
        T = Tools(nc, ctx, "sch")
        sb, ps, sem = T.sb, T.ps, T.sem
        last_dst = sb("last_dst", [1, ET], I32)
        last_tile_i = sb("last_tile_i", [1, ET], I32)
        last_tile = sb("last_tile", [1, ET])
        tile_no = sb("tile_no", [P, ET])
        J = sb("J", [P, ET])
        L = sb("L", [P, ET])
        junk = sb("junk", [P, ET])
        step_no = sb("step_no", [P, KC])
        part_no = sb("part_no", [P, 1])
        i_of = sb("i_of", [P, KC])
        i_int = sb("i_int", [P, KC], I32)
        j_of = sb("j_of", [P, KC])
        j_base = sb("j_base", [P, KC])
        diag = sb("diag", [P, KC, P])
        j_row = sb("j_row", [P, STEPS])
        is_last = sb("is_last", [1, STEPS])
        end_of = sb("end_of", [P, 1])
        end_int = sb("end_int", [P, 1], I32)
        end_slot_i = sb("end_slot_i", [P, 1], I32)
        end_slot = sb("end_slot", [P, 1])
        end_row = sb("end_row", [P, 1])
        end_diag = sb("end_diag", [P, P])
        slot_off = sb("slot_off", [P, 1])
        src_r = sb("src_r", [P, KC, P], I32)
        dst_r = sb("dst_r", [P, KC, P], I32)
        w_r = sb("w_r", [P, KC, P])
        src_f = sb("src_f", [P, KC, P])
        dst_f = sb("dst_f", [P, KC, P])
        rel = sb("rel", [P, KC, P])
        prev_f = sb("prev_f", [P, KC, P])
        gate = sb("gate", [P, KC, P])
        mask = sb("mask", [P, KC, P])
        over = sb("over", [P, KC, P])
        minus1 = sb("minus1", [1, P])
        minus_big = sb("minus_big", [1, P])
        wide = ps("wide", [P, 2048])
        turned = ps("turned", [P, 4, 512])

        last_in = sem("last_in")
        iotas = sem("iotas")
        dve = sem("dve")
        j_bcast = sem("j_bcast")
        steps_ok = sem("steps_ok")
        diag_ok = sem("diag_ok")
        row_ok = sem("row_ok")
        end_ok = sem("end_ok")
        endb_ok = sem("endb_ok")
        rows_in = sem("rows_in")
        dst_ready = sem("dst_ready")
        dst_out = sem("dst_out")
        pads_out = sem("pads_out")
        prev_in = sem("prev_in")
        gates_ready = sem("gates_ready")
        gates_out = sem("gates_out")
        turn_ready = sem("turn_ready")
        turned_ok = sem("turned_ok")
        kept_ok = sem("kept_ok")

        groups = [(a, c0) for a in range(3) for c0 in range(0, KC, 4)]
        block = ctx.enter_context(nc.Block())

        @block.sync
        def _(sp):
            with nc.allow_non_contiguous_dma(reason="one element of each edge tile"):
                sp.dma_start(last_dst[:], dst_d[0:ET, P - 1:P].rearrange("t a -> a t")).then_inc(last_in, 16)
            sp.wait_ge(iotas, 7)
            sp.dma_start(dram["dst_flat"][0:P].rearrange("(a e) -> a e", a=1), minus1[:]).then_inc(pads_out, 16)
            sp.wait_ge(dst_ready, 1)
            sp.dma_start(dram["dst_flat"][P:P + STEPS * P].rearrange("(c p e) -> p c e", p=P, e=P),
                         dst_f[:]).then_inc(dst_out, 16)
            sp.wait_ge(dst_out, 16)
            sp.wait_ge(pads_out, 16)
            sp.dma_start(prev_f[:], dram["dst_flat"][P - 1:P - 1 + STEPS * P]
                         .rearrange("(c p e) -> p c e", p=P, e=P)).then_inc(prev_in, 16)
            sp.wait_ge(gates_ready, 2)
            rows = dram["gates"].rearrange("(c p) w -> p c w", p=P)
            stored = 0
            with nc.allow_non_contiguous_dma(reason="single elements of each step"):
                for out, in_ in (
                        (rows[:, :, 0:P], gate[:]),
                        (rows[:, :, P:2 * P - 1], gate[:, :, 1:]),
                        (dram["gates"][0:P - 1, 2 * P - 1:2 * P], gate[1:P, 0, 0:1]),
                        (dram["gates"][P - 1:STEPS - 1, 2 * P - 1:2 * P].rearrange("(c p) w -> p c w", p=P),
                         gate[:, 1:, 0:1]),
                        (dram["gates"][STEPS - 1:STEPS, 2 * P - 1:2 * P], minus_big[:, 0:1]),
                        (rows[:, :, 2 * P:3 * P], mask[:]),
                        (rows[:, :, 3 * P:], rel[:, :, 0:1])):
                    sp.dma_start(out, in_).then_inc(gates_out, 16)
                    stored += 16
            sp.wait_ge(gates_out, stored)

        @block.gpsimd
        def _(pool):
            nc.gpsimd.iota(tile_no[:], [[1, ET]], base=0, channel_multiplier=0,
                           allow_small_or_imprecise_dtypes=True).then_inc(iotas, 1)
            nc.gpsimd.iota(step_no[:], [[P, KC]], base=0, channel_multiplier=1,
                           allow_small_or_imprecise_dtypes=True).then_inc(iotas, 1)
            nc.gpsimd.iota(part_no[:], [[1, 1]], base=0, channel_multiplier=1,
                           allow_small_or_imprecise_dtypes=True).then_inc(iotas, 1)
            nc.gpsimd.iota(K["node_no"][:], [[1, P]], base=0, channel_multiplier=0,
                           allow_small_or_imprecise_dtypes=True).then_inc(iotas, 1)
            nc.gpsimd.memset(K["ones"][:], 1.0).then_inc(iotas, 1)
            nc.gpsimd.memset(minus1[:], -1.0).then_inc(iotas, 1)
            nc.gpsimd.memset(minus_big[:], -BIG).then_inc(iotas, 1)
            pool.wait_ge(steps_ok, 1)
            for c in range(KC):
                for rows, table in ((src_r, src_d), (dst_r, dst_d), (w_r, w_d)):
                    pool.indirect_dma_start(
                        out=rows[:, c, :], out_offset=None, in_=table,
                        in_offset=bass.IndirectOffsetOnAxis(ap=i_int[:, c:c + 1], axis=0)).then_inc(rows_in, 16)

        @block.tensor
        def _(pe):
            pe.wait_ge(dve, 3)
            for a in range(0, ET, 512):
                b = min(a + 512, ET)
                mm = nc.tensor.matmul(wide[:, a:b], K["ones"][0:1, :], last_tile[0:1, a:b], start=True, stop=True)
            mm.then_inc(j_bcast, 1)
            pe.wait_ge(diag_ok, 1)
            flat = diag[:].rearrange("p c e -> p (c e)")
            for a in range(0, STEPS, 512):
                b = min(a + 512, STEPS)
                mm = nc.tensor.matmul(wide[:, a:b], K["ones"][:], flat[:, a:b], start=True, stop=True)
            mm.then_inc(row_ok, 1)
            pe.wait_ge(end_ok, 1)
            nc.tensor.matmul(turned[:, 3, 0:P], K["ones"][:], end_diag[:], start=True, stop=True).then_inc(endb_ok, 1)
            for n, (a, c0) in enumerate(groups):
                rows = (src_f, rel, w_r)[a]
                pe.wait_ge(turn_ready, 1)
                if n >= 3:
                    pe.wait_ge(kept_ok, n - 2)
                for c in range(c0, min(c0 + 4, KC)):
                    mm = nc.tensor.transpose(turned[:, n % 3, (c - c0) * P:(c - c0 + 1) * P], rows[:, c, :],
                                             K["ident"][:])
                mm.then_inc(turned_ok, 1)

        @block.vector
        def _(v):
            count = [0]

            def then(ins):
                count[0] += 1
                ins.then_inc(dve, 1)
                v.wait_ge(dve, count[0])

            v.wait_ge(iotas, 7)
            then(nc.vector.tensor_scalar(K["ident"][:], K["node_no"][:], part_no[:, 0:1], None, ALU.is_equal))
            v.wait_ge(last_in, 16)
            then(nc.vector.tensor_scalar(last_tile_i[:], last_dst[:], 7, None, ALU.arith_shift_right))
            then(nc.vector.tensor_scalar(last_tile[:], last_tile_i[:], float(NT - 1), None, ALU.min))
            v.wait_ge(j_bcast, 1)
            then(nc.vector.tensor_copy(J[:], wide[:, 0:ET]))
            then(nc.vector.tensor_tensor(L[:], J[:], tile_no[:], ALU.add))
            for c in range(KC):
                then(nc.vector.tensor_scalar(junk[:], L[:], step_no[:, c:c + 1], 0.0, ALU.is_lt, ALU.add,
                                             accum_out=i_of[:, c:c + 1]))
            then(nc.vector.tensor_scalar(junk[:], J[:], part_no[:, 0:1], 0.0, ALU.is_le, ALU.add,
                                         accum_out=end_of[:]))
            then(nc.vector.tensor_scalar(end_of[:], end_of[:], part_no[:, 0:1], float(STEPS - 1), ALU.add, ALU.min))
            nc.vector.tensor_copy(i_int[:], i_of[:]).then_inc(steps_ok, 1)
            then(nc.vector.tensor_tensor(j_of[:], step_no[:], i_of[:], ALU.subtract))
            then(nc.vector.tensor_scalar(j_of[:], j_of[:], float(NT - 1), None, ALU.min))
            then(nc.vector.tensor_scalar(j_base[:], j_of[:], float(P), None, ALU.mult))
            nc.vector.tensor_tensor(diag[:], K["ident"][:].unsqueeze(1).to_broadcast([P, KC, P]),
                                    j_of[:].unsqueeze(2).to_broadcast([P, KC, P]), ALU.mult).then_inc(diag_ok, 1)
            then(nc.vector.tensor_copy(end_int[:], end_of[:]))
            then(nc.vector.tensor_scalar(end_slot_i[:], end_int[:], GA - 1, None, ALU.bitwise_and))
            then(nc.vector.tensor_copy(end_slot[:], end_slot_i[:]))
            then(nc.vector.tensor_scalar(end_row[:], end_of[:], float(P), None, ALU.mult))
            then(nc.vector.scalar_tensor_tensor(out=end_row[:], in0=end_slot[:], scalar=float(1 - P), in1=end_row[:],
                                                op0=ALU.mult, op1=ALU.add))
            nc.vector.tensor_scalar(end_diag[:], K["ident"][:], end_row[:, 0:1], None, ALU.mult).then_inc(end_ok, 1)
            then(nc.vector.tensor_scalar(slot_off[:], part_no[:], float(GA), None, ALU.mult))
            v.wait_ge(row_ok, 1)
            then(nc.vector.tensor_copy(j_row[:], wide[:, 0:STEPS]))
            nc.vector.memset(K["keep"][:, 0:1], 0.0)
            nc.vector.tensor_tensor(K["keep"][:, 1:], j_row[:, 1:], j_row[:, 0:STEPS - 1], ALU.is_equal)
            nc.vector.tensor_copy(K["j_int"][:, 0:STEPS], j_row[0:1, :])
            then(nc.vector.memset(is_last[:, STEPS - 1:STEPS], 1.0))
            then(nc.vector.tensor_tensor(is_last[:, 0:STEPS - 1], j_row[0:1, 1:], j_row[0:1, 0:STEPS - 1],
                                         ALU.not_equal))
            nc.vector.tensor_copy(K["last_int"][:, 0:STEPS], is_last[:])
            v.wait_ge(endb_ok, 1)
            then(nc.vector.tensor_scalar(K["end_idx"][:], turned[:, 3, 0:NT], slot_off[:, 0:1], None, ALU.add))
            v.wait_ge(rows_in, 16 * 3 * KC)
            nc.vector.tensor_copy(src_f[:], src_r[:])
            then(nc.vector.tensor_copy(dst_f[:], dst_r[:]))
            v.nop(nofuse=True).then_inc(dst_ready, 1)
            then(nc.vector.tensor_tensor(rel[:], dst_f[:], j_base[:].unsqueeze(2).to_broadcast([P, KC, P]),
                                         ALU.subtract))
            v.nop(nofuse=True).then_inc(turn_ready, 1)
            then(nc.vector.tensor_scalar(mask[:], rel[:], 0.0, -BIG, ALU.is_lt, ALU.mult))
            then(nc.vector.tensor_scalar(over[:], rel[:], float(P), -BIG, ALU.is_ge, ALU.mult))
            nc.vector.tensor_tensor(mask[:], mask[:], over[:], ALU.add).then_inc(gates_ready, 1)
            v.wait_ge(prev_in, 16)
            then(nc.vector.tensor_tensor(gate[:], dst_f[:], prev_f[:], ALU.not_equal))
            nc.vector.tensor_scalar(gate[:], gate[:], -BIG, None, ALU.mult).then_inc(gates_ready, 1)
            for n, (a, c0) in enumerate(groups):
                v.wait_ge(turned_ok, n + 1)
                c1 = min(c0 + 4, KC)
                nc.vector.tensor_copy((K["src_idx"], K["rel"], K["w"])[a][:, c0 * P:c1 * P],
                                      turned[:, n % 3, 0:(c1 - c0) * P]).then_inc(kept_ok, 1)


GA = 32
GC = 16


def edge_phase(nc, K, part, heads, features, feat_w, tab_d, tab_w, dram, out_d):
    G = GA if heads == 1 else GC
    R = heads * G
    NB = max(1, R // 32)
    HB = 32 // G if heads > 1 else 1
    chunks = STEPS // G
    assert STEPS % (2 * G) == 0 and R in (32, 128)
    gat_w = feat_w
    row_w = DA if heads == 1 else gat_w
    sum_w = DA if heads == 1 else WC
    with ExitStack() as ctx:
        T = Tools(nc, ctx, part)
        sb, ps, sem = T.sb, T.ps, T.sem
        X = sb("X", [P, 2, G, row_w])
        M = sb("M", [P, 2, G, P])
        MT = sb("MT", [P, 2, P])
        tab = sb("tab", [P, NT, tab_w])
        idx = sb("idx", [P, 2, G], I32)
        rel = sb("rel", [P, 2, G])
        keep = sb("keep", [P, 2, G])
        junk = sb("junk", [P, 4, DA])
        score = sb("score", [P, G * heads])
        gates = sb("gates", [R, 2, GATE_W])
        gate_f, gate_b, maskr, frel = (gates[:, :, n * P:min((n + 1) * P, GATE_W)] for n in range(4))
        raw = sb("raw", [R, P])
        S = sb("S", [R, P])
        fwd = sb("fwd", [R, P])
        fwd2 = sb("fwd2", [R, P])
        bwd = sb("bwd", [R, P])
        top = sb("top", [R, P])
        wts = sb("wts", [R, P])
        ends = sb("ends", [R, 64])
        endsT = sb("endsT", [R, 64])
        run = sb("run", [R, 32])
        shift = sb("shift", [R, 32])
        cin = sb("cin", [R, 32])
        bin_ = sb("bin", [R, 32])
        carry = sb("carry", [R, HB])
        inj = sb("inj", [R, HB])
        dlt = sb("dlt", [R, 1])
        V = sb("V", [R, P])
        head_sel = sb("head_sel", [R, heads])
        wtT = sb("wtT", [P, R])
        fac = sb("fac", [P, heads])
        kfac = sb("kfac", [P, 1])
        if heads == 1:
            aX = sb("aX", [P, 2, row_w])
            acc = sb("acc", [P, 2, G, sum_w])
            pE = ps("pE", [P, 2, 512])
            pS = ps("pS", [P, 2, 512])
        else:
            aX = sb("aX", [P, 2, sum_w])
            acc = sb("acc", [P, 4, sum_w])
            last = sb("last", [P, sum_w])
            selfs = sb("selfs", [P, G * heads])
            score2 = sb("score2", [P, G * heads])
            raw2 = sb("raw2", [R, P])
            S2 = sb("S2", [R, P])
            wts2 = sb("wts2", [R, P])
            wtT2 = sb("wtT2", [P, R])
            pE = ps("pE", [P, 1, 512])
            pS = ps("pS", [P, 2, 1024])
        pMT = ps("pMT", [P, 2, 512])
        pT = ps("pT", [P, 2 if heads == 1 else 1, 512])
        p_fac = pT[:, 1, 0:heads] if heads == 1 else pE[:, 0, 512 - heads:512]

        rows_in = [sem(f"rows_in{b}") for b in (0, 1)]
        tab_in = sem("tab_in")
        gates_in = [sem(f"gates_in{b}") for b in (0, 1)]
        slot_free = sem("slot_free")
        scored = sem("scored")
        idx_copied = sem("idx_copied")
        small_ok = sem("small_ok")
        m_ok = sem("m_ok")
        mt_ps = sem("mt_ps")
        mt_ok = sem("mt_ok")
        spread = sem("spread")
        read_e = sem("read_e")
        score_ok = sem("score_ok")
        score_ps = sem("score_ps")
        diff_ok = sem("diff_ok")
        wts_ok = sem("wts_ok")
        wt_ps = sem("wt_ps")
        v_ok = sem("v_ok")
        fac_ps = sem("fac_ps")
        fac_ok = sem("fac_ok")
        wtT_ok = sem("wtT_ok")
        ax_dve = sem("ax_dve")
        ax_ok = sem("ax_ok")
        sum_ps = sem("sum_ps")
        sum_ok = sem("sum_ok")
        out_done = [sem(f"out{b}") for b in range(2 if heads == 1 else 4)]
        dve = sem("dve")
        act = sem("act")
        HD = H * D
        HA = 3

        block = ctx.enter_context(nc.Block())

        def pair(engine):
            return engine.Fori(0, chunks // 2)

        @block.gpsimd
        def _(pool):
            nc.gpsimd.memset(head_sel[:], 1.0).then_inc(small_ok, 1)
            pool.wait_ge(small_ok, 1)
            for h in range(heads):
                nc.gpsimd.affine_select(out=head_sel[:, h:h + 1], in_=head_sel[:, h:h + 1], pattern=[[0, 1]],
                                        compare_op=ALU.is_equal, fill=0.0, base=-h * G,
                                        channel_multiplier=1).then_inc(small_ok, 1)
            with pair(pool) as i:
                for b in (0, 1):
                    until(pool, slot_free, i * 2 + b + 1)
                    nc.gpsimd.tensor_copy(idx[:, b, :],
                                          K["src_idx"][:, bass.ds(i * (2 * G) + b * G, G)]).then_inc(idx_copied, 1)
                    until(pool, idx_copied, i * 2 + b + 1)
                    for g in range(G):
                        pool.indirect_dma_start(
                            out=X[:, b, g, 0:gat_w], out_offset=None, in_=features,
                            in_offset=bass.IndirectOffsetOnAxis(ap=idx[:, b, g:g + 1], axis=0)
                        ).then_inc(rows_in[b], 16)

        @block.sync
        def _(sp):
            sp.dma_start(tab[:], tab_d.rearrange("(t p) w -> p t w", p=P)).then_inc(tab_in, 16)
            with pair(sp) as i:
                for b in (0, 1):
                    k0 = i * (2 * G) + b * G
                    until(sp, scored, i * 2 + b + 1)

                    for h in range(heads):
                        sp.dma_start(gates[h * G:(h + 1) * G, b, :],
                                     dram["gates"][bass.ds(k0, G), :]).then_inc(gates_in[b], 16)
                    if heads == 1:
                        until(sp, sum_ok, i * (2 * G) + (b + 1) * G)
                        sp.dma_start(out_d[bass.ds(i * 2 + b, 1)].rearrange("a p g w -> p (a g w)"),
                                     acc[:, b, :, :].rearrange("p g w -> p (g w)")).then_inc(out_done[b], 16)
                    else:
                        _, tiles = nc.values_load_multi_w_load_instructions(
                            K["j_int"][0:1, bass.ds(k0, G)], engines=[SP_ENGINE], min_val=0, max_val=NT - 1,
                            skip_runtime_bounds_check_because="j of a step is at most NT - 1")
                        _, lasts = nc.values_load_multi_w_load_instructions(
                            K["last_int"][0:1, bass.ds(k0, G)], engines=[SP_ENGINE], min_val=0, max_val=1,
                            skip_runtime_bounds_check_because="a flag")
                        for g in range(G):
                            until(sp, sum_ok, i * (2 * G) + b * G + g + 1)
                            sp.dma_start(out_d[bass.ds(tiles[g] * P, P), :], acc[:, g % 4, :],
                                         cond=(lasts[g] > 0)).then_inc(out_done[g % 4], 16)
            for s in out_done:
                sp.wait_ge(s, 16 + 16 * (chunks // 2 if heads == 1 else STEPS // 4))

        @block.tensor
        def _(pe):
            pe.wait_ge(tab_in, 16)
            with pair(pe) as i:
                for b in (0, 1):
                    k0 = i * (2 * G) + b * G
                    c = i * 2 + b
                    for g in range(G + 1):
                        if g % 8 == 0 and g < G:
                            _, loaded = nc.values_load_multi_w_load_instructions(
                                K["j_int"][0:1, bass.ds(k0 + g, 8)], engines=[PE_ENGINE], min_val=0, max_val=NT - 1,
                                skip_runtime_bounds_check_because="j of a step is at most NT - 1")
                            tiles = (tiles if g else ()) + tuple(loaded)
                        if g < G:
                            pe.wait_ge(m_ok, k0 + g + 1)
                            if g >= 2:
                                pe.wait_ge(mt_ok, k0 + g - 1)
                            mt = pMT[:, g % 2, 0:P]
                            nc.tensor.transpose(mt, M[:, b, g, :], K["ident"][:]).then_inc(mt_ps, 1)
                        if g >= 1:
                            q = g - 1
                            pe.wait_ge(mt_ok, k0 + q + 1)
                            if heads == 1:
                                pe.wait_ge(read_e, k0 + q + 1)
                                o = pE[:, q % 2, 0:tab_w]
                            else:
                                o = pE[:, 0, q * tab_w:(q + 1) * tab_w]
                                if q == 0:
                                    pe.wait_ge(read_e, c + 1)
                            nc.tensor.matmul(o, MT[:, q % 2, :],
                                             tab[:, bass.ds(tiles[q], 1), :].rearrange("p a w -> p (a w)"), start=True,
                                             stop=True).then_inc(spread, 1)
                    pe.wait_ge(score_ok, c + 1)
                    mm = nc.tensor.transpose(pT[0:R, 0, 0:P], score[:], K["ident"][:])
                    if heads > 1:
                        mm = nc.tensor.transpose(pT[0:R, 0, P:2 * P], score2[:], K["ident"][:])
                    mm.then_inc(score_ps, 1)
                    pe.wait_ge(v_ok, c + 1)
                    nc.tensor.matmul(p_fac, V[:], head_sel[:], start=True,
                                     stop=True).then_inc(fac_ps, 1)
                    until(pe, wts_ok, c + 1)
                    mm = nc.tensor.transpose(pT[:, 0, 0:R], wts[:], K["ident"][0:R, 0:R])
                    if heads > 1:
                        mm = nc.tensor.transpose(pT[:, 0, P:P + R], wts2[:], K["ident"][0:R, 0:R])
                    mm.then_inc(wt_ps, 1)
                    for g in range(G):
                        pe.wait_ge(ax_ok, k0 + g + 1)
                        if g >= 2:
                            pe.wait_ge(sum_ok, k0 + g - 1)
                        if heads == 1:
                            mm = nc.tensor.matmul(pS[:, g % 2, 0:sum_w], M[:, b, g, :], aX[:, g % 2, :], start=True,
                                                  stop=True)
                        else:
                            nc.tensor.matmul(pS[:, g % 2, 0:HD], M[:, b, g, :], aX[:, g % 2, 0:HD], start=True,
                                             stop=True)
                            mm = nc.tensor.matmul(pS[:, g % 2, HD:WC], M[:, b, g, :], aX[:, g % 2, HD:WC], start=True,
                                                  stop=True)
                        mm.then_inc(sum_ps, 1)

        @block.scalar
        def _(sc):
            with pair(sc) as i:
                for b in (0, 1):
                    k0 = i * (2 * G) + b * G
                    c = i * 2 + b
                    for g in range(G):
                        sc.wait_ge(mt_ps, k0 + g + 1)
                        if g >= 2:
                            sc.wait_ge(spread, k0 + g - 1)
                        mt = pMT[:, g % 2, 0:P]
                        nc.scalar.copy(MT[:, g % 2, :], mt).then_inc(mt_ok, 1)
                    sc.wait_ge(fac_ps, c + 1)
                    nc.scalar.activation(fac[:], p_fac, ACT.Exp).then_inc(fac_ok, 1)
                    sc.wait_ge(diff_ok, c + 1)
                    ins = nc.scalar.activation(wts[:], S[:], ACT.Exp)
                    if heads > 1:
                        ins = nc.scalar.activation(raw2[:], S2[:], ACT.Exp)
                    ins.then_inc(wts_ok if heads == 1 else act, 1)
                    sc.wait_ge(wtT_ok, c + 1)
                    for g in range(G):
                        if g >= 2:
                            sc.wait_ge(sum_ps, k0 + g - 1)
                        if heads == 1:
                            nc.scalar.activation(aX[:, g % 2, :], X[:, b, g, :], ACT.Copy,
                                                 scale=wtT[:, g:g + 1]).then_inc(ax_ok, 1)
                        else:
                            for h in range(HA):
                                ins = nc.scalar.activation(aX[:, g % 2, h * D:(h + 1) * D], X[:, b, g, 0:D],
                                                           ACT.Copy, scale=wtT[:, h * G + g:h * G + g + 1])
                            sc.wait_ge(ax_dve, k0 + g + 1)
                            nc.scalar.copy(aX[:, g % 2, HD:HD + H], wtT[:, g::G])
                            nc.scalar.copy(aX[:, g % 2, HD + H:WC], wtT2[:, g::G]).then_inc(ax_ok, 1)

        @block.vector
        def _(v):
            counter = [0]
            base = [0]

            def then(ins):
                counter[0] += 1
                ins.then_inc(dve, 1)
                v.wait_ge(dve, base[0] + counter[0])

            if heads == 1:
                nc.vector.memset(X[:, :, :, D + 1:DA], 1.0)
            nc.vector.memset(ends[:], 0.0)
            nc.vector.memset(cin[:], -BIG)
            nc.vector.memset(bin_[:], -BIG)
            nc.vector.memset(acc[:], 0.0)
            then(nc.vector.memset(carry[:], -BIG))
            v.nop(nofuse=True).then_inc(slot_free, 2)
            v.nop(nofuse=True).then_inc(scored, 2)
            v.nop(nofuse=True).then_inc(read_e, 2 if heads == 1 else 1)
            for s in out_done:
                v.nop(nofuse=True).then_inc(s, 16)
            v.wait_ge(small_ok, 1 + heads)
            before = counter[0]
            with pair(v) as i:
                per_pair = LINKS[heads] * 2
                base[0] = i * per_pair
                for b in (0, 1):
                    k0 = i * (2 * G) + b * G
                    c = i * 2 + b
                    nc.vector.tensor_copy(keep[:, b, :], K["keep"][:, bass.ds(k0, G)])
                    then(nc.vector.tensor_copy(rel[:, b, :], K["rel"][:, bass.ds(k0, G)]))
                    v.wait_ge(rows_in[b], i * (16 * G) + 16 * G)
                    if heads == 1:
                        then(nc.vector.tensor_copy(X[:, b, :, D], K["w"][:, bass.ds(k0, G)]))

                    def one_hot(g):
                        nc.vector.tensor_scalar(M[:, b, g, :], K["node_no"][:], rel[:, b, g:g + 1], None,
                                                ALU.is_equal).then_inc(m_ok, 1)

                    LEAD = 3
                    for g in range(G + LEAD):
                        if g < G:
                            one_hot(g)
                        q = g - LEAD
                        if heads == 1 and q >= 0:
                            v.wait_ge(spread, k0 + q + 1)
                            if q >= 4:
                                v.wait_ge(read_e, k0 + q - 1)
                            ins = nc.vector.tensor_tensor_reduce(
                                out=junk[:, q % 4, :], in0=pE[:, q % 2, 0:DA], in1=X[:, b, q, :], scale=1.0, scalar=0.0,
                                op0=ALU.mult, op1=ALU.add, accum_out=score[:, q:q + 1])
                            ins.then_inc(read_e, 1)
                    if heads == 1:
                        until(v, read_e, k0 + G + 2)
                        v.nop(nofuse=True).then_inc(score_ok, 1)
                    else:
                        v.wait_ge(spread, k0 + G)
                        e3 = pE[:, 0, 0:G * 2 * heads].rearrange("p (g w) -> p g w", w=2 * heads)
                        s3 = score[:].rearrange("p (h g) -> p g h", g=G)
                        nc.vector.tensor_copy(score2[:].rearrange("p (h g) -> p g h", g=G), e3[:, :, heads:])
                        then(nc.vector.tensor_tensor(s3, e3[:, :, 0:heads], X[:, b, :, D:D + heads], ALU.add))
                        v.nop(nofuse=True).then_inc(read_e, 1)
                        nc.vector.scalar_tensor_tensor(out=score[:], in0=score[:], scalar=SLOPE, in1=score[:],
                                                       op0=ALU.mult, op1=ALU.max).then_inc(score_ok, 1)
                    v.wait_ge(gates_in[b], i * (16 * heads) + 16 * heads)
                    nc.vector.tensor_reduce(ends[:, 32:33], gate_f[:, b, :], AX.X, ALU.add)
                    v.wait_ge(score_ps, c + 1)
                    if heads > 1:
                        then(nc.vector.tensor_tensor(S2[:], pT[0:R, 0, P:2 * P], maskr[:, b, :], ALU.add))
                    then(nc.vector.tensor_tensor(S[:], pT[0:R, 0, 0:P], maskr[:, b, :], ALU.add))
                    if heads > 1:
                        then(nc.vector.tensor_tensor(raw[:], S[:], S2[:], ALU.max))
                    T0 = raw if heads > 1 else S
                    then(nc.vector.tensor_tensor_scan(fwd[:], gate_f[:, b, :], T0[:], -BIG, ALU.add, ALU.max))
                    then(nc.vector.tensor_copy(ends[:, 0:1], fwd[:, P - 1:P]))
                    then(nc.vector.transpose(endsT[:], ends[:]))
                    then(nc.vector.tensor_tensor(inj[:], carry[:], endsT[:, 32:64:G][:, 0:HB], ALU.add))
                    then(nc.vector.tensor_tensor(endsT[:, 0:32:G][:, 0:HB], endsT[:, 0:32:G][:, 0:HB], inj[:],
                                                 ALU.max))
                    then(nc.vector.memset(endsT[:, 32:64:G][:, 0:HB], -BIG))
                    then(nc.vector.tensor_tensor_scan(run[:], endsT[:, 32:64], endsT[:, 0:32], -BIG, ALU.add, ALU.max))
                    then(nc.vector.tensor_copy(shift[:, 1:32], run[:, 0:31]))
                    then(nc.vector.tensor_copy(shift[:, 0:32:G][:, 0:HB], carry[:]))
                    nc.vector.tensor_copy(carry[:], run[:, G - 1:32:G][:, 0:HB])
                    then(nc.vector.transpose(cin[:], shift[:]))
                    then(nc.vector.tensor_tensor_scan(fwd2[:], gate_f[:, b, :], T0[:], cin[:, 0:1], ALU.add, ALU.max))
                    nc.vector.tensor_reduce(ends[:, 32:33], gate_b[:, b, :], AX.X, ALU.add)
                    then(nc.vector.tensor_tensor_scan(bwd[:, ::-1], gate_b[:, b, ::-1], fwd2[:, ::-1], -BIG, ALU.add,
                                                      ALU.max))
                    then(nc.vector.tensor_copy(ends[:, 0:1], bwd[:, 0:1]))
                    then(nc.vector.transpose(endsT[:], ends[:]))
                    then(nc.vector.memset(endsT[:, 32 + G - 1:64:G][:, 0:HB], -BIG))
                    then(nc.vector.tensor_tensor_scan(run[:, ::-1], endsT[:, 63:31:-1], endsT[:, 31::-1], -BIG, ALU.add,
                                                      ALU.max))
                    then(nc.vector.tensor_copy(shift[:, 0:31], run[:, 1:32]))
                    then(nc.vector.memset(shift[:, G - 1:32:G][:, 0:HB], -BIG))
                    then(nc.vector.transpose(bin_[:], shift[:]))
                    then(nc.vector.tensor_tensor_scan(top[:, ::-1], gate_b[:, b, ::-1], fwd2[:, ::-1], bin_[:, 0:1],
                                                      ALU.add, ALU.max))
                    then(nc.vector.tensor_tensor(dlt[:], cin[:, 0:1], top[:, 0:1], ALU.subtract))
                    then(nc.vector.scalar_tensor_tensor(out=dlt[:], in0=gate_f[:, b, 0:1], scalar=0.0, in1=dlt[:],
                                                        op0=ALU.is_equal, op1=ALU.mult))
                    nc.vector.tensor_scalar(V[:], K["node_no"][0:R, :], frel[:, b, :], dlt[:, 0:1], ALU.is_equal,
                                            ALU.mult).then_inc(v_ok, 1)
                    if heads > 1:
                        nc.vector.tensor_tensor(S2[:], S2[:], top[:], ALU.subtract)
                    nc.vector.tensor_tensor(S[:], S[:], top[:], ALU.subtract).then_inc(diff_ok, 1)
                    if heads > 1:
                        v.wait_ge(act, c + 1)
                        nc.vector.scalar_tensor_tensor(out=wts2[:], in0=gate_b[:, b, :], scalar=0.0, in1=raw2[:],
                                                       op0=ALU.not_equal, op1=ALU.mult).then_inc(wts_ok, 1)
                    v.wait_ge(wt_ps, c + 1)
                    if heads > 1:
                        nc.vector.tensor_copy(wtT2[:], pT[:, 0, P:P + R])
                    then(nc.vector.tensor_copy(wtT[:], pT[:, 0, 0:R]))
                    v.nop(nofuse=True).then_inc(wtT_ok, 1)
                    until(v, fac_ok, c + 1)
                    v.nop(nofuse=True).then_inc(scored, 1)
                    if heads == 1:
                        then(nc.vector.tensor_tensor(kfac[:], keep[:, b, 0:1], fac[:], ALU.mult))
                        for g in range(G):
                            v.wait_ge(sum_ps, k0 + g + 1)
                            prev = acc[:, b, g - 1, :] if g else acc[:, 1 - b, G - 1, :]
                            if g == 0:
                                v.wait_ge(out_done[b], i * 16 + 16)
                            nc.vector.scalar_tensor_tensor(
                                out=acc[:, b, g, :], in0=prev, scalar=keep[:, b, g:g + 1] if g else kfac[:],
                                in1=pS[:, g % 2, 0:sum_w], op0=ALU.mult, op1=ALU.add).then_inc(sum_ok, 1)
                            v.wait_ge(sum_ok, k0 + g + 1)
                    else:
                        nc.vector.tensor_tensor(last[:, 0:HD].rearrange("p (h d) -> p h d", h=H),
                                                acc[:, 3, 0:HD].rearrange("p (h d) -> p h d", h=H),
                                                fac[:].unsqueeze(2).to_broadcast([P, H, D]), ALU.mult)
                        then(nc.vector.tensor_tensor(last[:, HD:WC].rearrange("p (a h) -> p a h", h=H),
                                                     acc[:, 3, HD:WC].rearrange("p (a h) -> p a h", h=H),
                                                     fac[:].unsqueeze(1).to_broadcast([P, 2, H]), ALU.mult))

                        def weigh(g):
                            if g >= 2:
                                v.wait_ge(sum_ps, k0 + g - 1)
                            nc.vector.tensor_tensor(
                                aX[:, g % 2, HA * D:HD].rearrange("p (h d) -> p h d", d=D),
                                X[:, b, g, 0:D].unsqueeze(1).to_broadcast([P, H - HA, D]),
                                wtT[:, HA * G + g::G].unsqueeze(2).to_broadcast([P, H - HA, D]),
                                ALU.mult).then_inc(ax_dve, 1)

                        weigh(0)
                        for g in range(G):
                            if g + 1 < G:
                                weigh(g + 1)
                            v.wait_ge(sum_ps, k0 + g + 1)
                            v.wait_ge(out_done[g % 4], i * (2 * G * 4) + (b * G + g - g % 4) * 4 + 16)
                            nc.vector.scalar_tensor_tensor(
                                out=acc[:, g % 4, :], in0=acc[:, (g - 1) % 4, :] if g else last[:],
                                scalar=keep[:, b, g:g + 1], in1=pS[:, g % 2, 0:WC], op0=ALU.mult,
                                op1=ALU.add).then_inc(sum_ok, 1)
                            v.wait_ge(sum_ok, k0 + g + 1)
                    v.nop(nofuse=True).then_inc(slot_free, 1)
                    if b == 1:
                        assert counter[0] - before == per_pair, (counter[0] - before, per_pair)


LINKS = {1: 27, H: 29}


def group_loop(engine):
    return engine.Fori(0, NG // 2)


def group_rows(tensor, i, b):
    return tensor[bass.ds((i * 2 + b) * (GT * P), GT * P), :].rearrange("(t p) w -> p t w", p=P)


CUTS = ((0, 512), (512, GT * P))


def table_phase(nc, K, x_d, wq, bq, wk_t, tab_d):
    with ExitStack() as ctx:
        T = Tools(nc, ctx, "tab")
        x = T.sb("x", [P, 2, GT, D])
        xT = T.sb("xT", [D, 2, GT * P])
        qT = T.sb("qT", [D, 2, GT * P])
        out = T.sb("out", [P, 2, GT, DA])
        pA = [T.ps(f"pA{b}", [P, 1024]) for b in (0, 1)]
        pB = [T.ps(f"pB{b}", [P, 1024]) for b in (0, 1)]
        slot_free = [T.sem(f"slot_free{b}") for b in (0, 1)]
        x_in = [T.sem(f"x_in{b}") for b in (0, 1)]
        xT_ps, xT_ok, q_ps, q_ok, t_ps, t_ok = (T.sem(n) for n in ("xT_ps", "xT_ok", "q_ps", "q_ok", "t_ps", "t_ok"))
        block = ctx.enter_context(nc.Block())

        @block.gpsimd
        def _(pool):
            with group_loop(pool) as i:
                for b in (0, 1):
                    pool.wait_ge(slot_free[b], i * 16 + 16)
                    pool.dma_start(x[:, b], group_rows(x_d, i, b)).then_inc(x_in[b], 16)

        @block.tensor
        def _(pe):
            with group_loop(pe) as i:
                for b in (0, 1):
                    n = i * 2 + b + 1
                    until(pe, x_in[b], i * 16 + 16)
                    for t in range(GT):
                        mm = nc.tensor.transpose(pA[b][0:D, t * P:(t + 1) * P], x[:, b, t, :], K["ident"][:])
                    mm.then_inc(xT_ps, 1)
                    until(pe, xT_ok, n)
                    for lo, hi in CUTS:
                        mm = nc.tensor.matmul(pB[b][0:D, lo:hi], wq, xT[:, b, lo:hi], start=True, stop=True)
                    mm.then_inc(q_ps, 1)
                    until(pe, q_ok, n)
                    for t in range(GT):
                        mm = nc.tensor.matmul(pA[b][:, t * DA:(t + 1) * DA], qT[:, b, t * P:(t + 1) * P], wk_t,
                                              start=True, stop=True)
                    mm.then_inc(t_ps, 1)

        @block.scalar
        def _(sc):
            with group_loop(sc) as i:
                for b in (0, 1):
                    n = i * 2 + b + 1
                    sc.wait_ge(xT_ps, n)
                    nc.scalar.copy(xT[:, b, :], pA[b][0:D, 0:GT * P]).then_inc(xT_ok, 1)
                    sc.wait_ge(q_ps, n)
                    nc.scalar.activation(qT[:, b, :], pB[b][0:D, 0:GT * P], ACT.Identity, bias=bq).then_inc(q_ok, 1)

        @block.vector
        def _(v):
            for s in slot_free:
                v.nop(nofuse=True).then_inc(s, 16)
            with group_loop(v) as i:
                for b in (0, 1):
                    v.wait_ge(t_ps, i * 2 + b + 1)
                    nc.vector.tensor_scalar(out[:, b].rearrange("p t w -> p (t w)"), pA[b][:, 0:GT * DA],
                                            float(D) ** -0.5, None, ALU.mult).then_inc(t_ok, 1)

        @block.sync
        def _(sp):
            with group_loop(sp) as i:
                for b in (0, 1):
                    until(sp, t_ok, i * 2 + b + 1)
                    sp.dma_start(group_rows(tab_d, i, b), out[:, b]).then_inc(slot_free[b], 16)
            for s in slot_free:
                sp.wait_ge(s, 16 + 16 * (NG // 2))


class Chain:

    def __init__(self, engine, sem, per_round):
        self.engine, self.sem, self.per_round, self.n, self.base = engine, sem, per_round, 0, 0

    def start_round(self, i):
        self.before = self.n
        self.base = i * self.per_round

    def __call__(self, ins):
        self.n += 1
        ins.then_inc(self.sem, 1)
        self.engine.wait_ge(self.sem, self.base + self.n)

    def end_round(self):
        assert self.n - self.before == self.per_round, (self.n - self.before, self.per_round)


def spread_rows(x, shape):
    return x.unsqueeze(2).to_broadcast(shape)


def layer_norm(v, then, x, out, sq, stat, var_ok, std_ok, n):
    shape = [P, GT, D]
    mean, var = stat[:, 0, :], stat[:, 1, :]
    then(v.tensor_reduce(mean, x, AX.X, ALU.add))
    then(v.tensor_scalar(mean, mean, -1.0 / D, None, ALU.mult))
    then(v.tensor_tensor(x, x, spread_rows(mean, shape), ALU.add))
    then(v.tensor_tensor(sq, x, x, ALU.mult))
    then(v.tensor_reduce(var, sq, AX.X, ALU.add))
    v.tensor_scalar(var, var, 1.0 / D, LN_EPS, ALU.mult, ALU.add).then_inc(var_ok, 1)
    v.wait_ge(std_ok, n)
    then(v.reciprocal(stat[:, 3, :], stat[:, 2, :]))
    then(v.tensor_tensor(out, x, spread_rows(stat[:, 3, :], shape), ALU.mult))


def gather_sums(pool, nc, K, idx, b, out, sums_d, idx_ok, n, done):
    for t in range(GT):
        pool.indirect_dma_start(out=out[:, b, t, :], out_offset=None, in_=sums_d,
                                in_offset=bass.IndirectOffsetOnAxis(ap=idx[:, b, t:t + 1], axis=0)).then_inc(done, 16)


def middle_phase(nc, K, W, sums_d, x_d, h_d, tab_d):
    with ExitStack() as ctx:
        T = Tools(nc, ctx, "mid")
        idx = T.sb("idx", [P, 2, GT], I32)
        agg = T.sb("agg", [P, 2, GT, DA])
        x = T.sb("x", [P, 2, GT, D])
        rd = T.sb("rd", [P, 2, GT])
        aggT = T.sb("aggT", [DA, 2, GT * P])
        xT = T.sb("xT", [D, 2, GT * P])
        hT = T.sb("hT", [D, 2, GT * P])
        qT = T.sb("qT", [D, 2, GT * P])
        h = T.sb("h", [P, 2, GT, D])
        out = T.sb("out", [P, 2, GT, DA])
        pA = [T.ps(f"pA{b}", [P, 1024]) for b in (0, 1)]
        pB = [T.ps(f"pB{b}", [P, 1024]) for b in (0, 1)]
        slot_free = [T.sem(f"slot_free{b}") for b in (0, 1)]
        sums_in = [T.sem(f"sums_in{b}") for b in (0, 1)]
        x_in = [T.sem(f"x_in{b}") for b in (0, 1)]
        idx_ok, norm_ok, agg_ps, x_ps, aggT_ok, xT_ok, h_ps, h_ok, q_ps, q_ok, t_ps, t_ok, dve = (
            T.sem(n) for n in ("idx_ok", "norm_ok", "agg_ps", "x_ps", "aggT_ok", "xT_ok", "h_ps", "h_ok", "q_ps",
                               "q_ok", "t_ps", "t_ok", "dve"))
        block = ctx.enter_context(nc.Block())

        @block.gpsimd
        def _(pool):
            with group_loop(pool) as i:
                for b in (0, 1):
                    until(pool, slot_free[b], i * 32 + 32)
                    nc.gpsimd.tensor_copy(idx[:, b, :],
                                          K["end_idx"][:, bass.ds((i * 2 + b) * GT, GT)]).then_inc(idx_ok, 1)
                    until(pool, idx_ok, i * 2 + b + 1)
                    gather_sums(pool, nc, K, idx, b, agg, sums_d, idx_ok, i * 2 + b + 1, sums_in[b])

        @block.sync
        def _(sp):
            with group_loop(sp) as i:
                for b in (0, 1):
                    until(sp, t_ok, i * 2 + b + 1)
                    sp.dma_start(group_rows(tab_d, i, b), out[:, b]).then_inc(slot_free[b], 16)
                    sp.dma_start(group_rows(h_d, i, b), h[:, b]).then_inc(slot_free[b], 16)
            for s in slot_free:
                sp.wait_ge(s, 32 + 32 * (NG // 2))

        @block.tensor
        def _(pe):
            with group_loop(pe) as i:
                for b in (0, 1):
                    n = i * 2 + b + 1
                    until(pe, x_in[b], i * 16 + 16)
                    for t in range(GT):
                        mm = nc.tensor.transpose(pB[b][0:D, t * P:(t + 1) * P], x[:, b, t, :], K["ident"][:])
                    mm.then_inc(x_ps, 1)
                    until(pe, norm_ok, n)
                    for t in range(GT):
                        mm = nc.tensor.transpose(pA[b][0:DA, t * P:(t + 1) * P], agg[:, b, t, :], K["ident"][:])
                    mm.then_inc(agg_ps, 1)
                    until(pe, xT_ok, n)
                    until(pe, aggT_ok, n)
                    for lo, hi in CUTS:
                        nc.tensor.matmul(pA[b][0:D, lo:hi], W["wva1"][:], aggT[:, b, lo:hi], start=True, stop=False)
                        mm = nc.tensor.matmul(pA[b][0:D, lo:hi], W["ws1"][:], xT[:, b, lo:hi], start=False, stop=True)
                    mm.then_inc(h_ps, 1)
                    until(pe, h_ok, n)
                    for lo, hi in CUTS:
                        mm = nc.tensor.matmul(pB[b][0:D, lo:hi], W["wq2"][:], hT[:, b, lo:hi], start=True, stop=True)
                    mm.then_inc(q_ps, 1)
                    for t in range(GT):
                        nc.tensor.transpose(pA[b][:, t * D:(t + 1) * D], hT[:, b, t * P:(t + 1) * P],
                                            K["ident"][0:D, 0:D])
                    until(pe, q_ok, n)
                    for t in range(GT):
                        mm = nc.tensor.matmul(pB[b][:, t * DA:(t + 1) * DA], qT[:, b, t * P:(t + 1) * P],
                                              W["wk_t2"][:], start=True, stop=True)
                    mm.then_inc(t_ps, 1)

        @block.scalar
        def _(sc):
            with group_loop(sc) as i:
                for b in (0, 1):
                    n = i * 2 + b + 1
                    until(sc, slot_free[b], i * 32 + 32)
                    sc.dma_start(x[:, b], group_rows(x_d, i, b)).then_inc(x_in[b], 16)
                    sc.wait_ge(x_ps, n)
                    nc.scalar.copy(xT[:, b, :], pB[b][0:D, 0:GT * P]).then_inc(xT_ok, 1)
                    sc.wait_ge(h_ps, n)
                    nc.scalar.activation(hT[:, b, :], pA[b][0:D, 0:GT * P], ACT.Relu,
                                         bias=W["bs1"][:]).then_inc(h_ok, 1)
                    sc.wait_ge(q_ps, n)
                    nc.scalar.activation(qT[:, b, :], pB[b][0:D, 0:GT * P], ACT.Identity,
                                         bias=W["bq2"][:]).then_inc(q_ok, 1)

        @block.vector
        def _(v):
            for s in slot_free:
                v.nop(nofuse=True).then_inc(s, 32)
            then = Chain(v, dve, 4)
            with group_loop(v) as i:
                then.start_round(i)
                for b in (0, 1):
                    n = i * 2 + b + 1
                    v.wait_ge(sums_in[b], i * (16 * GT) + 16 * GT)
                    then(nc.vector.tensor_scalar(rd[:, b], agg[:, b, :, DA - 1], 0.5, None, ALU.max))
                    then(nc.vector.reciprocal(rd[:, b], rd[:, b]))
                    nc.vector.tensor_tensor(agg[:, b], agg[:, b], spread_rows(rd[:, b], [P, GT, DA]),
                                            ALU.mult).then_inc(norm_ok, 1)
                    v.wait_ge(agg_ps, n)
                    nc.vector.tensor_copy(aggT[:, b, :], pA[b][0:DA, 0:GT * P]).then_inc(aggT_ok, 1)
                    v.wait_ge(t_ps, n)
                    nc.vector.tensor_copy(h[:, b].rearrange("p t w -> p (t w)"), pA[b][:, 0:GT * D])
                    nc.vector.tensor_scalar(out[:, b].rearrange("p t w -> p (t w)"), pB[b][:, 0:GT * DA],
                                            float(D) ** -0.5, None, ALU.mult).then_inc(t_ok, 1)
                then.end_round()


def second_phase(nc, K, W, sums_d, h_d, x_d, x1_d, tab_d):
    with ExitStack() as ctx:
        T = Tools(nc, ctx, "sec")
        idx = T.sb("idx", [P, 2, GT], I32)
        agg = T.sb("agg", [P, 2, GT, DA])
        x = T.sb("x", [P, 2, GT, D])
        h = T.sb("h", [P, 2, GT, D])
        rd = T.sb("rd", [P, 2, GT])
        aggT = T.sb("aggT", [DA, 2, GT * P])
        hT = T.sb("hT", [D, 2, GT * P])
        y = T.sb("y", [P, 2, GT, D])
        sq = T.sb("sq", [P, GT, D])
        stat = T.sb("stat", [P, 4, GT])
        x1 = T.sb("x1", [P, 2, GT, D + H])
        x1T = T.sb("x1T", [D, 2, GT * P])
        out = T.sb("out", [P, 2, GT, 2 * H])
        pA = [T.ps(f"pA{b}", [P, 1024]) for b in (0, 1)]
        pB = [T.ps(f"pB{b}", [P, 1024]) for b in (0, 1)]
        slot_free = [T.sem(f"slot_free{b}") for b in (0, 1)]
        sums_in = [T.sem(f"sums_in{b}") for b in (0, 1)]
        x_in = [T.sem(f"x_in{b}") for b in (0, 1)]
        h_in = [T.sem(f"h_in{b}") for b in (0, 1)]
        idx_ok, norm_ok, agg_ps, h_ps, aggT_ok, hT_ok, y_ps, x1_ok, x1_ps, x1T_ok, a_ps, t_ok, dve, var_ok, std_ok = (
            T.sem(n) for n in ("idx_ok", "norm_ok", "agg_ps", "h_ps", "aggT_ok", "hT_ok", "y_ps", "x1_ok", "x1_ps",
                               "x1T_ok", "a_ps", "t_ok", "dve", "var_ok", "std_ok"))
        block = ctx.enter_context(nc.Block())

        @block.gpsimd
        def _(pool):
            with group_loop(pool) as i:
                for b in (0, 1):
                    until(pool, slot_free[b], i * 32 + 32)
                    nc.gpsimd.tensor_copy(idx[:, b, :],
                                          K["end_idx"][:, bass.ds((i * 2 + b) * GT, GT)]).then_inc(idx_ok, 1)
                    until(pool, idx_ok, i * 2 + b + 1)
                    gather_sums(pool, nc, K, idx, b, agg, sums_d, idx_ok, i * 2 + b + 1, sums_in[b])

        @block.sync
        def _(sp):
            with group_loop(sp) as i:
                for b in (0, 1):
                    until(sp, t_ok, i * 2 + b + 1)
                    sp.dma_start(group_rows(tab_d, i, b), out[:, b]).then_inc(slot_free[b], 16)
                    sp.dma_start(group_rows(x1_d, i, b), x1[:, b]).then_inc(slot_free[b], 16)
            for s in slot_free:
                sp.wait_ge(s, 32 + 32 * (NG // 2))

        @block.tensor
        def _(pe):
            with group_loop(pe) as i:
                for b in (0, 1):
                    n = i * 2 + b + 1
                    until(pe, h_in[b], i * 16 + 16)
                    for t in range(GT):
                        mm = nc.tensor.transpose(pB[b][0:D, t * P:(t + 1) * P], h[:, b, t, :], K["ident"][:])
                    mm.then_inc(h_ps, 1)
                    until(pe, norm_ok, n)
                    for t in range(GT):
                        mm = nc.tensor.transpose(pA[b][0:DA, t * P:(t + 1) * P], agg[:, b, t, :], K["ident"][:])
                    mm.then_inc(agg_ps, 1)
                    until(pe, hT_ok, n)
                    until(pe, aggT_ok, n)
                    for t in range(GT):
                        nc.tensor.matmul(pA[b][:, t * D:(t + 1) * D], aggT[:, b, t * P:(t + 1) * P], W["wva2"][:],
                                         start=True, stop=False)
                        mm = nc.tensor.matmul(pA[b][:, t * D:(t + 1) * D], hT[:, b, t * P:(t + 1) * P], W["ws2"][:],
                                              start=False, stop=True)
                    mm.then_inc(y_ps, 1)
                    until(pe, x1_ok, n)
                    for t in range(GT):
                        mm = nc.tensor.transpose(pB[b][0:D, t * P:(t + 1) * P], x1[:, b, t, 0:D], K["ident"][:])
                    mm.then_inc(x1_ps, 1)
                    until(pe, x1T_ok, n)
                    for t in range(GT):
                        mm = nc.tensor.matmul(pA[b][:, t * 2 * H:(t + 1) * 2 * H], x1T[:, b, t * P:(t + 1) * P],
                                              W["a_sd"][:], start=True, stop=True)
                    mm.then_inc(a_ps, 1)

        @block.scalar
        def _(sc):
            with group_loop(sc) as i:
                for b in (0, 1):
                    n = i * 2 + b + 1
                    until(sc, slot_free[b], i * 32 + 32)
                    sc.dma_start(h[:, b], group_rows(h_d, i, b)).then_inc(h_in[b], 16)
                    sc.dma_start(x[:, b], group_rows(x_d, i, b)).then_inc(x_in[b], 16)
                    sc.wait_ge(h_ps, n)
                    nc.scalar.copy(hT[:, b, :], pB[b][0:D, 0:GT * P]).then_inc(hT_ok, 1)
                    sc.wait_ge(var_ok, n)
                    nc.scalar.activation(stat[:, 2, :], stat[:, 1, :], ACT.Sqrt).then_inc(std_ok, 1)
                    sc.wait_ge(x1_ps, n)
                    nc.scalar.copy(x1T[:, b, :], pB[b][0:D, 0:GT * P]).then_inc(x1T_ok, 1)

        @block.vector
        def _(v):
            for s in slot_free:
                v.nop(nofuse=True).then_inc(s, 32)
            then = Chain(v, dve, 2 * 14)
            with group_loop(v) as i:
                then.start_round(i)
                for b in (0, 1):
                    n = i * 2 + b + 1
                    v.wait_ge(sums_in[b], i * (16 * GT) + 16 * GT)
                    then(nc.vector.tensor_scalar(rd[:, b], agg[:, b, :, DA - 1], 0.5, None, ALU.max))
                    then(nc.vector.reciprocal(rd[:, b], rd[:, b]))
                    nc.vector.tensor_tensor(agg[:, b], agg[:, b], spread_rows(rd[:, b], [P, GT, DA]),
                                            ALU.mult).then_inc(norm_ok, 1)
                    v.wait_ge(agg_ps, n)
                    nc.vector.tensor_copy(aggT[:, b, :], pA[b][0:DA, 0:GT * P]).then_inc(aggT_ok, 1)
                    v.wait_ge(y_ps, n)
                    v.wait_ge(x_in[b], i * 16 + 16)
                    p3 = pA[b][:, 0:GT * D].rearrange("p (t w) -> p t w", w=D)
                    then(nc.vector.tensor_tensor(y[:, b], p3, x[:, b], ALU.add))
                    then(nc.vector.tensor_tensor(y[:, b], y[:, b], over_tiles(W["bs2"]), ALU.add))
                    layer_norm(v, then, y[:, b], x1[:, b, :, 0:D], sq[:], stat, var_ok, std_ok, n)
                    v.nop(nofuse=True).then_inc(x1_ok, 1)
                    v.wait_ge(a_ps, n)
                    a3 = pA[b][:, 0:GT * 2 * H].rearrange("p (t w) -> p t w", w=2 * H)
                    then(nc.vector.tensor_copy(x1[:, b, :, D:], a3[:, :, 0:H]))
                    nc.vector.tensor_copy(out[:, b, :, 0:H], a3[:, :, H:])
                    then(nc.vector.tensor_tensor(out[:, b, :, H:], x1[:, b, :, D:], a3[:, :, H:], ALU.add))
                    then(nc.vector.scalar_tensor_tensor(out=out[:, b, :, H:], in0=out[:, b, :, H:], scalar=SLOPE,
                                                        in1=out[:, b, :, H:], op0=ALU.mult, op1=ALU.max))
                    v.nop(nofuse=True).then_inc(t_ok, 1)
                then.end_round()


def over_tiles(row):
    return row[:].unsqueeze(1).to_broadcast([P, GT, D])


def last_phase(nc, K, W, sums_d, x1_d, out_d):
    with ExitStack() as ctx:
        T = Tools(nc, ctx, "fin")
        agg = T.sb("agg", [P, 2, GT, WC])
        x1 = T.sb("x1", [P, 2, GT, D + H])
        own = T.sb("own", [P, GT, H])
        den = T.sb("den", [P, GT, H])
        ox = T.sb("ox", [P, H, D])
        aggT = T.sb("aggT", [P, GT, 4 * P])
        y = T.sb("y", [P, 2, GT, D])
        sq = T.sb("sq", [P, GT, D])
        stat = T.sb("stat", [P, 4, GT])
        z = T.sb("z", [P, 2, GT, D])
        zT = T.sb("zT", [D, 2, GT * P])
        hid = T.sb("hid", [P, 2, GT * P])
        out = T.sb("out", [P, 2, GT, D])
        pA = [T.ps(f"pA{b}", [P, 1024]) for b in (0, 1)]
        pB = [T.ps(f"pB{b}", [P, 1024]) for b in (0, 1)]
        slot_free = [T.sem(f"slot_free{b}") for b in (0, 1)]
        in_ok = [T.sem(f"in{b}") for b in (0, 1)]
        norm_ok, agg_ps, aggT_ok, y_ps, z_ok, z_ps, zT_ok, hid_ps, hid_ok, f_ps, o_ok, dve, var_ok, std_ok = (
            T.sem(n) for n in ("norm_ok", "agg_ps", "aggT_ok", "y_ps", "z_ok", "z_ps", "zT_ok", "hid_ps", "hid_ok",
                               "f_ps", "o_ok", "dve", "var_ok", "std_ok"))
        block = ctx.enter_context(nc.Block())
        HD = H * D

        @block.gpsimd
        def _(pool):
            with group_loop(pool) as i:
                for b in (0, 1):
                    until(pool, slot_free[b], i * 16 + 16)
                    pool.dma_start(agg[:, b], group_rows(sums_d, i, b)).then_inc(in_ok[b], 16)
                    pool.dma_start(x1[:, b], group_rows(x1_d, i, b)).then_inc(in_ok[b], 16)

        @block.sync
        def _(sp):
            with group_loop(sp) as i:
                for b in (0, 1):
                    until(sp, o_ok, i * 2 + b + 1)
                    sp.dma_start(group_rows(out_d, i, b), out[:, b]).then_inc(slot_free[b], 16)
            for s in slot_free:
                sp.wait_ge(s, 16 + 16 * (NG // 2))

        @block.tensor
        def _(pe):
            with group_loop(pe) as i:
                for b in (0, 1):
                    n = i * 2 + b + 1
                    t0 = (i * 2 + b) * GT
                    for t in range(GT + 1):
                        if t < GT:
                            until(pe, norm_ok, t0 + t + 1)
                            if t >= 2:
                                until(pe, aggT_ok, t0 + t - 1)
                            for q in range(4):
                                mm = nc.tensor.transpose(pA[b][:, (t % 2) * 512 + q * P:(t % 2) * 512 + (q + 1) * P],
                                                         agg[:, b, t, q * P:(q + 1) * P], K["ident"][:])
                            mm.then_inc(agg_ps, 1)
                        if t:
                            until(pe, aggT_ok, t0 + t)
                            for q in range(4):
                                mm = nc.tensor.matmul(pB[b][:, (t - 1) * D:t * D], aggT[:, t - 1, q * P:(q + 1) * P],
                                                      W["watt2"][:, q, :], start=(q == 0), stop=(q == 3))
                    mm.then_inc(y_ps, 1)
                    until(pe, z_ok, n)
                    for t in range(GT):
                        mm = nc.tensor.transpose(pA[b][0:D, t * P:(t + 1) * P], z[:, b, t, :], K["ident"][:])
                    mm.then_inc(z_ps, 1)
                    until(pe, zT_ok, n)
                    for lo, hi in CUTS:
                        mm = nc.tensor.matmul(pB[b][:, lo:hi], W["w1"][:], zT[:, b, lo:hi], start=True, stop=True)
                    mm.then_inc(hid_ps, 1)
                    until(pe, hid_ok, n)
                    for t in range(GT):
                        mm = nc.tensor.matmul(pA[b][:, t * D:(t + 1) * D], hid[:, b, t * P:(t + 1) * P], W["w2"][:],
                                              start=True, stop=True)
                    mm.then_inc(f_ps, 1)

        @block.scalar
        def _(sc):
            def root(n):
                sc.wait_ge(var_ok, n)
                nc.scalar.activation(stat[:, 2, :], stat[:, 1, :], ACT.Sqrt).then_inc(std_ok, 1)

            with group_loop(sc) as i:
                for b in (0, 1):
                    n = i * 2 + b + 1
                    t0 = (i * 2 + b) * GT
                    for t in range(GT):
                        sc.wait_ge(agg_ps, t0 + t + 1)
                        nc.scalar.copy(aggT[:, t, :], pA[b][:, (t % 2) * 512:(t % 2) * 512 + 4 * P]).then_inc(aggT_ok, 1)
                    root(i * 6 + b * 3 + 1)
                    sc.wait_ge(z_ps, n)
                    nc.scalar.copy(zT[:, b, :], pA[b][0:D, 0:GT * P]).then_inc(zT_ok, 1)
                    sc.wait_ge(hid_ps, n)
                    nc.scalar.activation(hid[:, b, :], pB[b][:, 0:GT * P], ACT.Relu, bias=W["b1"][:]).then_inc(hid_ok, 1)
                    root(i * 6 + b * 3 + 2)
                    root(i * 6 + b * 3 + 3)

        @block.vector
        def _(v):
            for s in slot_free:
                v.nop(nofuse=True).then_inc(s, 16)
            then = Chain(v, dve, 2 * FIN_LINKS)
            with group_loop(v) as i:
                then.start_round(i)
                for b in (0, 1):
                    n = i * 2 + b + 1
                    v.wait_ge(in_ok[b], i * 32 + 32)
                    sums = agg[:, b, :, HD:HD + H]
                    then(nc.vector.tensor_tensor(den[:], sums, agg[:, b, :, HD + H:], ALU.add))
                    then(nc.vector.scalar_tensor_tensor(out=own[:], in0=den[:], scalar=0.5, in1=agg[:, b, :, HD + H:],
                                                        op0=ALU.is_lt, op1=ALU.add))
                    then(nc.vector.tensor_tensor(den[:], sums, own[:], ALU.add))
                    then(nc.vector.tensor_scalar(den[:], den[:], SM_EPS, float(H), ALU.add, ALU.mult))
                    then(nc.vector.reciprocal(den[:], den[:]))
                    for t in range(GT):
                        a3 = agg[:, b, t, 0:HD].rearrange("p (h d) -> p h d", d=D)
                        then(nc.vector.tensor_tensor(ox[:], x1[:, b, t, 0:D].unsqueeze(1).to_broadcast([P, H, D]),
                                                     own[:, t, :].unsqueeze(2).to_broadcast([P, H, D]), ALU.mult))
                        then(nc.vector.tensor_tensor(a3, a3, ox[:], ALU.add))
                        nc.vector.tensor_tensor(a3, a3, den[:, t, :].unsqueeze(2).to_broadcast([P, H, D]),
                                                ALU.mult).then_inc(norm_ok, 1)
                    v.wait_ge(y_ps, n)
                    y3 = pB[b][:, 0:GT * D].rearrange("p (t w) -> p t w", w=D)
                    then(nc.vector.tensor_tensor(y[:, b], y3, x1[:, b, :, 0:D], ALU.add))
                    then(nc.vector.tensor_tensor(y[:, b], y[:, b], over_tiles(W["bias_att"]), ALU.add))
                    layer_norm(v, then, y[:, b], z[:, b], sq[:], stat, var_ok, std_ok, i * 6 + b * 3 + 1)
                    then(nc.vector.tensor_tensor(z[:, b], z[:, b], over_tiles(W["ln1_g"]), ALU.mult))
                    then(nc.vector.tensor_tensor(z[:, b], z[:, b], over_tiles(W["ln1_b"]), ALU.add))
                    v.nop(nofuse=True).then_inc(z_ok, 1)
                    v.wait_ge(f_ps, n)
                    f3 = pA[b][:, 0:GT * D].rearrange("p (t w) -> p t w", w=D)
                    then(nc.vector.tensor_tensor(y[:, b], f3, z[:, b], ALU.add))
                    then(nc.vector.tensor_tensor(y[:, b], y[:, b], over_tiles(W["b2"]), ALU.add))
                    layer_norm(v, then, y[:, b], z[:, b], sq[:], stat, var_ok, std_ok, i * 6 + b * 3 + 2)
                    then(nc.vector.tensor_tensor(z[:, b], z[:, b], over_tiles(W["ln2_g"]), ALU.mult))
                    then(nc.vector.tensor_tensor(z[:, b], z[:, b], over_tiles(W["ln2_b"]), ALU.add))
                    then(nc.vector.tensor_tensor(y[:, b], z[:, b], x1[:, b, :, 0:D], ALU.add))
                    layer_norm(v, then, y[:, b], out[:, b], sq[:], stat, var_ok, std_ok, i * 6 + b * 3 + 3)
                    v.nop(nofuse=True).then_inc(o_ok, 1)
                then.end_round()


FIN_LINKS = 5 + 2 * GT + 2 + 7 + 2 + 2 + 7 + 3 + 7


def load_weights(nc, K, W, w):
    with ExitStack() as ctx:
        T = Tools(nc, ctx, "wgt")
        att = T.sb("att", [D, H, D])
        vec = T.sb("vec", [D, 2, H, D])
        prod = T.sb("prod", [D, H, D])
        stack = [T.sb(f"stack{n}", [DA, D]) for n in (0, 1)]
        turned = T.ps("turned", [D, 2, 512])
        loads = T.sem("loads")
        dve = T.sem("dve")
        turned_ok = T.sem("turned_ok")
        block = ctx.enter_context(nc.Block())
        row = lambda a: a.rearrange("(a d) -> a d", a=1)
        col = lambda a: a.rearrange("(d a) -> d a", a=1)
        copies = [(att[:], w["W_att"].rearrange("d (h c) -> d h c", h=H)),
                  (vec[:, 0], w["att_src"].partition_broadcast(D)), (vec[:, 1], w["att_dst"].partition_broadcast(D)),
                  (W["w1"][:], w["W1"]), (W["b1"][:], col(w["b1"])), (W["w2"][:], w["W2"])]
        for n in (1, 2):
            s = stack[n - 1]
            copies += [(s[0:D, :], w[f"Wk{n}"]), (s[D:D + 1, :], w[f"We{n}"]), (s[D + 1:DA, :], row(w[f"bk{n}"])),
                       (W[f"wva{n}"][0:D, :], w[f"Wv{n}"]), (W[f"wva{n}"][D:D + 1, :], w[f"We{n}"]),
                       (W[f"wva{n}"][D + 1:DA, :], row(w[f"bv{n}"])), (W[f"wq{n}"][:], w[f"Wq{n}"]),
                       (W[f"bq{n}"][:], col(w[f"bq{n}"])), (W[f"ws{n}"][:], w[f"Ws{n}"])]
        copies += [(W["bs1"][:], col(w["bs1"])), (W["bs2"][:], w["bs2"].partition_broadcast(P))]
        copies += [(W[n][:], w[n].partition_broadcast(P)) for n in ("bias_att", "b2", "ln1_g", "ln1_b", "ln2_g",
                                                                    "ln2_b")]
        by_pair = w["W_att"].rearrange("d (q a o) -> a d q o", a=2, o=D)
        copies += [(W["watt2"][a * D:(a + 1) * D, :, :], by_pair[a]) for a in (0, 1)]

        @block.sync
        def _(sp):
            for dst, src in copies:
                sp.dma_start(dst, src).then_inc(loads, 16)
            sp.wait_ge(loads, 16 * len(copies))

        @block.tensor
        def _(pe):
            until(pe, loads, 16 * len(copies))
            for n in (0, 1):
                mm = nc.tensor.transpose(turned[:, n, 0:DA], stack[n][:], K["ident"][0:DA, 0:DA])
            mm.then_inc(turned_ok, 1)

        @block.vector
        def _(v):
            v.wait_ge(loads, 16 * len(copies))
            for n in (0, 1):
                nc.vector.tensor_tensor(prod[:], att[:], vec[:, n], ALU.mult).then_inc(dve, 1)
                v.wait_ge(dve, 2 * n + 1)
                nc.vector.tensor_reduce(W["a_sd"][:, n * H:(n + 1) * H], prod[:], AX.X, ALU.add).then_inc(dve, 1)
                v.wait_ge(dve, 2 * n + 2)
            v.wait_ge(turned_ok, 1)
            for n in (1, 2):
                nc.vector.tensor_copy(W[f"wk_t{n}"][:], turned[:, n - 1, 0:DA])


WEIGHTS = ["Wq1", "bq1", "Wk1", "bk1", "Wv1", "bv1", "We1", "Ws1", "bs1", "Wq2", "bq2", "Wk2", "bk2", "Wv2", "bv2",
           "We2", "Ws2", "bs2"]
WEIGHTS_L1 = ["W_att", "att_src", "att_dst", "bias_att", "W1", "b1", "W2", "b2", "ln1_g", "ln1_b", "ln2_g", "ln2_b"]


def build(nc, x, src, dst, ew, w, out):
    def scratch(name, shape):
        return nc.dram_tensor(f"scratch_{name}", shape, F32, kind="Internal").ap()

    dram = {"dst_flat": scratch("dst_flat", (STEPS * P + P,)), "gates": scratch("gates", (STEPS, GATE_W))}
    tab1, tab2 = scratch("tab1", (N_PAD, DA)), scratch("tab2", (N_PAD, DA))
    tab3 = scratch("tab3", (N_PAD, 2 * H))
    sums1, sums2 = (scratch(f"sums{n}", (STEPS // GA, P, GA, DA)) for n in (1, 2))
    sums3 = scratch("sums3", (N_PAD, WC))
    h, x1 = scratch("h", (N_PAD, D)), scratch("x1", (N_PAD, D + H))
    with ExitStack() as ctx:
        T = Tools(nc, ctx, "all")
        K = {"ident": T.sb("ident", [P, P]), "ones": T.sb("ones", [P, P]), "node_no": T.sb("node_no", [P, P]),
             "keep": T.sb("keep", [P, STEPS]), "j_int": T.sb("j_int", [1, STEPS], I32),
             "last_int": T.sb("last_int", [1, STEPS], I32), "end_idx": T.sb("end_idx", [P, NT], I32),
             "src_idx": T.sb("src_idx", [P, STEPS], I32), "rel": T.sb("rel", [P, STEPS]), "w": T.sb("w", [P, STEPS])}
        W = {"w1": T.sb("w1", [D, 2 * D]), "b1": T.sb("b1", [2 * D, 1]), "w2": T.sb("w2", [2 * D, D]),
             "a_sd": T.sb("a_sd", [D, 2 * H]), "watt2": T.sb("watt2", [P, H // 2, D]), "bs1": T.sb("bs1", [D, 1])}
        for n in (1, 2):
            W |= {f"wk_t{n}": T.sb(f"wk_t{n}", [D, DA]), f"wva{n}": T.sb(f"wva{n}", [DA, D]),
                  f"wq{n}": T.sb(f"wq{n}", [D, D]), f"bq{n}": T.sb(f"bq{n}", [D, 1]), f"ws{n}": T.sb(f"ws{n}", [D, D])}
        for n in ("bs2", "bias_att", "b2", "ln1_g", "ln1_b", "ln2_g", "ln2_b"):
            W[n] = T.sb(n, [P, D])
        build_schedule(nc, K, src, dst, ew, dram)
        load_weights(nc, K, W, w)
        table_phase(nc, K, x, W["wq1"][:], W["bq1"][:], W["wk_t1"][:], tab1)
        edge_phase(nc, K, "e1", 1, x, D, tab1, DA, dram, sums1)
        by_row = lambda s: s.rearrange("c p g w -> (c p g) w")
        middle_phase(nc, K, W, by_row(sums1), x, h, tab2)
        edge_phase(nc, K, "e2", 1, h, D, tab2, DA, dram, sums2)
        second_phase(nc, K, W, by_row(sums2), h, x, x1, tab3)
        edge_phase(nc, K, "e3", H, x1, D + H, tab3, 2 * H, dram, sums3)
        last_phase(nc, K, W, sums3, x1, out)


def lay_out(inputs):
    import numpy as np

    def edges(a, fill):
        a = np.ascontiguousarray(a).reshape(-1)
        return np.concatenate([a, np.full(E_PAD - E, fill, a.dtype)]).reshape(-1, P)

    x = np.ascontiguousarray(inputs["x"])
    arrays = {"x": np.concatenate([x, np.zeros((N_PAD - N, D), x.dtype)]), "src": edges(inputs["src"], 0),
              "dst": edges(inputs["dst"], NODE_PAD), "ew": edges(inputs["edge_weight1"], 0)}
    for n in WEIGHTS:
        arrays["w_" + n] = np.ascontiguousarray(inputs["L0_gnn_" + n])
    for n in WEIGHTS_L1:
        arrays["w_" + n] = np.ascontiguousarray(inputs["L1_gnn_" + n])
    return arrays


def kernel(**inputs):
    import concourse.bacc as bacc
    from concourse.bass_utils import run_bass_kernel_spmd

    arrays = lay_out(inputs)
    nc = bacc.Bacc("TRN2", target_bir_lowering=False, num_devices=1)
    t = {n: nc.dram_tensor(n, a.shape, mybir.dt.from_np(a.dtype), kind="ExternalInput").ap()
         for n, a in arrays.items()}
    out = nc.dram_tensor("out", (N_PAD, D), F32, kind="ExternalOutput").ap()
    build(nc, t["x"], t["src"], t["dst"], t["ew"], {n: t["w_" + n] for n in WEIGHTS + WEIGHTS_L1}, out)
    r = run_bass_kernel_spmd(nc, [arrays], core_ids=[0])
    return r.results[0]["out"][:N]
```

```python
import concourse.bass as bass
from concourse import mybir
from contextlib import ExitStack

F32 = mybir.dt.float32
I32 = mybir.dt.int32
ALU = mybir.AluOpType
ACT = mybir.ActivationFunctionType
AX = mybir.AxisListType
SP_ENGINE = mybir.EngineType.SP
PE_ENGINE = mybir.EngineType.PE

P = 128
N = 12500
E = 200000
D = 64
H = 8
DA = D + 2
NT = -(-N // P)
ET = -(-E // P)
N_PAD = NT * P
E_PAD = (ET + 1) * P
NODE_PAD = 1 << 20
STEPS = 13 * P
KC = STEPS // P
assert STEPS >= ET + NT - 1 and STEPS - NT < ET + P
GT = 7
NG = NT // GT
assert NT % GT == 0 and NG % 2 == 0
GATE_W = 3 * P + 2
BIG = 1.0e30
LN_EPS = 1e-5
SM_EPS = 1e-16
SLOPE = 0.2
WC = H * D + 2 * H


def until(engine, sem, value):
    engine.wait_ge(sem, value)
    engine.nop(nofuse=True)


class Tools:

    def __init__(self, nc, ctx, part):
        self.nc, self.ctx, self.part, self.sems = nc, ctx, part, []
        ctx.callback(self.clear)

    def clear(self):
        if self.sems:
            self.nc.clear_and_free_semaphores(self.sems)
            self.nc.all_engine_barrier()

    def sb(self, name, shape, dt=F32):
        return self.ctx.enter_context(self.nc.sbuf_tensor(f"{self.part}_{name}", shape, dt))

    def ps(self, name, shape, dt=F32):
        return self.ctx.enter_context(self.nc.psum_tensor(f"{self.part}_{name}", shape, dt))

    def sem(self, name):
        self.sems.append(self.nc.alloc_semaphore(f"{self.part}_{name}"))
        return self.sems[-1]


def build_schedule(nc, K, src_d, dst_d, w_d, dram):
    with ExitStack() as ctx:
        T = Tools(nc, ctx, "sch")
        sb, ps, sem = T.sb, T.ps, T.sem
        last_dst = sb("last_dst", [1, ET], I32)
        last_tile_i = sb("last_tile_i", [1, ET], I32)
        last_tile = sb("last_tile", [1, ET])
        tile_no = sb("tile_no", [P, ET])
        J = sb("J", [P, ET])
        L = sb("L", [P, ET])
        junk = sb("junk", [P, ET])
        step_no = sb("step_no", [P, KC])
        part_no = sb("part_no", [P, 1])
        i_of = sb("i_of", [P, KC])
        i_int = sb("i_int", [P, KC], I32)
        j_of = sb("j_of", [P, KC])
        j_base = sb("j_base", [P, KC])
        diag = sb("diag", [P, KC, P])
        j_row = sb("j_row", [P, STEPS])
        is_last = sb("is_last", [1, STEPS])
        end_of = sb("end_of", [P, 1])
        end_int = sb("end_int", [P, 1], I32)
        end_slot_i = sb("end_slot_i", [P, 1], I32)
        end_slot = sb("end_slot", [P, 1])
        end_row = sb("end_row", [P, 1])
        end_diag = sb("end_diag", [P, P])
        slot_off = sb("slot_off", [P, 1])
        src_r = sb("src_r", [P, KC, P], I32)
        dst_r = sb("dst_r", [P, KC, P], I32)
        w_r = sb("w_r", [P, KC, P])
        src_f = sb("src_f", [P, KC, P])
        dst_f = sb("dst_f", [P, KC, P])
        rel = sb("rel", [P, KC, P])
        prev_f = sb("prev_f", [P, KC, P])
        gate = sb("gate", [P, KC, P])
        mask = sb("mask", [P, KC, P])
        over = sb("over", [P, KC, P])
        inner = sb("inner", [P, KC])
        minus1 = sb("minus1", [1, P])
        minus_big = sb("minus_big", [1, P])
        wide = ps("wide", [P, 2048])
        turned = ps("turned", [P, 4, 512])

        last_in = sem("last_in")
        iotas = sem("iotas")
        dve = sem("dve")
        j_bcast = sem("j_bcast")
        steps_ok = sem("steps_ok")
        diag_ok = sem("diag_ok")
        row_ok = sem("row_ok")
        end_ok = sem("end_ok")
        endb_ok = sem("endb_ok")
        rows_in = sem("rows_in")
        dst_ready = sem("dst_ready")
        dst_out = sem("dst_out")
        pads_out = sem("pads_out")
        prev_in = sem("prev_in")
        gates_ready = sem("gates_ready")
        gates_out = sem("gates_out")
        turn_ready = sem("turn_ready")
        turned_ok = sem("turned_ok")
        kept_ok = sem("kept_ok")

        groups = [(a, c0) for a in range(3) for c0 in range(0, KC, 4)]
        block = ctx.enter_context(nc.Block())

        @block.sync
        def _(sp):
            with nc.allow_non_contiguous_dma(reason="one element of each edge tile"):
                sp.dma_start(last_dst[:], dst_d[0:ET, P - 1:P].rearrange("t a -> a t")).then_inc(last_in, 16)
            sp.wait_ge(iotas, 7)
            sp.dma_start(dram["dst_flat"][0:P].rearrange("(a e) -> a e", a=1), minus1[:]).then_inc(pads_out, 16)
            sp.wait_ge(dst_ready, 1)
            sp.dma_start(dram["dst_flat"][P:P + STEPS * P].rearrange("(c p e) -> p c e", p=P, e=P),
                         dst_f[:]).then_inc(dst_out, 16)
            sp.wait_ge(dst_out, 16)
            sp.wait_ge(pads_out, 16)
            sp.dma_start(prev_f[:], dram["dst_flat"][P - 1:P - 1 + STEPS * P]
                         .rearrange("(c p e) -> p c e", p=P, e=P)).then_inc(prev_in, 16)
            sp.wait_ge(gates_ready, 2)
            rows = dram["gates"].rearrange("(c p) w -> p c w", p=P)
            stored = 0
            with nc.allow_non_contiguous_dma(reason="single elements of each step"):
                for out, in_ in (
                        (rows[:, :, 0:P], gate[:]),
                        (rows[:, :, P:2 * P - 1], gate[:, :, 1:]),
                        (dram["gates"][0:P - 1, 2 * P - 1:2 * P], gate[1:P, 0, 0:1]),
                        (dram["gates"][P - 1:STEPS - 1, 2 * P - 1:2 * P].rearrange("(c p) w -> p c w", p=P),
                         gate[:, 1:, 0:1]),
                        (dram["gates"][STEPS - 1:STEPS, 2 * P - 1:2 * P], minus_big[:, 0:1]),
                        (rows[:, :, 2 * P:3 * P], mask[:]),
                        (rows[:, :, 3 * P:3 * P + 1], rel[:, :, 0:1]),
                        (rows[:, :, 3 * P + 1:], inner[:].unsqueeze(2))):
                    sp.dma_start(out, in_).then_inc(gates_out, 16)
                    stored += 16
            sp.wait_ge(gates_out, stored)

        @block.gpsimd
        def _(pool):
            nc.gpsimd.iota(tile_no[:], [[1, ET]], base=0, channel_multiplier=0,
                           allow_small_or_imprecise_dtypes=True).then_inc(iotas, 1)
            nc.gpsimd.iota(step_no[:], [[P, KC]], base=0, channel_multiplier=1,
                           allow_small_or_imprecise_dtypes=True).then_inc(iotas, 1)
            nc.gpsimd.iota(part_no[:], [[1, 1]], base=0, channel_multiplier=1,
                           allow_small_or_imprecise_dtypes=True).then_inc(iotas, 1)
            nc.gpsimd.iota(K["node_no"][:], [[1, P]], base=0, channel_multiplier=0,
                           allow_small_or_imprecise_dtypes=True).then_inc(iotas, 1)
            nc.gpsimd.memset(K["ones"][:], 1.0).then_inc(iotas, 1)
            nc.gpsimd.memset(minus1[:], -1.0).then_inc(iotas, 1)
            nc.gpsimd.memset(minus_big[:], -BIG).then_inc(iotas, 1)
            pool.wait_ge(steps_ok, 1)
            for c in range(KC):
                for rows, table in ((src_r, src_d), (dst_r, dst_d), (w_r, w_d)):
                    pool.indirect_dma_start(
                        out=rows[:, c, :], out_offset=None, in_=table,
                        in_offset=bass.IndirectOffsetOnAxis(ap=i_int[:, c:c + 1], axis=0)).then_inc(rows_in, 16)

        @block.tensor
        def _(pe):
            pe.wait_ge(dve, 3)
            for a in range(0, ET, 512):
                b = min(a + 512, ET)
                mm = nc.tensor.matmul(wide[:, a:b], K["ones"][0:1, :], last_tile[0:1, a:b], start=True, stop=True)
            mm.then_inc(j_bcast, 1)
            pe.wait_ge(diag_ok, 1)
            flat = diag[:].rearrange("p c e -> p (c e)")
            for a in range(0, STEPS, 512):
                b = min(a + 512, STEPS)
                mm = nc.tensor.matmul(wide[:, a:b], K["ones"][:], flat[:, a:b], start=True, stop=True)
            mm.then_inc(row_ok, 1)
            pe.wait_ge(end_ok, 1)
            nc.tensor.matmul(turned[:, 3, 0:P], K["ones"][:], end_diag[:], start=True, stop=True).then_inc(endb_ok, 1)
            for n, (a, c0) in enumerate(groups):
                rows = (src_f, rel, w_r)[a]
                pe.wait_ge(turn_ready, 1)
                if n >= 3:
                    pe.wait_ge(kept_ok, n - 2)
                for c in range(c0, min(c0 + 4, KC)):
                    mm = nc.tensor.transpose(turned[:, n % 3, (c - c0) * P:(c - c0 + 1) * P], rows[:, c, :],
                                             K["ident"][:])
                mm.then_inc(turned_ok, 1)

        @block.vector
        def _(v):
            count = [0]

            def then(ins):
                count[0] += 1
                ins.then_inc(dve, 1)
                v.wait_ge(dve, count[0])

            v.wait_ge(iotas, 7)
            then(nc.vector.tensor_scalar(K["ident"][:], K["node_no"][:], part_no[:, 0:1], None, ALU.is_equal))
            v.wait_ge(last_in, 16)
            then(nc.vector.tensor_scalar(last_tile_i[:], last_dst[:], 7, None, ALU.arith_shift_right))
            then(nc.vector.tensor_scalar(last_tile[:], last_tile_i[:], float(NT - 1), None, ALU.min))
            v.wait_ge(j_bcast, 1)
            then(nc.vector.tensor_copy(J[:], wide[:, 0:ET]))
            then(nc.vector.tensor_tensor(L[:], J[:], tile_no[:], ALU.add))
            for c in range(KC):
                then(nc.vector.tensor_scalar(junk[:], L[:], step_no[:, c:c + 1], 0.0, ALU.is_lt, ALU.add,
                                             accum_out=i_of[:, c:c + 1]))
            then(nc.vector.tensor_scalar(junk[:], J[:], part_no[:, 0:1], 0.0, ALU.is_le, ALU.add,
                                         accum_out=end_of[:]))
            then(nc.vector.tensor_scalar(end_of[:], end_of[:], part_no[:, 0:1], float(STEPS - 1), ALU.add, ALU.min))
            nc.vector.tensor_copy(i_int[:], i_of[:]).then_inc(steps_ok, 1)
            then(nc.vector.tensor_tensor(j_of[:], step_no[:], i_of[:], ALU.subtract))
            then(nc.vector.tensor_scalar(j_of[:], j_of[:], float(NT - 1), None, ALU.min))
            then(nc.vector.tensor_scalar(j_base[:], j_of[:], float(P), None, ALU.mult))
            nc.vector.tensor_tensor(diag[:], K["ident"][:].unsqueeze(1).to_broadcast([P, KC, P]),
                                    j_of[:].unsqueeze(2).to_broadcast([P, KC, P]), ALU.mult).then_inc(diag_ok, 1)
            then(nc.vector.tensor_copy(end_int[:], end_of[:]))
            then(nc.vector.tensor_scalar(end_slot_i[:], end_int[:], GA - 1, None, ALU.bitwise_and))
            then(nc.vector.tensor_copy(end_slot[:], end_slot_i[:]))
            then(nc.vector.tensor_scalar(end_row[:], end_of[:], float(P), None, ALU.mult))
            then(nc.vector.scalar_tensor_tensor(out=end_row[:], in0=end_slot[:], scalar=float(1 - P), in1=end_row[:],
                                                op0=ALU.mult, op1=ALU.add))
            nc.vector.tensor_scalar(end_diag[:], K["ident"][:], end_row[:, 0:1], None, ALU.mult).then_inc(end_ok, 1)
            then(nc.vector.tensor_scalar(slot_off[:], part_no[:], float(GA), None, ALU.mult))
            v.wait_ge(row_ok, 1)
            then(nc.vector.tensor_copy(j_row[:], wide[:, 0:STEPS]))
            nc.vector.memset(K["keep"][:, 0:1], 0.0)
            nc.vector.tensor_tensor(K["keep"][:, 1:], j_row[:, 1:], j_row[:, 0:STEPS - 1], ALU.is_equal)
            nc.vector.tensor_copy(K["j_int"][:, 0:STEPS], j_row[0:1, :])
            then(nc.vector.memset(is_last[:, STEPS - 1:STEPS], 1.0))
            then(nc.vector.tensor_tensor(is_last[:, 0:STEPS - 1], j_row[0:1, 1:], j_row[0:1, 0:STEPS - 1],
                                         ALU.not_equal))
            nc.vector.tensor_copy(K["last_int"][:, 0:STEPS], is_last[:])
            v.wait_ge(endb_ok, 1)
            then(nc.vector.tensor_scalar(K["end_idx"][:], turned[:, 3, 0:NT], slot_off[:, 0:1], None, ALU.add))
            v.wait_ge(rows_in, 16 * 3 * KC)
            nc.vector.tensor_copy(src_f[:], src_r[:])
            then(nc.vector.tensor_copy(dst_f[:], dst_r[:]))
            v.nop(nofuse=True).then_inc(dst_ready, 1)
            then(nc.vector.tensor_tensor(rel[:], dst_f[:], j_base[:].unsqueeze(2).to_broadcast([P, KC, P]),
                                         ALU.subtract))
            v.nop(nofuse=True).then_inc(turn_ready, 1)
            then(nc.vector.tensor_scalar(mask[:], rel[:], 0.0, -BIG, ALU.is_lt, ALU.mult))
            then(nc.vector.tensor_scalar(over[:], rel[:], float(P), -BIG, ALU.is_ge, ALU.mult))
            nc.vector.tensor_tensor(mask[:], mask[:], over[:], ALU.add).then_inc(gates_ready, 1)
            v.wait_ge(prev_in, 16)
            then(nc.vector.tensor_tensor(gate[:], dst_f[:], prev_f[:], ALU.not_equal))
            then(nc.vector.tensor_scalar(gate[:], gate[:], -BIG, None, ALU.mult))
            nc.vector.tensor_reduce(inner[:], gate[:, :, 1:], AX.X, ALU.add).then_inc(gates_ready, 1)
            for n, (a, c0) in enumerate(groups):
                v.wait_ge(turned_ok, n + 1)
                c1 = min(c0 + 4, KC)
                nc.vector.tensor_copy((K["src_idx"], K["rel"], K["w"])[a][:, c0 * P:c1 * P],
                                      turned[:, n % 3, 0:(c1 - c0) * P]).then_inc(kept_ok, 1)


GA = 32
GC = 16


class Links:

    def __init__(self, engine, sem, per_chunk):
        self.engine, self.sem, self.per_chunk = engine, sem, per_chunk

    def start(self, c):
        self.base, self.n = c * self.per_chunk, 0

    def wrote(self, ins):
        self.n += 1
        ins.then_inc(self.sem, 1)

    def wait(self):
        self.engine.wait_ge(self.sem, self.base + self.n)

    def __call__(self, ins):
        self.wrote(ins)
        self.wait()

    def later(self, ins):
        self.wrote(ins)
        yield
        self.wait()

    def end(self):
        assert self.n == self.per_chunk, (self.n, self.per_chunk)


def wait_from(engine, sem, value):
    if not isinstance(value, int) or value > 0:
        engine.wait_ge(sem, value)


SPREAD, TAIL, SUM, SUMS_END, SCORE, CHAIN = range(6)


def round_events(G, lead, early, chain_steps):
    events = [(SPREAD, g) for g in range(lead)] + [(TAIL, 0)]
    left = G - lead
    done = 0
    for n in range(left):
        events.append((SPREAD, lead + n))
        while done < early * (n + 1) // left:
            events.append((SUM, done))
            done += 1
    events.append((SCORE, 0))
    chained = 0
    for n in range(G - early):
        want = chain_steps * (n + 1) // (G - early)
        events += [(CHAIN, s) for s in range(chained, want)]
        chained = want
        events.append((SUM, early + n))
    return events + [(SUMS_END, 0)]


def edge_phase(nc, K, part, heads, features, feat_w, tab_d, tab_w, dram, out_d):
    G = GA if heads == 1 else GC
    R = heads * G
    HB = 32 // G
    HD = H * D
    HA = 3
    chunks = STEPS // G
    Q = 8
    assert STEPS % (2 * G) == 0 and R in (32, 128) and G % Q == 0
    row_w = DA if heads == 1 else feat_w
    sum_w = DA if heads == 1 else WC
    chain_steps = CHAIN_STEPS[heads]
    events = round_events(G, 4, G * 3 // 4 if heads == 1 else G // 2, chain_steps)
    with ExitStack() as ctx:
        T = Tools(nc, ctx, part)
        sb, ps, sem = T.sb, T.ps, T.sem
        X = sb("X", [P, 2, G, row_w])
        M = sb("M", [P, 2, G, P])
        MT = sb("MT", [P, 4, P])
        tab = sb("tab", [P, NT, tab_w])
        idx = sb("idx", [P, 2, G], I32)
        rel = sb("rel", [P, 2, G])
        keep = sb("keep", [P, 2, G])
        score = sb("score", [P, G * heads])
        gates = sb("gates", [R, 2, GATE_W])
        raw = sb("raw", [R, P])
        S = sb("S", [R, P])
        fwd = sb("fwd", [R, P])
        fwd2 = sb("fwd2", [R, P])
        bwd = sb("bwd", [R, P])
        top = sb("top", [R, P])
        wts = sb("wts", [R, P])
        gsum = sb("gsum", [R, 64])
        gsumT = sb("gsumT", [R, 64])
        ends = sb("ends", [R, 32])
        inj_gate = sb("inj_gate", [R, HB])
        inj = sb("inj", [R, HB])
        run = sb("run", [R, 33])
        cin = sb("cin", [R, 32])
        ends_b = sb("ends_b", [R, 32])
        run_b = sb("run_b", [R, 33])
        bin_ = sb("bin", [R, 32])
        carry = sb("carry", [R, 2, HB])
        dlt = sb("dlt", [R, 1])
        V = sb("V", [R, P])
        head_sel = sb("head_sel", [R, heads])
        wtT = sb("wtT", [P, R])
        fac = sb("fac", [P, heads])
        kfac = sb("kfac", [P, 1])
        aX = sb("aX", [P, 4, sum_w])
        if heads == 1:
            junk = sb("junk", [P, 4, DA])
            acc = sb("acc", [P, 2, G, sum_w])
            pE = ps("pE", [P, 2, 512])
            pS = ps("pS", [P, 2, 512])
        else:
            acc = sb("acc", [P, 4, sum_w])
            last = sb("last", [P, sum_w])
            score2 = sb("score2", [P, G * heads])
            raw2 = sb("raw2", [R, P])
            S2 = sb("S2", [R, P])
            wts2 = sb("wts2", [R, P])
            wtT2 = sb("wtT2", [P, R])
            pE = ps("pE", [P, 1, 512])
            pS = ps("pS", [P, 2, 1024])
        pMT = ps("pMT", [P, 2, 512])
        pT = ps("pT", [P, 2 if heads == 1 else 1, 512])
        p_fac = pT[:, 1, 0:heads] if heads == 1 else pE[:, 0, 512 - heads:512]

        rows_in = [[sem(f"rows_in{b}_{q}") for q in range(G // Q)] for b in (0, 1)]
        tab_in = sem("tab_in")
        gates_in = [sem(f"gates_in{b}") for b in (0, 1)]
        gates_free = sem("gates_free")
        idx_copied = sem("idx_copied")
        small_ok = sem("small_ok")
        m_ok = sem("m_ok")
        mt_ps = sem("mt_ps")
        mt_ok = sem("mt_ok")
        spread = sem("spread")
        read_e = sem("read_e")
        score_ok = sem("score_ok")
        score_ps = sem("score_ps")
        diff_ok = sem("diff_ok")
        exp_ok = sem("exp_ok")
        wts_ok = sem("wts_ok")
        wt_ps = sem("wt_ps")
        wtT_ok = sem("wtT_ok")
        v_ok = sem("v_ok")
        fac_ps = sem("fac_ps")
        fac_ok = sem("fac_ok")
        ax_dve = sem("ax_dve")
        ax_ok = sem("ax_ok")
        sum_ps = sem("sum_ps")
        sum_ok = sem("sum_ok")
        out_done = [sem(f"out{b}") for b in range(2 if heads == 1 else 4)]
        link_s, link_t, link_c = sem("link_s"), sem("link_t"), sem("link_c")

        block = ctx.enter_context(nc.Block())

        def pairs(engine):
            return engine.Fori(0, chunks // 2)

        def rounds(engine, one_round):
            one_round(0, 0, True, False)
            with engine.Fori(0, (chunks - 2) // 2) as i:
                one_round(i * 2 + 1, 1, True, True)
                one_round(i * 2 + 2, 0, True, True)
            one_round(chunks - 1, 1, True, True)
            one_round(chunks, 0, False, True)

        @block.gpsimd
        def _(pool):
            nc.gpsimd.memset(head_sel[:], 1.0).then_inc(small_ok, 1)
            pool.wait_ge(small_ok, 1)
            for h in range(heads):
                nc.gpsimd.affine_select(out=head_sel[:, h:h + 1], in_=head_sel[:, h:h + 1], pattern=[[0, 1]],
                                        compare_op=ALU.is_equal, fill=0.0, base=-h * G,
                                        channel_multiplier=1).then_inc(small_ok, 1)
            with pairs(pool) as i:
                for b in (0, 1):
                    for q in range(G // Q):
                        until(pool, sum_ok, i * (2 * G) + b * G + q * Q + Q)
                        if q == 0:
                            nc.gpsimd.tensor_copy(
                                idx[:, b, :], K["src_idx"][:, bass.ds(i * (2 * G) + b * G, G)]).then_inc(idx_copied, 1)
                            until(pool, idx_copied, i * 2 + b + 1)
                        for g in range(q * Q, q * Q + Q):
                            pool.indirect_dma_start(
                                out=X[:, b, g, 0:feat_w], out_offset=None, in_=features,
                                in_offset=bass.IndirectOffsetOnAxis(ap=idx[:, b, g:g + 1], axis=0)
                            ).then_inc(rows_in[b][q], 16)

        @block.sync
        def _(sp):
            sp.dma_start(tab[:], tab_d.rearrange("(t p) w -> p t w", p=P)).then_inc(tab_in, 16)

            def load_gates(c, b):
                until(sp, gates_free, c + 1)
                for h in range(heads):
                    sp.dma_start(gates[h * G:(h + 1) * G, b, :],
                                 dram["gates"][bass.ds(c * G, G), :]).then_inc(gates_in[b], 16)

            def store(c, b):
                if heads == 1:
                    until(sp, sum_ok, c * G + 3 * G)
                    sp.dma_start(out_d[bass.ds(c, 1)].rearrange("a p g w -> p (a g w)"),
                                 acc[:, b, :, :].rearrange("p g w -> p (g w)")).then_inc(out_done[b], 16)
                    return
                _, tiles = nc.values_load_multi_w_load_instructions(
                    K["j_int"][0:1, bass.ds(c * G, G)], engines=[SP_ENGINE], min_val=0, max_val=NT - 1,
                    skip_runtime_bounds_check_because="j of a step is at most NT - 1")
                _, lasts = nc.values_load_multi_w_load_instructions(
                    K["last_int"][0:1, bass.ds(c * G, G)], engines=[SP_ENGINE], min_val=0, max_val=1,
                    skip_runtime_bounds_check_because="a flag")
                for g in range(G):
                    until(sp, sum_ok, c * G + g + 1 + 2 * G)
                    sp.dma_start(out_d[bass.ds(tiles[g] * P, P), :], acc[:, g % 4, :],
                                 cond=(lasts[g] > 0)).then_inc(out_done[g % 4], 16)

            def one_round(c, b, scores, sums):
                if scores:
                    load_gates(c, b)
                if sums:
                    store(c - 1, 1 - b)

            rounds(sp, one_round)
            for s in out_done:
                sp.wait_ge(s, 16 + 16 * (chunks // 2 if heads == 1 else STEPS // 4))

        @block.tensor
        def _(pe):
            pe.wait_ge(tab_in, 16)

            def one_round(c, b, scores, sums):
                k0 = c * G
                k1 = (c - 1) * G
                tiles = []

                def spread_table(g):
                    pe.wait_ge(mt_ok, k0 + g + 1)
                    if heads == 1:
                        wait_from(pe, read_e, k0 + g - 1)
                        o = pE[:, g % 2, 0:tab_w]
                    else:
                        o = pE[:, 0, g * tab_w:(g + 1) * tab_w]
                        if g == 0:
                            wait_from(pe, read_e, c)
                    nc.tensor.matmul(o, MT[:, g % 4, :],
                                     tab[:, bass.ds(tiles[g], 1), :].rearrange("p a w -> p (a w)"), start=True,
                                     stop=True).then_inc(spread, 1)

                def add_up(g):
                    pe.wait_ge(ax_ok, k1 + g + 1)
                    pe.wait_ge(sum_ok, k1 + g - 1 + 2 * G)
                    m = M[:, 1 - b, g, :]
                    if heads == 1:
                        mm = nc.tensor.matmul(pS[:, g % 2, 0:sum_w], m, aX[:, g % 4, :], start=True, stop=True)
                    else:
                        nc.tensor.matmul(pS[:, g % 2, 0:HD], m, aX[:, g % 4, 0:HD], start=True, stop=True)
                        mm = nc.tensor.matmul(pS[:, g % 2, HD:WC], m, aX[:, g % 4, HD:WC], start=True, stop=True)
                    mm.then_inc(sum_ps, 1)

                for kind, g in events:
                    if kind == SPREAD and scores:
                        if g % 8 == 0:
                            _, loaded = nc.values_load_multi_w_load_instructions(
                                K["j_int"][0:1, bass.ds(k0 + g, 8)], engines=[PE_ENGINE], min_val=0,
                                max_val=NT - 1, skip_runtime_bounds_check_because="j of a step is at most NT - 1")
                            tiles += loaded
                        pe.wait_ge(m_ok, k0 + g + 1)
                        wait_from(pe, mt_ok, k0 + g - 1)
                        nc.tensor.transpose(pMT[:, g % 2, 0:P], M[:, b, g, :], K["ident"][:]).then_inc(mt_ps, 1)
                        if g:
                            spread_table(g - 1)
                    if kind == SCORE and scores:
                        spread_table(G - 1)
                        pe.wait_ge(score_ok, c + 1)
                        mm = nc.tensor.transpose(pT[0:R, 0, 0:P], score[:], K["ident"][:])
                        if heads > 1:
                            mm = nc.tensor.transpose(pT[0:R, 0, P:2 * P], score2[:], K["ident"][:])
                        mm.then_inc(score_ps, 1)
                    if kind == TAIL and sums:
                        until(pe, v_ok, c)
                        nc.tensor.matmul(p_fac, V[:], head_sel[:], start=True, stop=True).then_inc(fac_ps, 1)
                        until(pe, wts_ok, c)
                        mm = nc.tensor.transpose(pT[:, 0, 0:R], wts[:], K["ident"][0:R, 0:R])
                        if heads > 1:
                            mm = nc.tensor.transpose(pT[:, 0, P:P + R], wts2[:], K["ident"][0:R, 0:R])
                        mm.then_inc(wt_ps, 1)
                    if kind == SUM and sums and g:
                        add_up(g - 1)
                    if kind == SUMS_END and sums:
                        add_up(G - 1)

            rounds(pe, one_round)

        @block.scalar
        def _(sc):
            def one_round(c, b, scores, sums):
                k0, k1 = c * G, (c - 1) * G
                for kind, g in events:
                    if kind == SPREAD and scores:
                        sc.wait_ge(mt_ps, k0 + g + 1)
                        wait_from(sc, spread, k0 + g - 3)
                        nc.scalar.copy(MT[:, g % 4, :], pMT[:, g % 2, 0:P]).then_inc(mt_ok, 1)
                    if kind == TAIL and sums:
                        sc.wait_ge(diff_ok, c)
                        ins = nc.scalar.activation(wts[:], S[:], ACT.Exp)
                        if heads > 1:
                            ins = nc.scalar.activation(raw2[:], S2[:], ACT.Exp)
                        ins.then_inc(wts_ok if heads == 1 else exp_ok, 1)
                        sc.wait_ge(fac_ps, c)
                        nc.scalar.activation(fac[:], p_fac, ACT.Exp).then_inc(fac_ok, 1)
                        sc.wait_ge(wtT_ok, c)
                    if kind == SUM and sums:
                        sc.wait_ge(sum_ps, k1 + g - 3 + 4)
                        x = X[:, 1 - b, g, :]
                        if heads == 1:
                            nc.scalar.activation(aX[:, g % 4, :], x, ACT.Copy,
                                                 scale=wtT[:, g:g + 1]).then_inc(ax_ok, 1)
                            continue
                        for h in range(HA):
                            nc.scalar.activation(aX[:, g % 4, h * D:(h + 1) * D], x[:, 0:D], ACT.Copy,
                                                 scale=wtT[:, h * G + g:h * G + g + 1])
                        nc.scalar.copy(aX[:, g % 4, HD:HD + H], wtT[:, g::G])
                        sc.wait_ge(ax_dve, k1 + g + 1)
                        nc.scalar.copy(aX[:, g % 4, HD + H:WC], wtT2[:, g::G]).then_inc(ax_ok, 1)

            rounds(sc, one_round)

        @block.vector
        def _(v):
            then_s = Links(v, link_s, SCORE_LINKS[heads])
            then_t = Links(v, link_t, TAIL_LINKS[heads])
            then_c = Links(v, link_c, chain_steps)
            if heads == 1:
                nc.vector.memset(X[:, :, :, D + 1:DA], 1.0)
            nc.vector.memset(gsum[:], 0.0)
            nc.vector.memset(run_b[:], -BIG)
            nc.vector.memset(acc[:], 0.0)
            nc.vector.memset(carry[:], -BIG)
            v.nop(nofuse=True).then_inc(gates_free, 2)
            v.nop(nofuse=True).then_inc(sum_ps, 4)
            nc.vector.memset(run[:], -BIG).then_inc(sum_ok, 2 * G)
            for s in out_done:
                v.nop(nofuse=True).then_inc(s, 16)
            v.wait_ge(small_ok, 1 + heads)
            v.wait_ge(sum_ok, 2 * G)

            def chain(c, b, use):
                then = then_c.later
                at_end, at_start = slice(31, 32), slice(0, 1)
                gate_f, gate_b, mask = (gates[:, b, n * P:(n + 1) * P] for n in range(3))
                first_place, inner = (gates[:, b, 3 * P + n:3 * P + n + 1] for n in range(2))
                old, new = carry[:, 1 - b, :], carry[:, b, :]
                v.wait_ge(gates_in[b], use * (16 * heads) + 16 * heads)
                nc.vector.tensor_tensor(gsum[:, 31:32], inner, gate_f[:, 0:1], ALU.add)
                yield from then(nc.vector.tensor_tensor(gsum[:, 32:33], inner, gate_b[:, P - 1:P], ALU.add))
                yield from then(nc.vector.transpose(gsumT[:], gsum[:]))
                yield from then(nc.vector.tensor_tensor(inj[:], old, gsumT[:, 0:32:G], ALU.add))
                nc.vector.memset(gsumT[:, 32 + G - 1:64:G], -BIG)
                yield from then(nc.vector.memset(gsumT[:, 0:32:G], -BIG))
                v.wait_ge(score_ps, c + 1)
                if heads > 1:
                    nc.vector.tensor_tensor(S2[:], pT[0:R, 0, P:2 * P], mask, ALU.add)
                yield from then(nc.vector.tensor_tensor(S[:], pT[0:R, 0, 0:P], mask, ALU.add))
                if heads > 1:
                    yield from then(nc.vector.tensor_tensor(raw[:], S[:], S2[:], ALU.max))
                T0 = raw if heads > 1 else S
                yield from then(nc.vector.tensor_tensor_scan(fwd[:], gate_f, T0[:], -BIG, ALU.add, ALU.max))
                yield from then(nc.vector.transpose(ends[:], fwd[:, P - 32:P]))
                yield from then(nc.vector.tensor_tensor(ends[:, 0:32:G], ends[:, 0:32:G], inj[:], ALU.max))
                yield from then(nc.vector.tensor_tensor_scan(run[:, 1:33], gsumT[:, 0:32], ends[:], -BIG, ALU.add,
                                                             ALU.max))
                yield from then(nc.vector.tensor_copy(new, run[:, G:33:G]))
                yield from then(nc.vector.tensor_copy(run[:, 0:32:G], old))
                yield from then(nc.vector.transpose(cin[:], run[:, 0:32]))
                yield from then(nc.vector.tensor_tensor_scan(fwd2[:], gate_f, T0[:], cin[:, at_end], ALU.add, ALU.max))
                yield from then(nc.vector.tensor_tensor_scan(bwd[:, ::-1], gate_b[:, ::-1], fwd2[:, ::-1], -BIG,
                                                             ALU.add, ALU.max))
                yield from then(nc.vector.transpose(ends_b[:], bwd[:, 0:32]))
                yield from then(nc.vector.tensor_tensor_scan(run_b[:, 31::-1], gsumT[:, 63:31:-1], ends_b[:, ::-1],
                                                             -BIG, ALU.add, ALU.max))
                if heads > 1:
                    yield from then(nc.vector.memset(run_b[:, G:G + 1], -BIG))
                yield from then(nc.vector.transpose(bin_[:], run_b[:, 1:33]))
                yield from then(nc.vector.tensor_tensor_scan(top[:, ::-1], gate_b[:, ::-1], fwd2[:, ::-1],
                                                             bin_[:, at_start], ALU.add, ALU.max))
                if heads > 1:
                    nc.vector.tensor_tensor(S2[:], S2[:], top[:], ALU.subtract)
                nc.vector.tensor_tensor(S[:], S[:], top[:], ALU.subtract).then_inc(diff_ok, 1)
                yield from then(nc.vector.tensor_tensor(dlt[:], cin[:, at_end], top[:, 0:1], ALU.subtract))
                yield from then(nc.vector.scalar_tensor_tensor(out=dlt[:], in0=gate_f[:, 0:1], scalar=0.0,
                                                               in1=dlt[:], op0=ALU.is_equal, op1=ALU.mult))
                nc.vector.tensor_scalar(V[:], K["node_no"][0:R, :], first_place, dlt[:, 0:1], ALU.is_equal,
                                        ALU.mult).then_inc(v_ok, 1)

            def one_round(c, b, scores, sums):
                k0, k1 = c * G, (c - 1) * G
                o = 1 - b
                use = c // 2 if isinstance(c, int) else (c - b) // 2
                keep_o = keep[:, o, :]

                def score_step(g):
                    v.wait_ge(spread, k0 + g + 1)
                    if g % Q == 0:
                        v.wait_ge(rows_in[b][g // Q], use * (16 * Q) + 16 * Q)
                    if g >= 4:
                        v.wait_ge(read_e, k0 + g - 3)
                    nc.vector.tensor_tensor_reduce(
                        out=junk[:, g % 4, :], in0=pE[:, g % 2, 0:DA], in1=X[:, b, g, :], scale=1.0, scalar=0.0,
                        op0=ALU.mult, op1=ALU.add, accum_out=score[:, g:g + 1]).then_inc(read_e, 1)

                def add_step(g):
                    v.wait_ge(sum_ps, k1 + g + 1 + 4)
                    if g > 0:
                        v.wait_ge(sum_ok, k1 + g + 2 * G)
                    if heads == 1:
                        prev = acc[:, o, g - 1, :] if g else acc[:, b, G - 1, :]
                        dst = acc[:, o, g, :]
                        factor = keep_o[:, g:g + 1] if g else kfac[:]
                        if g == 0:
                            v.wait_ge(out_done[o], (use_o * 16) + 16)
                    else:
                        prev = acc[:, (g - 1) % 4, :] if g else last[:]
                        dst = acc[:, g % 4, :]
                        factor = keep_o[:, g:g + 1]
                        v.wait_ge(out_done[g % 4], (c - 1) * (4 * G) + 4 * (g - g % 4) + 16)
                    nc.vector.scalar_tensor_tensor(out=dst, in0=prev, scalar=factor, in1=pS[:, g % 2, 0:sum_w],
                                                   op0=ALU.mult, op1=ALU.add).then_inc(sum_ok, 1)

                def weigh(g):
                    v.wait_ge(sum_ps, k1 + g - 3 + 4)
                    nc.vector.tensor_tensor(
                        aX[:, g % 4, HA * D:HD].rearrange("p (h d) -> p h d", d=D),
                        X[:, o, g, 0:D].unsqueeze(1).to_broadcast([P, H - HA, D]),
                        wtT[:, HA * G + g::G].unsqueeze(2).to_broadcast([P, H - HA, D]),
                        ALU.mult).then_inc(ax_dve, 1)

                use_o = (c - 1) // 2 if isinstance(c, int) else (c - 1 - o) // 2
                if scores:
                    then_s.start(c)
                    nc.vector.tensor_copy(keep[:, b, :], K["keep"][:, bass.ds(k0, G)])
                    if heads == 1:
                        nc.vector.tensor_copy(X[:, b, :, D], K["w"][:, bass.ds(k0, G)])
                    then_s(nc.vector.tensor_copy(rel[:, b, :], K["rel"][:, bass.ds(k0, G)]))
                    steps = chain(c, b, use)
                for kind, g in events:
                    if kind == SPREAD and scores:
                        nc.vector.tensor_scalar(M[:, b, g, :], K["node_no"][:], rel[:, b, g:g + 1], None,
                                                ALU.is_equal).then_inc(m_ok, 1)
                        if heads == 1 and g >= 2:
                            score_step(g - 2)
                    if kind == TAIL and sums:
                        then_t.start(c - 1)
                        if heads > 1:
                            v.wait_ge(exp_ok, c)
                            nc.vector.scalar_tensor_tensor(out=wts2[:], in0=gates[:, o, P:2 * P], scalar=0.0,
                                                           in1=raw2[:], op0=ALU.not_equal,
                                                           op1=ALU.mult).then_inc(wts_ok, 1)
                        until(v, fac_ok, c)
                        if heads == 1:
                            then_t(nc.vector.tensor_tensor(kfac[:], keep_o[:, 0:1], fac[:], ALU.mult))
                        else:
                            nc.vector.tensor_tensor(last[:, 0:HD].rearrange("p (h d) -> p h d", h=H),
                                                    acc[:, 3, 0:HD].rearrange("p (h d) -> p h d", h=H),
                                                    fac[:].unsqueeze(2).to_broadcast([P, H, D]), ALU.mult)
                            then_t(nc.vector.tensor_tensor(last[:, HD:WC].rearrange("p (a h) -> p a h", h=H),
                                                           acc[:, 3, HD:WC].rearrange("p (a h) -> p a h", h=H),
                                                           fac[:].unsqueeze(1).to_broadcast([P, 2, H]), ALU.mult))
                        until(v, wt_ps, c)
                        v.nop(nofuse=True).then_inc(gates_free, 1)
                        if heads > 1:
                            then_t(nc.vector.tensor_copy(wtT2[:], pT[:, 0, P:P + R]))
                        nc.vector.tensor_copy(wtT[:], pT[:, 0, 0:R]).then_inc(wtT_ok, 1)
                        if heads > 1:
                            v.wait_ge(wtT_ok, c)
                        then_t.end()
                    if kind == SUM and sums:
                        if heads > 1:
                            weigh(g)
                        if g >= 2:
                            add_step(g - 2)
                    if kind == SUMS_END and sums:
                        add_step(G - 2)
                        add_step(G - 1)
                        v.wait_ge(sum_ok, k1 + 3 * G)
                    if kind == SCORE and scores:
                        if heads == 1:
                            score_step(G - 2)
                            score_step(G - 1)
                            until(v, read_e, k0 + G)
                            v.nop(nofuse=True).then_inc(score_ok, 1)
                        else:
                            v.wait_ge(spread, k0 + G)
                            for q in range(G // Q):
                                v.wait_ge(rows_in[b][q], use * (16 * Q) + 16 * Q)
                            e3 = pE[:, 0, 0:G * 2 * heads].rearrange("p (g w) -> p g w", w=2 * heads)
                            s3 = score[:].rearrange("p (h g) -> p g h", g=G)
                            nc.vector.tensor_copy(score2[:].rearrange("p (h g) -> p g h", g=G), e3[:, :, heads:])
                            then_s(nc.vector.tensor_tensor(s3, e3[:, :, 0:heads], X[:, b, :, D:D + heads], ALU.add))
                            v.nop(nofuse=True).then_inc(read_e, 1)
                            nc.vector.scalar_tensor_tensor(out=score[:], in0=score[:], scalar=SLOPE, in1=score[:],
                                                           op0=ALU.mult, op1=ALU.max).then_inc(score_ok, 1)
                        then_s.end()
                        then_c.start(c)
                    if kind == CHAIN and scores:
                        next(steps, None)
                if scores:
                    for _ in steps:
                        pass
                    then_c.end()

            rounds(v, one_round)


CHAIN_STEPS = {1: 20, H: 22}
SCORE_LINKS = {1: 1, H: 2}
TAIL_LINKS = {1: 1, H: 2}


def group_loop(engine):
    return engine.Fori(0, NG // 2)


def group_rows(tensor, i, b):
    return tensor[bass.ds((i * 2 + b) * (GT * P), GT * P), :].rearrange("(t p) w -> p t w", p=P)


CUTS = ((0, 512), (512, GT * P))


def table_phase(nc, K, x_d, wq, bq, wk_t, tab_d):
    with ExitStack() as ctx:
        T = Tools(nc, ctx, "tab")
        x = T.sb("x", [P, 2, GT, D])
        xT = T.sb("xT", [D, 2, GT * P])
        qT = T.sb("qT", [D, 2, GT * P])
        out = T.sb("out", [P, 2, GT, DA])
        pA = [T.ps(f"pA{b}", [P, 1024]) for b in (0, 1)]
        pB = [T.ps(f"pB{b}", [P, 1024]) for b in (0, 1)]
        slot_free = [T.sem(f"slot_free{b}") for b in (0, 1)]
        x_in = [T.sem(f"x_in{b}") for b in (0, 1)]
        xT_ps, xT_ok, q_ps, q_ok, t_ps, t_ok = (T.sem(n) for n in ("xT_ps", "xT_ok", "q_ps", "q_ok", "t_ps", "t_ok"))
        block = ctx.enter_context(nc.Block())

        @block.gpsimd
        def _(pool):
            with group_loop(pool) as i:
                for b in (0, 1):
                    pool.wait_ge(slot_free[b], i * 16 + 16)
                    pool.dma_start(x[:, b], group_rows(x_d, i, b)).then_inc(x_in[b], 16)

        @block.tensor
        def _(pe):
            with group_loop(pe) as i:
                for b in (0, 1):
                    n = i * 2 + b + 1
                    until(pe, x_in[b], i * 16 + 16)
                    for t in range(GT):
                        mm = nc.tensor.transpose(pA[b][0:D, t * P:(t + 1) * P], x[:, b, t, :], K["ident"][:])
                    mm.then_inc(xT_ps, 1)
                    until(pe, xT_ok, n)
                    for lo, hi in CUTS:
                        mm = nc.tensor.matmul(pB[b][0:D, lo:hi], wq, xT[:, b, lo:hi], start=True, stop=True)
                    mm.then_inc(q_ps, 1)
                    until(pe, q_ok, n)
                    for t in range(GT):
                        mm = nc.tensor.matmul(pA[b][:, t * DA:(t + 1) * DA], qT[:, b, t * P:(t + 1) * P], wk_t,
                                              start=True, stop=True)
                    mm.then_inc(t_ps, 1)

        @block.scalar
        def _(sc):
            with group_loop(sc) as i:
                for b in (0, 1):
                    n = i * 2 + b + 1
                    sc.wait_ge(xT_ps, n)
                    nc.scalar.copy(xT[:, b, :], pA[b][0:D, 0:GT * P]).then_inc(xT_ok, 1)
                    sc.wait_ge(q_ps, n)
                    nc.scalar.activation(qT[:, b, :], pB[b][0:D, 0:GT * P], ACT.Identity, bias=bq).then_inc(q_ok, 1)

        @block.vector
        def _(v):
            for s in slot_free:
                v.nop(nofuse=True).then_inc(s, 16)
            with group_loop(v) as i:
                for b in (0, 1):
                    v.wait_ge(t_ps, i * 2 + b + 1)
                    nc.vector.tensor_scalar(out[:, b].rearrange("p t w -> p (t w)"), pA[b][:, 0:GT * DA],
                                            float(D) ** -0.5, None, ALU.mult).then_inc(t_ok, 1)

        @block.sync
        def _(sp):
            with group_loop(sp) as i:
                for b in (0, 1):
                    until(sp, t_ok, i * 2 + b + 1)
                    sp.dma_start(group_rows(tab_d, i, b), out[:, b]).then_inc(slot_free[b], 16)
            for s in slot_free:
                sp.wait_ge(s, 16 + 16 * (NG // 2))


class Chain:

    def __init__(self, engine, sem, per_round):
        self.engine, self.sem, self.per_round, self.n, self.base = engine, sem, per_round, 0, 0

    def start_round(self, i):
        self.before = self.n
        self.base = i * self.per_round

    def __call__(self, ins):
        self.n += 1
        ins.then_inc(self.sem, 1)
        self.engine.wait_ge(self.sem, self.base + self.n)

    def end_round(self):
        assert self.n - self.before == self.per_round, (self.n - self.before, self.per_round)


def spread_rows(x, shape):
    return x.unsqueeze(2).to_broadcast(shape)


def layer_norm(v, then, x, out, sq, stat, var_ok, std_ok, n):
    shape = [P, GT, D]
    mean, var = stat[:, 0, :], stat[:, 1, :]
    then(v.tensor_reduce(mean, x, AX.X, ALU.add))
    then(v.tensor_scalar(mean, mean, -1.0 / D, None, ALU.mult))
    then(v.tensor_tensor(x, x, spread_rows(mean, shape), ALU.add))
    then(v.tensor_tensor(sq, x, x, ALU.mult))
    then(v.tensor_reduce(var, sq, AX.X, ALU.add))
    v.tensor_scalar(var, var, 1.0 / D, LN_EPS, ALU.mult, ALU.add).then_inc(var_ok, 1)
    v.wait_ge(std_ok, n)
    then(v.reciprocal(stat[:, 3, :], stat[:, 2, :]))
    then(v.tensor_tensor(out, x, spread_rows(stat[:, 3, :], shape), ALU.mult))


def gather_sums(pool, nc, K, idx, b, out, sums_d, idx_ok, n, done):
    for t in range(GT):
        pool.indirect_dma_start(out=out[:, b, t, :], out_offset=None, in_=sums_d,
                                in_offset=bass.IndirectOffsetOnAxis(ap=idx[:, b, t:t + 1], axis=0)).then_inc(done, 16)


def middle_phase(nc, K, W, sums_d, x_d, h_d, tab_d):
    with ExitStack() as ctx:
        T = Tools(nc, ctx, "mid")
        idx = T.sb("idx", [P, 2, GT], I32)
        agg = T.sb("agg", [P, 2, GT, DA])
        x = T.sb("x", [P, 2, GT, D])
        rd = T.sb("rd", [P, 2, GT])
        aggT = T.sb("aggT", [DA, 2, GT * P])
        xT = T.sb("xT", [D, 2, GT * P])
        hT = T.sb("hT", [D, 2, GT * P])
        qT = T.sb("qT", [D, 2, GT * P])
        h = T.sb("h", [P, 2, GT, D])
        out = T.sb("out", [P, 2, GT, DA])
        pA = [T.ps(f"pA{b}", [P, 1024]) for b in (0, 1)]
        pB = [T.ps(f"pB{b}", [P, 1024]) for b in (0, 1)]
        slot_free = [T.sem(f"slot_free{b}") for b in (0, 1)]
        sums_in = [T.sem(f"sums_in{b}") for b in (0, 1)]
        x_in = [T.sem(f"x_in{b}") for b in (0, 1)]
        idx_ok, norm_ok, agg_ps, x_ps, aggT_ok, xT_ok, h_ps, h_ok, q_ps, q_ok, t_ps, t_ok, dve = (
            T.sem(n) for n in ("idx_ok", "norm_ok", "agg_ps", "x_ps", "aggT_ok", "xT_ok", "h_ps", "h_ok", "q_ps",
                               "q_ok", "t_ps", "t_ok", "dve"))
        block = ctx.enter_context(nc.Block())

        @block.gpsimd
        def _(pool):
            with group_loop(pool) as i:
                for b in (0, 1):
                    until(pool, slot_free[b], i * 32 + 32)
                    nc.gpsimd.tensor_copy(idx[:, b, :],
                                          K["end_idx"][:, bass.ds((i * 2 + b) * GT, GT)]).then_inc(idx_ok, 1)
                    until(pool, idx_ok, i * 2 + b + 1)
                    gather_sums(pool, nc, K, idx, b, agg, sums_d, idx_ok, i * 2 + b + 1, sums_in[b])

        @block.sync
        def _(sp):
            with group_loop(sp) as i:
                for b in (0, 1):
                    until(sp, t_ok, i * 2 + b + 1)
                    sp.dma_start(group_rows(tab_d, i, b), out[:, b]).then_inc(slot_free[b], 16)
                    sp.dma_start(group_rows(h_d, i, b), h[:, b]).then_inc(slot_free[b], 16)
            for s in slot_free:
                sp.wait_ge(s, 32 + 32 * (NG // 2))

        @block.tensor
        def _(pe):
            with group_loop(pe) as i:
                for b in (0, 1):
                    n = i * 2 + b + 1
                    until(pe, x_in[b], i * 16 + 16)
                    for t in range(GT):
                        mm = nc.tensor.transpose(pB[b][0:D, t * P:(t + 1) * P], x[:, b, t, :], K["ident"][:])
                    mm.then_inc(x_ps, 1)
                    until(pe, norm_ok, n)
                    for t in range(GT):
                        mm = nc.tensor.transpose(pA[b][0:DA, t * P:(t + 1) * P], agg[:, b, t, :], K["ident"][:])
                    mm.then_inc(agg_ps, 1)
                    until(pe, xT_ok, n)
                    until(pe, aggT_ok, n)
                    for lo, hi in CUTS:
                        nc.tensor.matmul(pA[b][0:D, lo:hi], W["wva1"][:], aggT[:, b, lo:hi], start=True, stop=False)
                        mm = nc.tensor.matmul(pA[b][0:D, lo:hi], W["ws1"][:], xT[:, b, lo:hi], start=False, stop=True)
                    mm.then_inc(h_ps, 1)
                    until(pe, h_ok, n)
                    for lo, hi in CUTS:
                        mm = nc.tensor.matmul(pB[b][0:D, lo:hi], W["wq2"][:], hT[:, b, lo:hi], start=True, stop=True)
                    mm.then_inc(q_ps, 1)
                    for t in range(GT):
                        nc.tensor.transpose(pA[b][:, t * D:(t + 1) * D], hT[:, b, t * P:(t + 1) * P],
                                            K["ident"][0:D, 0:D])
                    until(pe, q_ok, n)
                    for t in range(GT):
                        mm = nc.tensor.matmul(pB[b][:, t * DA:(t + 1) * DA], qT[:, b, t * P:(t + 1) * P],
                                              W["wk_t2"][:], start=True, stop=True)
                    mm.then_inc(t_ps, 1)

        @block.scalar
        def _(sc):
            with group_loop(sc) as i:
                for b in (0, 1):
                    n = i * 2 + b + 1
                    until(sc, slot_free[b], i * 32 + 32)
                    sc.dma_start(x[:, b], group_rows(x_d, i, b)).then_inc(x_in[b], 16)
                    sc.wait_ge(x_ps, n)
                    nc.scalar.copy(xT[:, b, :], pB[b][0:D, 0:GT * P]).then_inc(xT_ok, 1)
                    sc.wait_ge(h_ps, n)
                    nc.scalar.activation(hT[:, b, :], pA[b][0:D, 0:GT * P], ACT.Relu,
                                         bias=W["bs1"][:]).then_inc(h_ok, 1)
                    sc.wait_ge(q_ps, n)
                    nc.scalar.activation(qT[:, b, :], pB[b][0:D, 0:GT * P], ACT.Identity,
                                         bias=W["bq2"][:]).then_inc(q_ok, 1)

        @block.vector
        def _(v):
            for s in slot_free:
                v.nop(nofuse=True).then_inc(s, 32)
            then = Chain(v, dve, 4)
            with group_loop(v) as i:
                then.start_round(i)
                for b in (0, 1):
                    n = i * 2 + b + 1
                    v.wait_ge(sums_in[b], i * (16 * GT) + 16 * GT)
                    then(nc.vector.tensor_scalar(rd[:, b], agg[:, b, :, DA - 1], 0.5, None, ALU.max))
                    then(nc.vector.reciprocal(rd[:, b], rd[:, b]))
                    nc.vector.tensor_tensor(agg[:, b], agg[:, b], spread_rows(rd[:, b], [P, GT, DA]),
                                            ALU.mult).then_inc(norm_ok, 1)
                    v.wait_ge(agg_ps, n)
                    nc.vector.tensor_copy(aggT[:, b, :], pA[b][0:DA, 0:GT * P]).then_inc(aggT_ok, 1)
                    v.wait_ge(t_ps, n)
                    nc.vector.tensor_copy(h[:, b].rearrange("p t w -> p (t w)"), pA[b][:, 0:GT * D])
                    nc.vector.tensor_scalar(out[:, b].rearrange("p t w -> p (t w)"), pB[b][:, 0:GT * DA],
                                            float(D) ** -0.5, None, ALU.mult).then_inc(t_ok, 1)
                then.end_round()


def second_phase(nc, K, W, sums_d, h_d, x_d, x1_d, tab_d):
    with ExitStack() as ctx:
        T = Tools(nc, ctx, "sec")
        idx = T.sb("idx", [P, 2, GT], I32)
        agg = T.sb("agg", [P, 2, GT, DA])
        x = T.sb("x", [P, 2, GT, D])
        h = T.sb("h", [P, 2, GT, D])
        rd = T.sb("rd", [P, 2, GT])
        aggT = T.sb("aggT", [DA, 2, GT * P])
        hT = T.sb("hT", [D, 2, GT * P])
        y = T.sb("y", [P, 2, GT, D])
        sq = T.sb("sq", [P, GT, D])
        stat = T.sb("stat", [P, 4, GT])
        x1 = T.sb("x1", [P, 2, GT, D + H])
        x1T = T.sb("x1T", [D, 2, GT * P])
        out = T.sb("out", [P, 2, GT, 2 * H])
        pA = [T.ps(f"pA{b}", [P, 1024]) for b in (0, 1)]
        pB = [T.ps(f"pB{b}", [P, 1024]) for b in (0, 1)]
        slot_free = [T.sem(f"slot_free{b}") for b in (0, 1)]
        sums_in = [T.sem(f"sums_in{b}") for b in (0, 1)]
        x_in = [T.sem(f"x_in{b}") for b in (0, 1)]
        h_in = [T.sem(f"h_in{b}") for b in (0, 1)]
        idx_ok, norm_ok, agg_ps, h_ps, aggT_ok, hT_ok, y_ps, x1_ok, x1_ps, x1T_ok, a_ps, t_ok, dve, var_ok, std_ok = (
            T.sem(n) for n in ("idx_ok", "norm_ok", "agg_ps", "h_ps", "aggT_ok", "hT_ok", "y_ps", "x1_ok", "x1_ps",
                               "x1T_ok", "a_ps", "t_ok", "dve", "var_ok", "std_ok"))
        block = ctx.enter_context(nc.Block())

        @block.gpsimd
        def _(pool):
            with group_loop(pool) as i:
                for b in (0, 1):
                    until(pool, slot_free[b], i * 32 + 32)
                    nc.gpsimd.tensor_copy(idx[:, b, :],
                                          K["end_idx"][:, bass.ds((i * 2 + b) * GT, GT)]).then_inc(idx_ok, 1)
                    until(pool, idx_ok, i * 2 + b + 1)
                    gather_sums(pool, nc, K, idx, b, agg, sums_d, idx_ok, i * 2 + b + 1, sums_in[b])

        @block.sync
        def _(sp):
            with group_loop(sp) as i:
                for b in (0, 1):
                    until(sp, t_ok, i * 2 + b + 1)
                    sp.dma_start(group_rows(tab_d, i, b), out[:, b]).then_inc(slot_free[b], 16)
                    sp.dma_start(group_rows(x1_d, i, b), x1[:, b]).then_inc(slot_free[b], 16)
            for s in slot_free:
                sp.wait_ge(s, 32 + 32 * (NG // 2))

        @block.tensor
        def _(pe):
            with group_loop(pe) as i:
                for b in (0, 1):
                    n = i * 2 + b + 1
                    until(pe, h_in[b], i * 16 + 16)
                    for t in range(GT):
                        mm = nc.tensor.transpose(pB[b][0:D, t * P:(t + 1) * P], h[:, b, t, :], K["ident"][:])
                    mm.then_inc(h_ps, 1)
                    until(pe, norm_ok, n)
                    for t in range(GT):
                        mm = nc.tensor.transpose(pA[b][0:DA, t * P:(t + 1) * P], agg[:, b, t, :], K["ident"][:])
                    mm.then_inc(agg_ps, 1)
                    until(pe, hT_ok, n)
                    until(pe, aggT_ok, n)
                    for t in range(GT):
                        nc.tensor.matmul(pA[b][:, t * D:(t + 1) * D], aggT[:, b, t * P:(t + 1) * P], W["wva2"][:],
                                         start=True, stop=False)
                        mm = nc.tensor.matmul(pA[b][:, t * D:(t + 1) * D], hT[:, b, t * P:(t + 1) * P], W["ws2"][:],
                                              start=False, stop=True)
                    mm.then_inc(y_ps, 1)
                    until(pe, x1_ok, n)
                    for t in range(GT):
                        mm = nc.tensor.transpose(pB[b][0:D, t * P:(t + 1) * P], x1[:, b, t, 0:D], K["ident"][:])
                    mm.then_inc(x1_ps, 1)
                    until(pe, x1T_ok, n)
                    for t in range(GT):
                        mm = nc.tensor.matmul(pA[b][:, t * 2 * H:(t + 1) * 2 * H], x1T[:, b, t * P:(t + 1) * P],
                                              W["a_sd"][:], start=True, stop=True)
                    mm.then_inc(a_ps, 1)

        @block.scalar
        def _(sc):
            with group_loop(sc) as i:
                for b in (0, 1):
                    n = i * 2 + b + 1
                    until(sc, slot_free[b], i * 32 + 32)
                    sc.dma_start(h[:, b], group_rows(h_d, i, b)).then_inc(h_in[b], 16)
                    sc.dma_start(x[:, b], group_rows(x_d, i, b)).then_inc(x_in[b], 16)
                    sc.wait_ge(h_ps, n)
                    nc.scalar.copy(hT[:, b, :], pB[b][0:D, 0:GT * P]).then_inc(hT_ok, 1)
                    sc.wait_ge(var_ok, n)
                    nc.scalar.activation(stat[:, 2, :], stat[:, 1, :], ACT.Sqrt).then_inc(std_ok, 1)
                    sc.wait_ge(x1_ps, n)
                    nc.scalar.copy(x1T[:, b, :], pB[b][0:D, 0:GT * P]).then_inc(x1T_ok, 1)

        @block.vector
        def _(v):
            for s in slot_free:
                v.nop(nofuse=True).then_inc(s, 32)
            then = Chain(v, dve, 2 * 14)
            with group_loop(v) as i:
                then.start_round(i)
                for b in (0, 1):
                    n = i * 2 + b + 1
                    v.wait_ge(sums_in[b], i * (16 * GT) + 16 * GT)
                    then(nc.vector.tensor_scalar(rd[:, b], agg[:, b, :, DA - 1], 0.5, None, ALU.max))
                    then(nc.vector.reciprocal(rd[:, b], rd[:, b]))
                    nc.vector.tensor_tensor(agg[:, b], agg[:, b], spread_rows(rd[:, b], [P, GT, DA]),
                                            ALU.mult).then_inc(norm_ok, 1)
                    v.wait_ge(agg_ps, n)
                    nc.vector.tensor_copy(aggT[:, b, :], pA[b][0:DA, 0:GT * P]).then_inc(aggT_ok, 1)
                    v.wait_ge(y_ps, n)
                    v.wait_ge(x_in[b], i * 16 + 16)
                    p3 = pA[b][:, 0:GT * D].rearrange("p (t w) -> p t w", w=D)
                    then(nc.vector.tensor_tensor(y[:, b], p3, x[:, b], ALU.add))
                    then(nc.vector.tensor_tensor(y[:, b], y[:, b], over_tiles(W["bs2"]), ALU.add))
                    layer_norm(v, then, y[:, b], x1[:, b, :, 0:D], sq[:], stat, var_ok, std_ok, n)
                    v.nop(nofuse=True).then_inc(x1_ok, 1)
                    v.wait_ge(a_ps, n)
                    a3 = pA[b][:, 0:GT * 2 * H].rearrange("p (t w) -> p t w", w=2 * H)
                    then(nc.vector.tensor_copy(x1[:, b, :, D:], a3[:, :, 0:H]))
                    nc.vector.tensor_copy(out[:, b, :, 0:H], a3[:, :, H:])
                    then(nc.vector.tensor_tensor(out[:, b, :, H:], x1[:, b, :, D:], a3[:, :, H:], ALU.add))
                    then(nc.vector.scalar_tensor_tensor(out=out[:, b, :, H:], in0=out[:, b, :, H:], scalar=SLOPE,
                                                        in1=out[:, b, :, H:], op0=ALU.mult, op1=ALU.max))
                    v.nop(nofuse=True).then_inc(t_ok, 1)
                then.end_round()


def over_tiles(row):
    return row[:].unsqueeze(1).to_broadcast([P, GT, D])


def last_phase(nc, K, W, sums_d, x1_d, out_d):
    with ExitStack() as ctx:
        T = Tools(nc, ctx, "fin")
        agg = T.sb("agg", [P, 2, GT, WC])
        x1 = T.sb("x1", [P, 2, GT, D + H])
        own = T.sb("own", [P, GT, H])
        den = T.sb("den", [P, GT, H])
        ox = T.sb("ox", [P, H, D])
        aggT = T.sb("aggT", [P, GT, 4 * P])
        y = T.sb("y", [P, 2, GT, D])
        sq = T.sb("sq", [P, GT, D])
        stat = T.sb("stat", [P, 4, GT])
        z = T.sb("z", [P, 2, GT, D])
        zT = T.sb("zT", [D, 2, GT * P])
        hid = T.sb("hid", [P, 2, GT * P])
        out = T.sb("out", [P, 2, GT, D])
        pA = [T.ps(f"pA{b}", [P, 1024]) for b in (0, 1)]
        pB = [T.ps(f"pB{b}", [P, 1024]) for b in (0, 1)]
        slot_free = [T.sem(f"slot_free{b}") for b in (0, 1)]
        in_ok = [T.sem(f"in{b}") for b in (0, 1)]
        norm_ok, agg_ps, aggT_ok, y_ps, z_ok, z_ps, zT_ok, hid_ps, hid_ok, f_ps, o_ok, dve, var_ok, std_ok = (
            T.sem(n) for n in ("norm_ok", "agg_ps", "aggT_ok", "y_ps", "z_ok", "z_ps", "zT_ok", "hid_ps", "hid_ok",
                               "f_ps", "o_ok", "dve", "var_ok", "std_ok"))
        block = ctx.enter_context(nc.Block())
        HD = H * D

        @block.gpsimd
        def _(pool):
            with group_loop(pool) as i:
                for b in (0, 1):
                    until(pool, slot_free[b], i * 16 + 16)
                    pool.dma_start(agg[:, b], group_rows(sums_d, i, b)).then_inc(in_ok[b], 16)
                    pool.dma_start(x1[:, b], group_rows(x1_d, i, b)).then_inc(in_ok[b], 16)

        @block.sync
        def _(sp):
            with group_loop(sp) as i:
                for b in (0, 1):
                    until(sp, o_ok, i * 2 + b + 1)
                    sp.dma_start(group_rows(out_d, i, b), out[:, b]).then_inc(slot_free[b], 16)
            for s in slot_free:
                sp.wait_ge(s, 16 + 16 * (NG // 2))

        @block.tensor
        def _(pe):
            with group_loop(pe) as i:
                for b in (0, 1):
                    n = i * 2 + b + 1
                    t0 = (i * 2 + b) * GT
                    for t in range(GT + 1):
                        if t < GT:
                            until(pe, norm_ok, t0 + t + 1)
                            if t >= 2:
                                until(pe, aggT_ok, t0 + t - 1)
                            for q in range(4):
                                mm = nc.tensor.transpose(pA[b][:, (t % 2) * 512 + q * P:(t % 2) * 512 + (q + 1) * P],
                                                         agg[:, b, t, q * P:(q + 1) * P], K["ident"][:])
                            mm.then_inc(agg_ps, 1)
                        if t:
                            until(pe, aggT_ok, t0 + t)
                            for q in range(4):
                                mm = nc.tensor.matmul(pB[b][:, (t - 1) * D:t * D], aggT[:, t - 1, q * P:(q + 1) * P],
                                                      W["watt2"][:, q, :], start=(q == 0), stop=(q == 3))
                    mm.then_inc(y_ps, 1)
                    until(pe, z_ok, n)
                    for t in range(GT):
                        mm = nc.tensor.transpose(pA[b][0:D, t * P:(t + 1) * P], z[:, b, t, :], K["ident"][:])
                    mm.then_inc(z_ps, 1)
                    until(pe, zT_ok, n)
                    for lo, hi in CUTS:
                        mm = nc.tensor.matmul(pB[b][:, lo:hi], W["w1"][:], zT[:, b, lo:hi], start=True, stop=True)
                    mm.then_inc(hid_ps, 1)
                    until(pe, hid_ok, n)
                    for t in range(GT):
                        mm = nc.tensor.matmul(pA[b][:, t * D:(t + 1) * D], hid[:, b, t * P:(t + 1) * P], W["w2"][:],
                                              start=True, stop=True)
                    mm.then_inc(f_ps, 1)

        @block.scalar
        def _(sc):
            def root(n):
                sc.wait_ge(var_ok, n)
                nc.scalar.activation(stat[:, 2, :], stat[:, 1, :], ACT.Sqrt).then_inc(std_ok, 1)

            with group_loop(sc) as i:
                for b in (0, 1):
                    n = i * 2 + b + 1
                    t0 = (i * 2 + b) * GT
                    for t in range(GT):
                        sc.wait_ge(agg_ps, t0 + t + 1)
                        nc.scalar.copy(aggT[:, t, :], pA[b][:, (t % 2) * 512:(t % 2) * 512 + 4 * P]).then_inc(aggT_ok, 1)
                    root(i * 6 + b * 3 + 1)
                    sc.wait_ge(z_ps, n)
                    nc.scalar.copy(zT[:, b, :], pA[b][0:D, 0:GT * P]).then_inc(zT_ok, 1)
                    sc.wait_ge(hid_ps, n)
                    nc.scalar.activation(hid[:, b, :], pB[b][:, 0:GT * P], ACT.Relu, bias=W["b1"][:]).then_inc(hid_ok, 1)
                    root(i * 6 + b * 3 + 2)
                    root(i * 6 + b * 3 + 3)

        @block.vector
        def _(v):
            for s in slot_free:
                v.nop(nofuse=True).then_inc(s, 16)
            then = Chain(v, dve, 2 * FIN_LINKS)
            with group_loop(v) as i:
                then.start_round(i)
                for b in (0, 1):
                    n = i * 2 + b + 1
                    v.wait_ge(in_ok[b], i * 32 + 32)
                    sums = agg[:, b, :, HD:HD + H]
                    then(nc.vector.tensor_tensor(den[:], sums, agg[:, b, :, HD + H:], ALU.add))
                    then(nc.vector.scalar_tensor_tensor(out=own[:], in0=den[:], scalar=0.5, in1=agg[:, b, :, HD + H:],
                                                        op0=ALU.is_lt, op1=ALU.add))
                    then(nc.vector.tensor_tensor(den[:], sums, own[:], ALU.add))
                    then(nc.vector.tensor_scalar(den[:], den[:], SM_EPS, float(H), ALU.add, ALU.mult))
                    then(nc.vector.reciprocal(den[:], den[:]))
                    for t in range(GT):
                        a3 = agg[:, b, t, 0:HD].rearrange("p (h d) -> p h d", d=D)
                        then(nc.vector.tensor_tensor(ox[:], x1[:, b, t, 0:D].unsqueeze(1).to_broadcast([P, H, D]),
                                                     own[:, t, :].unsqueeze(2).to_broadcast([P, H, D]), ALU.mult))
                        then(nc.vector.tensor_tensor(a3, a3, ox[:], ALU.add))
                        nc.vector.tensor_tensor(a3, a3, den[:, t, :].unsqueeze(2).to_broadcast([P, H, D]),
                                                ALU.mult).then_inc(norm_ok, 1)
                    v.wait_ge(y_ps, n)
                    y3 = pB[b][:, 0:GT * D].rearrange("p (t w) -> p t w", w=D)
                    then(nc.vector.tensor_tensor(y[:, b], y3, x1[:, b, :, 0:D], ALU.add))
                    then(nc.vector.tensor_tensor(y[:, b], y[:, b], over_tiles(W["bias_att"]), ALU.add))
                    layer_norm(v, then, y[:, b], z[:, b], sq[:], stat, var_ok, std_ok, i * 6 + b * 3 + 1)
                    then(nc.vector.tensor_tensor(z[:, b], z[:, b], over_tiles(W["ln1_g"]), ALU.mult))
                    then(nc.vector.tensor_tensor(z[:, b], z[:, b], over_tiles(W["ln1_b"]), ALU.add))
                    v.nop(nofuse=True).then_inc(z_ok, 1)
                    v.wait_ge(f_ps, n)
                    f3 = pA[b][:, 0:GT * D].rearrange("p (t w) -> p t w", w=D)
                    then(nc.vector.tensor_tensor(y[:, b], f3, z[:, b], ALU.add))
                    then(nc.vector.tensor_tensor(y[:, b], y[:, b], over_tiles(W["b2"]), ALU.add))
                    layer_norm(v, then, y[:, b], z[:, b], sq[:], stat, var_ok, std_ok, i * 6 + b * 3 + 2)
                    then(nc.vector.tensor_tensor(z[:, b], z[:, b], over_tiles(W["ln2_g"]), ALU.mult))
                    then(nc.vector.tensor_tensor(z[:, b], z[:, b], over_tiles(W["ln2_b"]), ALU.add))
                    then(nc.vector.tensor_tensor(y[:, b], z[:, b], x1[:, b, :, 0:D], ALU.add))
                    layer_norm(v, then, y[:, b], out[:, b], sq[:], stat, var_ok, std_ok, i * 6 + b * 3 + 3)
                    v.nop(nofuse=True).then_inc(o_ok, 1)
                then.end_round()


FIN_LINKS = 5 + 2 * GT + 2 + 7 + 2 + 2 + 7 + 3 + 7


def load_weights(nc, K, W, w):
    with ExitStack() as ctx:
        T = Tools(nc, ctx, "wgt")
        att = T.sb("att", [D, H, D])
        vec = T.sb("vec", [D, 2, H, D])
        prod = T.sb("prod", [D, H, D])
        stack = [T.sb(f"stack{n}", [DA, D]) for n in (0, 1)]
        turned = T.ps("turned", [D, 2, 512])
        loads = T.sem("loads")
        dve = T.sem("dve")
        turned_ok = T.sem("turned_ok")
        block = ctx.enter_context(nc.Block())
        row = lambda a: a.rearrange("(a d) -> a d", a=1)
        col = lambda a: a.rearrange("(d a) -> d a", a=1)
        copies = [(att[:], w["W_att"].rearrange("d (h c) -> d h c", h=H)),
                  (vec[:, 0], w["att_src"].partition_broadcast(D)), (vec[:, 1], w["att_dst"].partition_broadcast(D)),
                  (W["w1"][:], w["W1"]), (W["b1"][:], col(w["b1"])), (W["w2"][:], w["W2"])]
        for n in (1, 2):
            s = stack[n - 1]
            copies += [(s[0:D, :], w[f"Wk{n}"]), (s[D:D + 1, :], w[f"We{n}"]), (s[D + 1:DA, :], row(w[f"bk{n}"])),
                       (W[f"wva{n}"][0:D, :], w[f"Wv{n}"]), (W[f"wva{n}"][D:D + 1, :], w[f"We{n}"]),
                       (W[f"wva{n}"][D + 1:DA, :], row(w[f"bv{n}"])), (W[f"wq{n}"][:], w[f"Wq{n}"]),
                       (W[f"bq{n}"][:], col(w[f"bq{n}"])), (W[f"ws{n}"][:], w[f"Ws{n}"])]
        copies += [(W["bs1"][:], col(w["bs1"])), (W["bs2"][:], w["bs2"].partition_broadcast(P))]
        copies += [(W[n][:], w[n].partition_broadcast(P)) for n in ("bias_att", "b2", "ln1_g", "ln1_b", "ln2_g",
                                                                    "ln2_b")]
        by_pair = w["W_att"].rearrange("d (q a o) -> a d q o", a=2, o=D)
        copies += [(W["watt2"][a * D:(a + 1) * D, :, :], by_pair[a]) for a in (0, 1)]

        @block.sync
        def _(sp):
            for dst, src in copies:
                sp.dma_start(dst, src).then_inc(loads, 16)
            sp.wait_ge(loads, 16 * len(copies))

        @block.tensor
        def _(pe):
            until(pe, loads, 16 * len(copies))
            for n in (0, 1):
                mm = nc.tensor.transpose(turned[:, n, 0:DA], stack[n][:], K["ident"][0:DA, 0:DA])
            mm.then_inc(turned_ok, 1)

        @block.vector
        def _(v):
            v.wait_ge(loads, 16 * len(copies))
            for n in (0, 1):
                nc.vector.tensor_tensor(prod[:], att[:], vec[:, n], ALU.mult).then_inc(dve, 1)
                v.wait_ge(dve, 2 * n + 1)
                nc.vector.tensor_reduce(W["a_sd"][:, n * H:(n + 1) * H], prod[:], AX.X, ALU.add).then_inc(dve, 1)
                v.wait_ge(dve, 2 * n + 2)
            v.wait_ge(turned_ok, 1)
            for n in (1, 2):
                nc.vector.tensor_copy(W[f"wk_t{n}"][:], turned[:, n - 1, 0:DA])


WEIGHTS = ["Wq1", "bq1", "Wk1", "bk1", "Wv1", "bv1", "We1", "Ws1", "bs1", "Wq2", "bq2", "Wk2", "bk2", "Wv2", "bv2",
           "We2", "Ws2", "bs2"]
WEIGHTS_L1 = ["W_att", "att_src", "att_dst", "bias_att", "W1", "b1", "W2", "b2", "ln1_g", "ln1_b", "ln2_g", "ln2_b"]


def build(nc, x, src, dst, ew, w, out):
    def scratch(name, shape):
        return nc.dram_tensor(f"scratch_{name}", shape, F32, kind="Internal").ap()

    dram = {"dst_flat": scratch("dst_flat", (STEPS * P + P,)), "gates": scratch("gates", (STEPS, GATE_W))}
    tab1, tab2 = scratch("tab1", (N_PAD, DA)), scratch("tab2", (N_PAD, DA))
    tab3 = scratch("tab3", (N_PAD, 2 * H))
    sums1, sums2 = (scratch(f"sums{n}", (STEPS // GA, P, GA, DA)) for n in (1, 2))
    sums3 = scratch("sums3", (N_PAD, WC))
    h, x1 = scratch("h", (N_PAD, D)), scratch("x1", (N_PAD, D + H))
    with ExitStack() as ctx:
        T = Tools(nc, ctx, "all")
        K = {"ident": T.sb("ident", [P, P]), "ones": T.sb("ones", [P, P]), "node_no": T.sb("node_no", [P, P]),
             "keep": T.sb("keep", [P, STEPS]), "j_int": T.sb("j_int", [1, STEPS], I32),
             "last_int": T.sb("last_int", [1, STEPS], I32), "end_idx": T.sb("end_idx", [P, NT], I32),
             "src_idx": T.sb("src_idx", [P, STEPS], I32), "rel": T.sb("rel", [P, STEPS]), "w": T.sb("w", [P, STEPS])}
        W = {"w1": T.sb("w1", [D, 2 * D]), "b1": T.sb("b1", [2 * D, 1]), "w2": T.sb("w2", [2 * D, D]),
             "a_sd": T.sb("a_sd", [D, 2 * H]), "watt2": T.sb("watt2", [P, H // 2, D]), "bs1": T.sb("bs1", [D, 1])}
        for n in (1, 2):
            W |= {f"wk_t{n}": T.sb(f"wk_t{n}", [D, DA]), f"wva{n}": T.sb(f"wva{n}", [DA, D]),
                  f"wq{n}": T.sb(f"wq{n}", [D, D]), f"bq{n}": T.sb(f"bq{n}", [D, 1]), f"ws{n}": T.sb(f"ws{n}", [D, D])}
        for n in ("bs2", "bias_att", "b2", "ln1_g", "ln1_b", "ln2_g", "ln2_b"):
            W[n] = T.sb(n, [P, D])
        build_schedule(nc, K, src, dst, ew, dram)
        load_weights(nc, K, W, w)
        table_phase(nc, K, x, W["wq1"][:], W["bq1"][:], W["wk_t1"][:], tab1)
        edge_phase(nc, K, "e1", 1, x, D, tab1, DA, dram, sums1)
        by_row = lambda s: s.rearrange("c p g w -> (c p g) w")
        middle_phase(nc, K, W, by_row(sums1), x, h, tab2)
        edge_phase(nc, K, "e2", 1, h, D, tab2, DA, dram, sums2)
        second_phase(nc, K, W, by_row(sums2), h, x, x1, tab3)
        edge_phase(nc, K, "e3", H, x1, D + H, tab3, 2 * H, dram, sums3)
        last_phase(nc, K, W, sums3, x1, out)


def lay_out(inputs):
    import numpy as np

    def edges(a, fill):
        a = np.ascontiguousarray(a).reshape(-1)
        return np.concatenate([a, np.full(E_PAD - E, fill, a.dtype)]).reshape(-1, P)

    x = np.ascontiguousarray(inputs["x"])
    arrays = {"x": np.concatenate([x, np.zeros((N_PAD - N, D), x.dtype)]), "src": edges(inputs["src"], 0),
              "dst": edges(inputs["dst"], NODE_PAD), "ew": edges(inputs["edge_weight1"], 0)}
    for n in WEIGHTS:
        arrays["w_" + n] = np.ascontiguousarray(inputs["L0_gnn_" + n])
    for n in WEIGHTS_L1:
        arrays["w_" + n] = np.ascontiguousarray(inputs["L1_gnn_" + n])
    return arrays


def kernel(**inputs):
    import concourse.bacc as bacc
    from concourse.bass_utils import run_bass_kernel_spmd

    arrays = lay_out(inputs)
    nc = bacc.Bacc("TRN2", target_bir_lowering=False, num_devices=1)
    t = {n: nc.dram_tensor(n, a.shape, mybir.dt.from_np(a.dtype), kind="ExternalInput").ap()
         for n, a in arrays.items()}
    out = nc.dram_tensor("out", (N_PAD, D), F32, kind="ExternalOutput").ap()
    build(nc, t["x"], t["src"], t["dst"], t["ew"], {n: t["w_" + n] for n in WEIGHTS + WEIGHTS_L1}, out)
    r = run_bass_kernel_spmd(nc, [arrays], core_ids=[0])
    return r.results[0]["out"][:N]
```

```python
import concourse.bass as bass
from concourse import mybir
from contextlib import ExitStack

F32 = mybir.dt.float32
I32 = mybir.dt.int32
BF16 = mybir.dt.bfloat16
ALU = mybir.AluOpType
ACT = mybir.ActivationFunctionType
AX = mybir.AxisListType
SP_ENGINE = mybir.EngineType.SP
PE_ENGINE = mybir.EngineType.PE
DVE_ENGINE = mybir.EngineType.DVE

P = 128
N = 12500
E = 200000
D = 64
H = 8
DA = D + 2
NT = -(-N // P)
ET = -(-E // P)
N_PAD = NT * P
E_PAD = (ET + 1) * P
NODE_PAD = 1 << 20
STEPS = 13 * P
KC = STEPS // P
assert STEPS >= ET + NT - 1 and STEPS - NT < ET + P
GT = 7
NG = NT // GT
assert NT % GT == 0 and NG % 2 == 0
GATE_W = 3 * P + 2
BIG = 1.0e30
LN_EPS = 1e-5
SM_EPS = 1e-16
SLOPE = 0.2
WC = H * D + 2 * H


def until(engine, sem, value):
    engine.wait_ge(sem, value)
    engine.nop(nofuse=True)


class Tools:

    def __init__(self, nc, ctx, part):
        self.nc, self.ctx, self.part, self.sems = nc, ctx, part, []
        ctx.callback(self.clear)

    def clear(self):
        if self.sems:
            self.nc.clear_and_free_semaphores(self.sems)
            self.nc.all_engine_barrier()

    def sb(self, name, shape, dt=F32):
        return self.ctx.enter_context(self.nc.sbuf_tensor(f"{self.part}_{name}", shape, dt))

    def ps(self, name, shape, dt=F32):
        return self.ctx.enter_context(self.nc.psum_tensor(f"{self.part}_{name}", shape, dt))

    def sem(self, name):
        self.sems.append(self.nc.alloc_semaphore(f"{self.part}_{name}"))
        return self.sems[-1]


def build_schedule(nc, K, src_d, dst_d, w_d, dram):
    with ExitStack() as ctx:
        T = Tools(nc, ctx, "sch")
        sb, ps, sem = T.sb, T.ps, T.sem
        last_dst = sb("last_dst", [1, ET], I32)
        last_tile_i = sb("last_tile_i", [1, ET], I32)
        last_tile = sb("last_tile", [1, ET])
        tile_no = sb("tile_no", [P, ET])
        J = sb("J", [P, ET])
        L = sb("L", [P, ET])
        junk = sb("junk", [P, ET])
        step_no = sb("step_no", [P, KC])
        part_no = sb("part_no", [P, 1])
        i_of = sb("i_of", [P, KC])
        i_int = sb("i_int", [P, KC], I32)
        j_of = sb("j_of", [P, KC])
        j_base = sb("j_base", [P, KC])
        diag = sb("diag", [P, KC, P])
        j_row = sb("j_row", [P, STEPS])
        is_last = sb("is_last", [1, STEPS])
        src_r = sb("src_r", [P, KC, P], I32)
        dst_r = sb("dst_r", [P, KC, P], I32)
        w_r = sb("w_r", [P, KC, P])
        src_f = sb("src_f", [P, KC, P])
        dst_f = sb("dst_f", [P, KC, P])
        rel = sb("rel", [P, KC, P])
        prev_f = sb("prev_f", [P, KC, P])
        gate = sb("gate", [P, KC, P])
        mask = sb("mask", [P, KC, P])
        over = sb("over", [P, KC, P])
        inner = sb("inner", [P, KC])
        minus1 = sb("minus1", [1, P])
        minus_big = sb("minus_big", [1, P])
        wide = ps("wide", [P, 2048])
        turned = ps("turned", [P, 4, 512])

        last_in = sem("last_in")
        iotas = sem("iotas")
        dve = sem("dve")
        j_bcast = sem("j_bcast")
        steps_ok = sem("steps_ok")
        diag_ok = sem("diag_ok")
        row_ok = sem("row_ok")
        rows_in = sem("rows_in")
        dst_ready = sem("dst_ready")
        dst_out = sem("dst_out")
        pads_out = sem("pads_out")
        prev_in = sem("prev_in")
        gates_ready = sem("gates_ready")
        gates_out = sem("gates_out")
        turn_ready = sem("turn_ready")
        turned_ok = sem("turned_ok")
        kept_ok = sem("kept_ok")

        groups = [(a, c0) for a in range(3) for c0 in range(0, KC, 4)]
        block = ctx.enter_context(nc.Block())

        @block.sync
        def _(sp):
            with nc.allow_non_contiguous_dma(reason="one element of each edge tile"):
                sp.dma_start(last_dst[:], dst_d[0:ET, P - 1:P].rearrange("t a -> a t")).then_inc(last_in, 16)
            sp.wait_ge(iotas, 7)
            sp.dma_start(dram["dst_flat"][0:P].rearrange("(a e) -> a e", a=1), minus1[:]).then_inc(pads_out, 16)
            sp.wait_ge(dst_ready, 1)
            sp.dma_start(dram["dst_flat"][P:P + STEPS * P].rearrange("(c p e) -> p c e", p=P, e=P),
                         dst_f[:]).then_inc(dst_out, 16)
            sp.wait_ge(dst_out, 16)
            sp.wait_ge(pads_out, 16)
            sp.dma_start(prev_f[:], dram["dst_flat"][P - 1:P - 1 + STEPS * P]
                         .rearrange("(c p e) -> p c e", p=P, e=P)).then_inc(prev_in, 16)
            sp.wait_ge(gates_ready, 2)
            rows = dram["gates"].rearrange("(c p) w -> p c w", p=P)
            stored = 0
            with nc.allow_non_contiguous_dma(reason="single elements of each step"):
                for out, in_ in (
                        (rows[:, :, 0:P], gate[:]),
                        (rows[:, :, P:2 * P - 1], gate[:, :, 1:]),
                        (dram["gates"][0:P - 1, 2 * P - 1:2 * P], gate[1:P, 0, 0:1]),
                        (dram["gates"][P - 1:STEPS - 1, 2 * P - 1:2 * P].rearrange("(c p) w -> p c w", p=P),
                         gate[:, 1:, 0:1]),
                        (dram["gates"][STEPS - 1:STEPS, 2 * P - 1:2 * P], minus_big[:, 0:1]),
                        (rows[:, :, 2 * P:3 * P], mask[:]),
                        (rows[:, :, 3 * P:3 * P + 1], rel[:, :, 0:1]),
                        (rows[:, :, 3 * P + 1:], inner[:].unsqueeze(2))):
                    sp.dma_start(out, in_).then_inc(gates_out, 16)
                    stored += 16
            sp.wait_ge(gates_out, stored)

        @block.gpsimd
        def _(pool):
            nc.gpsimd.iota(tile_no[:], [[1, ET]], base=0, channel_multiplier=0,
                           allow_small_or_imprecise_dtypes=True).then_inc(iotas, 1)
            nc.gpsimd.iota(step_no[:], [[P, KC]], base=0, channel_multiplier=1,
                           allow_small_or_imprecise_dtypes=True).then_inc(iotas, 1)
            nc.gpsimd.iota(part_no[:], [[1, 1]], base=0, channel_multiplier=1,
                           allow_small_or_imprecise_dtypes=True).then_inc(iotas, 1)
            nc.gpsimd.iota(K["node_no"][:], [[1, P]], base=0, channel_multiplier=0,
                           allow_small_or_imprecise_dtypes=True).then_inc(iotas, 1)
            nc.gpsimd.memset(K["ones"][:], 1.0).then_inc(iotas, 1)
            nc.gpsimd.memset(minus1[:], -1.0).then_inc(iotas, 1)
            nc.gpsimd.memset(minus_big[:], -BIG).then_inc(iotas, 1)
            pool.wait_ge(steps_ok, 1)
            for c in range(KC):
                for rows, table in ((src_r, src_d), (dst_r, dst_d), (w_r, w_d)):
                    pool.indirect_dma_start(
                        out=rows[:, c, :], out_offset=None, in_=table,
                        in_offset=bass.IndirectOffsetOnAxis(ap=i_int[:, c:c + 1], axis=0)).then_inc(rows_in, 16)

        @block.tensor
        def _(pe):
            pe.wait_ge(dve, 3)
            for a in range(0, ET, 512):
                b = min(a + 512, ET)
                mm = nc.tensor.matmul(wide[:, a:b], K["ones"][0:1, :], last_tile[0:1, a:b], start=True, stop=True)
            mm.then_inc(j_bcast, 1)
            pe.wait_ge(diag_ok, 1)
            flat = diag[:].rearrange("p c e -> p (c e)")
            for a in range(0, STEPS, 512):
                b = min(a + 512, STEPS)
                mm = nc.tensor.matmul(wide[:, a:b], K["ones"][:], flat[:, a:b], start=True, stop=True)
            mm.then_inc(row_ok, 1)
            for n, (a, c0) in enumerate(groups):
                rows = (src_f, rel, w_r)[a]
                pe.wait_ge(turn_ready, 1)
                if n >= 3:
                    pe.wait_ge(kept_ok, n - 2)
                for c in range(c0, min(c0 + 4, KC)):
                    mm = nc.tensor.transpose(turned[:, n % 3, (c - c0) * P:(c - c0 + 1) * P], rows[:, c, :],
                                             K["ident"][:])
                mm.then_inc(turned_ok, 1)

        @block.vector
        def _(v):
            count = [0]

            def then(ins):
                count[0] += 1
                ins.then_inc(dve, 1)
                v.wait_ge(dve, count[0])

            v.wait_ge(iotas, 7)
            then(nc.vector.tensor_scalar(K["ident"][:], K["node_no"][:], part_no[:, 0:1], None, ALU.is_equal))
            v.wait_ge(last_in, 16)
            then(nc.vector.tensor_scalar(last_tile_i[:], last_dst[:], 7, None, ALU.arith_shift_right))
            then(nc.vector.tensor_scalar(last_tile[:], last_tile_i[:], float(NT - 1), None, ALU.min))
            v.wait_ge(j_bcast, 1)
            then(nc.vector.tensor_copy(J[:], wide[:, 0:ET]))
            then(nc.vector.tensor_tensor(L[:], J[:], tile_no[:], ALU.add))
            for c in range(KC):
                then(nc.vector.tensor_scalar(junk[:], L[:], step_no[:, c:c + 1], 0.0, ALU.is_lt, ALU.add,
                                             accum_out=i_of[:, c:c + 1]))
            nc.vector.tensor_copy(i_int[:], i_of[:]).then_inc(steps_ok, 1)
            then(nc.vector.tensor_tensor(j_of[:], step_no[:], i_of[:], ALU.subtract))
            then(nc.vector.tensor_scalar(j_of[:], j_of[:], float(NT - 1), None, ALU.min))
            then(nc.vector.tensor_scalar(j_base[:], j_of[:], float(P), None, ALU.mult))
            nc.vector.tensor_tensor(diag[:], K["ident"][:].unsqueeze(1).to_broadcast([P, KC, P]),
                                    j_of[:].unsqueeze(2).to_broadcast([P, KC, P]), ALU.mult).then_inc(diag_ok, 1)
            v.wait_ge(row_ok, 1)
            then(nc.vector.tensor_copy(j_row[:], wide[:, 0:STEPS]))
            nc.vector.memset(K["keep"][:, 0:1], 0.0)
            nc.vector.tensor_tensor(K["keep"][:, 1:], j_row[:, 1:], j_row[:, 0:STEPS - 1], ALU.is_equal)
            nc.vector.tensor_copy(K["j_int"][:, 0:STEPS], j_row[0:1, :])
            then(nc.vector.memset(is_last[:, STEPS - 1:STEPS], 1.0))
            then(nc.vector.tensor_tensor(is_last[:, 0:STEPS - 1], j_row[0:1, 1:], j_row[0:1, 0:STEPS - 1],
                                         ALU.not_equal))
            nc.vector.tensor_copy(K["last_int"][:, 0:STEPS], is_last[:])
            v.wait_ge(rows_in, 16 * 3 * KC)
            nc.vector.tensor_copy(src_f[:], src_r[:])
            then(nc.vector.tensor_copy(dst_f[:], dst_r[:]))
            v.nop(nofuse=True).then_inc(dst_ready, 1)
            then(nc.vector.tensor_tensor(rel[:], dst_f[:], j_base[:].unsqueeze(2).to_broadcast([P, KC, P]),
                                         ALU.subtract))
            v.nop(nofuse=True).then_inc(turn_ready, 1)
            then(nc.vector.tensor_scalar(mask[:], rel[:], 0.0, -BIG, ALU.is_lt, ALU.mult))
            then(nc.vector.tensor_scalar(over[:], rel[:], float(P), -BIG, ALU.is_ge, ALU.mult))
            nc.vector.tensor_tensor(mask[:], mask[:], over[:], ALU.add).then_inc(gates_ready, 1)
            v.wait_ge(prev_in, 16)
            then(nc.vector.tensor_tensor(gate[:], dst_f[:], prev_f[:], ALU.not_equal))
            then(nc.vector.tensor_scalar(gate[:], gate[:], -BIG, None, ALU.mult))
            nc.vector.tensor_reduce(inner[:], gate[:, :, 1:], AX.X, ALU.add).then_inc(gates_ready, 1)
            for n, (a, c0) in enumerate(groups):
                v.wait_ge(turned_ok, n + 1)
                c1 = min(c0 + 4, KC)
                nc.vector.tensor_copy((K["src_idx"], K["rel"], K["w"])[a][:, c0 * P:c1 * P],
                                      turned[:, n % 3, 0:(c1 - c0) * P]).then_inc(kept_ok, 1)


LOADED = 16
GA = 32
GC = 16


class Links:

    def __init__(self, engine, sem, per_chunk):
        self.engine, self.sem, self.per_chunk = engine, sem, per_chunk

    def start(self, c):
        self.base, self.n = c * self.per_chunk, 0

    def wrote(self, ins):
        self.n += 1
        ins.then_inc(self.sem, 1)

    def wait(self):
        self.engine.wait_ge(self.sem, self.base + self.n)

    def __call__(self, ins):
        self.wrote(ins)
        self.wait()

    def later(self, ins):
        self.wrote(ins)
        yield
        self.wait()

    def end(self):
        assert self.n == self.per_chunk, (self.n, self.per_chunk)


def own(engine, value):
    if isinstance(value, int):
        return value
    register = engine.alloc_register()
    engine.reg_mov(register, value)
    return engine.snap(register)


def wait_from(engine, sem, value):
    if not isinstance(value, int) or value > 0:
        engine.wait_ge(sem, value)


(SPREAD, SPREAD_END, SCORE, SCALE, CHAIN, EXP, OWN, TURN, COLUMNS, SUM, SUMS_END) = range(11)


def round_events(G, chain_steps, chain_end):
    tail = {chain_end + n: kind for n, kind in enumerate((EXP, OWN, TURN, COLUMNS))}
    events, chained = [], 0
    for n in range(G):
        events.append((SPREAD, n))
        if n == LAG - 1:
            events += [(SCORE, 0), (SCALE, 0)]
        if n >= 1:
            want = min(chain_steps * n // (chain_end - 1), chain_steps)
            events += [(CHAIN, 0)] * (want - chained)
            chained = want
        if n in tail:
            events.append((tail[n], 0))
        if n >= LAG:
            events.append((SUM, n - LAG))
    return events + [(SPREAD_END, 0)] + [(SUM, n) for n in range(G - LAG, G)] + [(SUMS_END, 0)]


LAG = 1
SLOTS = 3


class Chunk:

    def __init__(self, no, slot, use, before):
        self.no, self.slot, self.use, self.before = no, slot, use, before


def edge_phase(nc, K, part, heads, features, feat_w, tab_d, tab_w, dram, out_d):
    G = GA if heads == 1 else GC
    R = heads * G
    HB = 32 // G
    HD = H * D
    HA = 3
    chunks = STEPS // G
    Q = 8
    assert STEPS % G == 0 and R in (32, 128) and G % Q == 0
    row_w = DA if heads == 1 else feat_w
    sum_w = DA if heads == 1 else WC
    chain_steps = CHAIN_STEPS[heads]
    events = round_events(G, chain_steps, CHAIN_END[heads])
    AHEAD = SLOTS * G + 4
    with ExitStack() as ctx:
        T = Tools(nc, ctx, part)
        sb, ps, sem = T.sb, T.ps, T.sem
        X = sb("X", [P, SLOTS, G, row_w])
        M = sb("M", [P, SLOTS, G, P])
        MT = sb("MT", [P, 4, P])
        tab = sb("tab", [P, NT, tab_w])
        idx = sb("idx", [P, SLOTS, G], I32)
        rel = sb("rel", [P, SLOTS, G])
        score = sb("score", [P, G * heads])
        gates = sb("gates", [R, SLOTS, GATE_W])
        raw = sb("raw", [R, P])
        S = sb("S", [R, P])
        fwd = sb("fwd", [R, P])
        fwd2 = sb("fwd2", [R, P])
        bwd = sb("bwd", [R, P])
        top = sb("top", [R, P])
        wts = sb("wts", [R, P])
        gsum = sb("gsum", [R, 64])
        gsumT = sb("gsumT", [R, 64])
        ends = sb("ends", [R, 32])
        inj = sb("inj", [R, HB])
        run = sb("run", [R, 33])
        cin = sb("cin", [R, 32])
        ends_b = sb("ends_b", [R, 32])
        run_b = sb("run_b", [R, 33])
        bin_ = sb("bin", [R, 32])
        carry = sb("carry", [R, SLOTS, HB])
        dlt = sb("dlt", [R, 1])
        V = sb("V", [R, P])
        head_sel = sb("head_sel", [R, heads])
        kinds = 1 if heads == 1 else 2
        wtT = sb("wtT", [P, SLOTS, kinds * R])
        fac = sb("fac", [P, heads])
        aX = sb("aX", [P, 4, row_w if heads == 1 else HD])
        node_sums = sb("node_sums", [P, 4, sum_w])
        if heads == 1:
            junk = sb("junk", [P, 4, DA])
            pE = ps("pE", [P, 2, 512])
            keep = sb("keep", [P, SLOTS, G])
            kfac = sb("kfac", [P, 1])
            pS = ps("pS", [P, 2, 512])
        else:
            score2 = sb("score2", [P, G * heads])
            raw2 = sb("raw2", [R, P])
            S2 = sb("S2", [R, P])
            wts2 = sb("wts2", [R, P])
            pE = ps("pE", [P, 1, 512])
            carried = sb("carried", [P, sum_w])
            zeros = sb("zeros", [P, 512], BF16)
            total = ps("total", [P, 1024])
        pMT = ps("pMT", [P, 2, 512])
        pT = ps("pT", [P, 2, 512])
        p_fac = pT[:, 1, 0:heads]

        rows_in = [[sem(f"rows_in{b}_{q}") for q in range(G // Q)] for b in range(SLOTS)]
        tab_in = sem("tab_in")
        gates_in = [sem(f"gates_in{b}") for b in range(SLOTS)]
        gates_free = sem("gates_free")
        idx_copied = sem("idx_copied")
        small_ok = sem("small_ok")
        m_ok = sem("m_ok")
        mt_ps = sem("mt_ps")
        mt_ok = sem("mt_ok")
        spread = sem("spread")
        read_e = sem("read_e")
        score_ok = sem("score_ok")
        score_ps = sem("score_ps")
        diff_ok = sem("diff_ok")
        exp_ok = sem("exp_ok")
        wts_ok = sem("wts_ok")
        wt_ps = sem("wt_ps")
        wtT_ok = sem("wtT_ok")
        v_ok = sem("v_ok")
        w_ok = sem("w_ok")
        fac_ps = sem("fac_ps")
        fac_ok = sem("fac_ok")
        ax_dve = sem("ax_dve")
        ax_ok = sem("ax_ok")
        sum_ps = sem("sum_ps")
        kfac_ok = sem("kfac_ok")
        scaled = sem("scaled")
        copied = sem("copied")
        closed = sem("closed")
        stored = sem("stored")
        rel_ok = sem("rel_ok")
        link_c = sem("link_c")

        sum_cuts = ((0, HD), (HD, WC))
        block = ctx.enter_context(nc.Block())

        def steps(engine, value):
            if engine.engine not in (PE_ENGINE, DVE_ENGINE):
                return value
            return nc.s_assert_within(own(engine, value), 0, STEPS - 2 * G,
                                      skip_runtime_bounds_check_because="steps before a chunk")

        def rounds(engine, one_round):
            def chunk(c, i):
                if i is None:
                    return Chunk(c, c % SLOTS, c // SLOTS, c * G) if 0 <= c < chunks else None
                return Chunk(i * SLOTS + c, c % SLOTS, i + c // SLOTS, steps(engine, (i * SLOTS + c) * G))

            def call(r, i=None):
                one_round(chunk(r, i), chunk(r - 1, i), chunk(r - 2, i))

            call(0)
            call(1)
            times = (chunks - 3) // SLOTS
            with engine.Fori(0, times) as i:
                for r in range(2, 2 + SLOTS):
                    call(r, i)
            for r in range(2 + times * SLOTS, chunks + 2):
                call(r)

        @block.gpsimd
        def _(pool):
            nc.gpsimd.memset(head_sel[:], 1.0).then_inc(small_ok, 1)
            pool.wait_ge(small_ok, 1)
            for h in range(heads):
                nc.gpsimd.affine_select(out=head_sel[:, h:h + 1], in_=head_sel[:, h:h + 1], pattern=[[0, 1]],
                                        compare_op=ALU.is_equal, fill=0.0, base=-h * G,
                                        channel_multiplier=1).then_inc(small_ok, 1)

            def gather(c, b):
                for q in range(G // Q):
                    until(pool, sum_ps, (c - SLOTS) * G + q * Q + Q + AHEAD)
                    if q == 0:
                        nc.gpsimd.tensor_copy(idx[:, b, :],
                                              K["src_idx"][:, bass.ds(c * G, G)]).then_inc(idx_copied, 1)
                        until(pool, idx_copied, c + 1)
                    for g in range(q * Q, q * Q + Q):
                        pool.indirect_dma_start(
                            out=X[:, b, g, 0:feat_w], out_offset=None, in_=features,
                            in_offset=bass.IndirectOffsetOnAxis(ap=idx[:, b, g:g + 1], axis=0)
                        ).then_inc(rows_in[b][q], 16)

            with pool.Fori(0, chunks // SLOTS) as i:
                for b in range(SLOTS):
                    gather(i * SLOTS + b, b)
            for c in range(chunks - chunks % SLOTS, chunks):
                gather(c, c % SLOTS)

        @block.sync
        def _(sp):
            sp.dma_start(tab[:], tab_d.rearrange("(t p) w -> p t w", p=P)).then_inc(tab_in, 16)

            def load_gates(new):
                until(sp, gates_free, new.no + 1)
                for h in range(heads):
                    sp.dma_start(gates[h * G:(h + 1) * G, new.slot, :],
                                 dram["gates"][bass.ds(new.before, G), :]).then_inc(gates_in[new.slot], 16)

            def store(old):
                for g in range(G):
                    if g % LOADED == 0:
                        _, tiles = nc.values_load_multi_w_load_instructions(
                            K["j_int"][0:1, bass.ds(old.before + g, LOADED)], engines=[SP_ENGINE], min_val=0,
                            max_val=NT - 1, skip_runtime_bounds_check_because="j of a step is at most NT - 1")
                        _, lasts = nc.values_load_multi_w_load_instructions(
                            K["last_int"][0:1, bass.ds(old.before + g, LOADED)], engines=[SP_ENGINE], min_val=0,
                            max_val=1, skip_runtime_bounds_check_because="a flag")
                    until(sp, closed, old.before + g + 1 + 2)
                    with sp.If(lasts[g % LOADED] > 0):
                        sp.dma_start(out_d[bass.ds(tiles[g % LOADED] * P, P), :],
                                     node_sums[:, g % 4, :]).then_inc(stored, 16)
                    with sp.Else():
                        sp.nop(nofuse=True).then_inc(stored, 16)
                    until(sp, stored, (old.before + g + 1) * 16 + 64)

            def one_round(new, mid, old):
                if new:
                    load_gates(new)
                if old:
                    store(old)

            rounds(sp, one_round)
            sp.wait_ge(stored, 16 * STEPS + 64)

        @block.tensor
        def _(pe):
            pe.wait_ge(tab_in, 16)

            def one_round(new, mid, old):
                tiles = []

                def spread_table(g):
                    if heads == 1:
                        o = pE[:, g % 2, 0:tab_w]
                    else:
                        o = pE[:, 0, g * tab_w:(g + 1) * tab_w]
                        if g == 0:
                            wait_from(pe, read_e, new.no)
                    nc.tensor.matmul(o, MT[:, g % 4, :],
                                     tab[:, bass.ds(tiles[g], 1), :].rearrange("p a w -> p (a w)"), start=True,
                                     stop=True).then_inc(spread, 1)

                lasts = []

                def product(m, rows, start, stop):
                    mm = None
                    for (lo, hi), part in zip(sum_cuts, rows):
                        mm = nc.tensor.matmul(total[:, lo:hi], m, part, start=start, stop=stop)
                    return mm

                def step_rows(g):
                    return [aX[:, g % 4, :], wtT[:, old.slot, g::G]]

                def start_sums():
                    pe.wait_ge(scaled, old.no + 1)
                    product(K["ident"][:], [carried[:, lo:hi] for lo, hi in sum_cuts], True, False)

                def load_lasts(g):
                    _, loaded = nc.values_load_multi_w_load_instructions(
                        K["last_int"][0:1, bass.ds(old.before + g, LOADED)], engines=[PE_ENGINE], min_val=0,
                        max_val=1, skip_runtime_bounds_check_because="a flag")
                    lasts.extend(loaded)

                def add_up(g):
                    pe.wait_ge(ax_ok, old.before + g + 1)
                    one_hot = M[:, old.slot, g, :]
                    if heads == 1:
                        pe.wait_ge(closed, old.before + g - 1 + 2)
                        nc.tensor.matmul(pS[:, g % 2, 0:DA], one_hot, aX[:, g % 4, :], start=True,
                                         stop=True).then_inc(sum_ps, 1)
                        return
                    pe.wait_ge(ax_dve, old.before + g + 1)
                    if g == G - 1:
                        product(one_hot, step_rows(g), False, True).then_inc(sum_ps, 1)
                        return
                    with pe.If(lasts[g] > 0):
                        product(one_hot, step_rows(g), False, True).then_inc(sum_ps, 1)
                        pe.wait_ge(closed, old.before + g + 1 + 2)
                        product(zeros[:, 0:P], [zeros[:, 0:hi - lo] for lo, hi in sum_cuts], True, False)
                    with pe.Else():
                        product(one_hot, step_rows(g), False, False).then_inc(sum_ps, 1)

                for kind, g in events:
                    if kind == SPREAD and new:
                        if g % LOADED == 0:
                            _, loaded = nc.values_load_multi_w_load_instructions(
                                K["j_int"][0:1, bass.ds(new.before + g, LOADED)], engines=[PE_ENGINE], min_val=0,
                                max_val=NT - 1, skip_runtime_bounds_check_because="j of a step is at most NT - 1")
                            tiles += loaded
                        pe.wait_ge(m_ok, new.before + g + 1)
                        wait_from(pe, mt_ok, new.before + g - 1)
                        nc.tensor.transpose(pMT[:, g % 2, 0:P], M[:, new.slot, g, :], K["ident"][:]).then_inc(mt_ps, 1)
                        if g >= 2:
                            spread_table(g - 2)
                    if kind == SPREAD_END and new:
                        for n in (G - 2, G - 1):
                            pe.wait_ge(mt_ok, new.before + n + 1)
                            if heads == 1:
                                wait_from(pe, read_e, new.before + n - 1)
                            spread_table(n)
                    if kind == SCORE and mid:
                        until(pe, score_ok, mid.no + 1)
                        mm = nc.tensor.transpose(pT[0:R, 0, 0:P], score[:], K["ident"][:])
                        if heads > 1:
                            mm = nc.tensor.transpose(pT[0:R, 0, P:2 * P], score2[:], K["ident"][:])
                        mm.then_inc(score_ps, 1)
                    if kind == EXP and mid:
                        until(pe, v_ok, mid.no + 1)
                        nc.tensor.matmul(p_fac, V[:], head_sel[:], start=True, stop=True).then_inc(fac_ps, 1)
                    if kind == TURN and mid:
                        until(pe, wts_ok, mid.no + 1)
                        mm = nc.tensor.transpose(pT[:, 0, 0:R], wts[:], K["ident"][0:R, 0:R])
                        if heads > 1:
                            mm = nc.tensor.transpose(pT[:, 0, P:P + R], wts2[:], K["ident"][0:R, 0:R])
                        mm.then_inc(wt_ps, 1)
                    if kind == SUM and old:
                        if heads > 1:
                            if g == 0:
                                start_sums()
                            if g % LOADED == 0:
                                load_lasts(g)
                        if g:
                            add_up(g - 1)
                    if kind == SUMS_END and old:
                        add_up(G - 1)

            rounds(pe, one_round)

        @block.scalar
        def _(sc):
            def one_round(new, mid, old):
                for kind, g in events:
                    if kind == SPREAD and new:
                        sc.wait_ge(mt_ps, new.before + g + 1)
                        wait_from(sc, spread, new.before + g - 3)
                        nc.scalar.copy(MT[:, g % 4, :], pMT[:, g % 2, 0:P]).then_inc(mt_ok, 1)
                    if kind == EXP and mid:
                        sc.wait_ge(diff_ok, mid.no + 1)
                        ins = nc.scalar.activation(wts[:], S[:], ACT.Exp)
                        if heads > 1:
                            ins = nc.scalar.activation(raw2[:], S2[:], ACT.Exp)
                        ins.then_inc(wts_ok if heads == 1 else exp_ok, 1)
                    if kind == TURN and mid:
                        sc.wait_ge(fac_ps, mid.no + 1)
                        nc.scalar.activation(fac[:], p_fac, ACT.Exp).then_inc(fac_ok, 1)
                    if kind == SUM and old:
                        if g == 0:
                            sc.wait_ge(wtT_ok, old.no + 1)
                        sc.wait_ge(sum_ps, old.before + g - 3 + AHEAD)
                        x = X[:, old.slot, g, :]
                        if heads == 1:
                            nc.scalar.activation(aX[:, g % 4, :], x, ACT.Copy,
                                                 scale=wtT[:, old.slot, g:g + 1]).then_inc(ax_ok, 1)
                            continue
                        for h in range(HA):
                            ins = nc.scalar.activation(aX[:, g % 4, h * D:(h + 1) * D], x[:, 0:D], ACT.Copy,
                                                       scale=wtT[:, old.slot, h * G + g:h * G + g + 1])
                        ins.then_inc(ax_ok, 1)

            rounds(sc, one_round)

        @block.vector
        def _(v):
            then_c = Links(v, link_c, chain_steps)
            if heads == 1:
                nc.vector.memset(X[:, :, :, D + 1:DA], 1.0)
            nc.vector.memset(gsum[:], 0.0)
            nc.vector.memset(run_b[:], -BIG)
            if heads == 1:
                nc.vector.memset(node_sums[:], 0.0).then_inc(closed, 2)
            else:
                nc.vector.memset(zeros[:], 0.0)
                nc.vector.memset(total[:, 0:sum_w], 0.0).then_inc(closed, 2)
            nc.vector.memset(carry[:], -BIG)
            v.nop(nofuse=True).then_inc(gates_free, SLOTS)
            nc.vector.memset(run[:], -BIG).then_inc(sum_ps, AHEAD)
            v.nop(nofuse=True).then_inc(stored, 64)
            v.wait_ge(small_ok, 1 + heads)
            v.wait_ge(sum_ps, AHEAD)

            def chain(mid):
                b = mid.slot
                then = then_c.later
                at_end, at_start = slice(31, 32), slice(0, 1)
                gate_f, gate_b, mask = (gates[:, b, n * P:(n + 1) * P] for n in range(3))
                first_place, inner = (gates[:, b, 3 * P + n:3 * P + n + 1] for n in range(2))
                old, new = carry[:, (b - 1) % SLOTS, :], carry[:, b, :]
                v.wait_ge(gates_in[b], mid.use * (16 * heads) + 16 * heads)
                nc.vector.tensor_tensor(gsum[:, 31:32], inner, gate_f[:, 0:1], ALU.add)
                yield from then(nc.vector.tensor_tensor(gsum[:, 32:33], inner, gate_b[:, P - 1:P], ALU.add))
                yield from then(nc.vector.transpose(gsumT[:], gsum[:]))
                yield from then(nc.vector.tensor_tensor(inj[:], old, gsumT[:, 0:32:G], ALU.add))
                nc.vector.memset(gsumT[:, 32 + G - 1:64:G], -BIG)
                yield from then(nc.vector.memset(gsumT[:, 0:32:G], -BIG))
                v.wait_ge(score_ps, mid.no + 1)
                if heads > 1:
                    nc.vector.tensor_tensor(S2[:], pT[0:R, 0, P:2 * P], mask, ALU.add)
                yield from then(nc.vector.tensor_tensor(S[:], pT[0:R, 0, 0:P], mask, ALU.add))
                if heads > 1:
                    yield from then(nc.vector.tensor_tensor(raw[:], S[:], S2[:], ALU.max))
                T0 = raw if heads > 1 else S
                yield from then(nc.vector.tensor_tensor_scan(fwd[:], gate_f, T0[:], -BIG, ALU.add, ALU.max))
                yield from then(nc.vector.transpose(ends[:], fwd[:, P - 32:P]))
                yield from then(nc.vector.tensor_tensor(ends[:, 0:32:G], ends[:, 0:32:G], inj[:], ALU.max))
                yield from then(nc.vector.tensor_tensor_scan(run[:, 1:33], gsumT[:, 0:32], ends[:], -BIG, ALU.add,
                                                             ALU.max))
                yield from then(nc.vector.tensor_copy(new, run[:, G:33:G]))
                yield from then(nc.vector.tensor_copy(run[:, 0:32:G], old))
                yield from then(nc.vector.transpose(cin[:], run[:, 0:32]))
                yield from then(nc.vector.tensor_tensor_scan(fwd2[:], gate_f, T0[:], cin[:, at_end], ALU.add, ALU.max))
                yield from then(nc.vector.tensor_tensor_scan(bwd[:, ::-1], gate_b[:, ::-1], fwd2[:, ::-1], -BIG,
                                                             ALU.add, ALU.max))
                yield from then(nc.vector.transpose(ends_b[:], bwd[:, 0:32]))
                yield from then(nc.vector.tensor_tensor_scan(run_b[:, 31::-1], gsumT[:, 63:31:-1], ends_b[:, ::-1],
                                                             -BIG, ALU.add, ALU.max))
                if heads > 1:
                    yield from then(nc.vector.memset(run_b[:, G:G + 1], -BIG))
                yield from then(nc.vector.transpose(bin_[:], run_b[:, 1:33]))
                yield from then(nc.vector.tensor_tensor_scan(top[:, ::-1], gate_b[:, ::-1], fwd2[:, ::-1],
                                                             bin_[:, at_start], ALU.add, ALU.max))
                if heads > 1:
                    nc.vector.tensor_tensor(S2[:], S2[:], top[:], ALU.subtract)
                nc.vector.tensor_tensor(S[:], S[:], top[:], ALU.subtract).then_inc(diff_ok, 1)
                yield from then(nc.vector.tensor_tensor(dlt[:], cin[:, at_end], top[:, 0:1], ALU.subtract))
                yield from then(nc.vector.scalar_tensor_tensor(out=dlt[:], in0=gate_f[:, 0:1], scalar=0.0,
                                                               in1=dlt[:], op0=ALU.is_equal, op1=ALU.mult))
                nc.vector.tensor_scalar(V[:], K["node_no"][0:R, :], first_place, dlt[:, 0:1], ALU.is_equal,
                                        ALU.mult).then_inc(v_ok, 1)

            def one_round(new, mid, old):
                if new:
                    k0, b = new.before, new.slot
                if old:
                    k1, o = old.before, old.slot
                lasts = []

                def load_rel(before, slot):
                    nc.vector.tensor_copy(rel[:, slot, :], K["rel"][:, bass.ds(before, G)]).then_inc(rel_ok, 1)

                def score_step(chunk, g):
                    v.wait_ge(spread, chunk.before + g + 1)
                    if g % Q == 0:
                        v.wait_ge(rows_in[chunk.slot][g // Q], chunk.use * (16 * Q) + 16 * Q)
                    if g >= 4:
                        v.wait_ge(read_e, chunk.before + g - 3)
                    nc.vector.tensor_tensor_reduce(
                        out=junk[:, g % 4, :], in0=pE[:, g % 2, 0:DA], in1=X[:, chunk.slot, g, :], scale=1.0, scalar=0.0,
                        op0=ALU.mult, op1=ALU.add, accum_out=score[:, g:g + 1]).then_inc(read_e, 1)

                def scale():
                    until(v, fac_ok, old.no + 1)
                    if heads == 1:
                        nc.vector.tensor_tensor(kfac[:], keep[:, o, 0:1], fac[:], ALU.mult).then_inc(kfac_ok, 1)
                        until(v, kfac_ok, old.no + 1)
                        return
                    v.wait_ge(sum_ps, k1 + AHEAD)
                    v.wait_ge(closed, k1 + 2)
                    nc.vector.tensor_tensor(carried[:, 0:HD].rearrange("p (h d) -> p h d", h=H),
                                            total[:, 0:HD].rearrange("p (h d) -> p h d", h=H),
                                            fac[:].unsqueeze(2).to_broadcast([P, H, D]), ALU.mult)
                    nc.vector.tensor_tensor(carried[:, HD:WC].rearrange("p (a h) -> p a h", h=H),
                                            total[:, HD:WC].rearrange("p (a h) -> p a h", h=H),
                                            fac[:].unsqueeze(1).to_broadcast([P, 2, H]), ALU.mult).then_inc(scaled, 1)

                def add(g):
                    v.wait_ge(sum_ps, k1 + g + 1 + AHEAD)
                    v.wait_ge(closed, k1 + g + 2)
                    v.wait_ge(stored, (k1 + g + 1) * 16)
                    nc.vector.scalar_tensor_tensor(
                        out=node_sums[:, g % 4, :], in0=node_sums[:, (g - 1) % 4, :],
                        scalar=keep[:, o, g:g + 1] if g else kfac[:], in1=pS[:, g % 2, 0:sum_w], op0=ALU.mult,
                        op1=ALU.add).then_inc(closed, 1)

                def close(g):
                    if g % LOADED == 0:
                        _, loaded = nc.values_load_multi_w_load_instructions(
                            K["last_int"][0:1, bass.ds(k1 + g, LOADED)], engines=[DVE_ENGINE], min_val=0, max_val=1,
                            skip_runtime_bounds_check_because="a flag")
                        lasts.extend(loaded)
                    with v.If(lasts[g] > 0):
                        v.wait_ge(closed, k1 + g + 2)
                        v.wait_ge(sum_ps, k1 + g + 1 + AHEAD)
                        v.wait_ge(stored, (k1 + g + 1) * 16)
                        ins = nc.vector.tensor_copy(node_sums[:, g % 4, :], total[:, 0:sum_w])
                        if g < G - 1:
                            ins.then_inc(closed, 1)
                        else:
                            ins.then_inc(copied, 1)
                            v.wait_ge(copied, old.no + 1)
                            nc.vector.memset(total[:, 0:sum_w], 0.0).then_inc(closed, 1)
                    with v.Else():
                        v.wait_ge(closed, k1 + g + 2)
                        if g == G - 1:
                            v.nop(nofuse=True).then_inc(copied, 1)
                        v.nop(nofuse=True).then_inc(closed, 1)

                def one_hot(before, slot, g):
                    if g % Q == 0 and old:
                        v.wait_ge(sum_ps, before - SLOTS * G + g + Q + AHEAD)
                    nc.vector.tensor_scalar(M[:, slot, g, :], K["node_no"][:], rel[:, slot, g:g + 1], None,
                                            ALU.is_equal).then_inc(m_ok, 1)

                def weigh(g):
                    v.wait_ge(sum_ps, k1 + g - 3 + AHEAD)
                    nc.vector.tensor_tensor(
                        aX[:, g % 4, HA * D:HD].rearrange("p (h d) -> p h d", d=D),
                        X[:, o, g, 0:D].unsqueeze(1).to_broadcast([P, H - HA, D]),
                        wtT[:, o, HA * G + g:R:G].unsqueeze(2).to_broadcast([P, H - HA, D]),
                        ALU.mult).then_inc(ax_dve, 1)

                if mid:
                    steps = chain(mid)
                    then_c.start(mid.no)
                if new and isinstance(new.no, int) and new.no == 0:
                    load_rel(0, 0)
                    v.wait_ge(rel_ok, 1)
                    for n in range(FIRST[heads]):
                        one_hot(0, 0, n)
                for kind, g in events:
                    if kind == SPREAD and new:
                        for n in range(FIRST[heads] if g == 0 else max(g + M_AHEAD[heads], FIRST[heads]),
                                       min(g + M_AHEAD[heads] + 1, G)):
                            one_hot(k0, b, n)
                        if heads == 1 and g >= 3:
                            if g == 3 and mid:
                                v.wait_ge(score_ps, mid.no + 1)
                            score_step(new, g - 3)
                    if kind == SCALE:
                        if old:
                            scale()
                        if new and heads == 1:
                            if old:
                                v.wait_ge(sum_ps, k1 + AHEAD)
                            nc.vector.tensor_copy(keep[:, b, :], K["keep"][:, bass.ds(k0, G)])
                            nc.vector.tensor_copy(X[:, b, :, D], K["w"][:, bass.ds(k0, G)]).then_inc(w_ok, 1)
                            v.wait_ge(w_ok, new.no + 1)
                    if kind == COLUMNS and new and not (isinstance(new.no, int) and new.no == chunks - 1):
                        load_rel(new.before + G, (b + 1) % SLOTS)
                    if kind == SUM and old:
                        if heads > 1:
                            weigh(g)
                            if g:
                                close(g - 1)
                        elif g >= 2:
                            add(g - 2)
                    if kind == SUMS_END and old:
                        if heads > 1:
                            close(G - 1)
                        else:
                            add(G - 2)
                            add(G - 1)
                    if kind == SPREAD_END and new:
                        if heads == 1:
                            score_step(new, G - 3)
                        if not (isinstance(new.no, int) and new.no == chunks - 1):
                            v.wait_ge(rel_ok, new.no + 2)
                            for n in range(FIRST[heads]):
                                one_hot(k0 + G, (b + 1) % SLOTS, n)
                    if kind == SCORE and mid:
                        if heads == 1:
                            score_step(mid, G - 2)
                            score_step(mid, G - 1)
                            until(v, read_e, mid.before + G)
                            v.nop(nofuse=True).then_inc(score_ok, 1)
                        else:
                            v.wait_ge(spread, mid.before + G)
                            for q in range(G // Q):
                                v.wait_ge(rows_in[mid.slot][q], mid.use * (16 * Q) + 16 * Q)
                            e3 = pE[:, 0, 0:G * 2 * heads].rearrange("p (g w) -> p g w", w=2 * heads)
                            s3 = score[:].rearrange("p (h g) -> p g h", g=G)
                            nc.vector.tensor_copy(score2[:].rearrange("p (h g) -> p g h", g=G), e3[:, :, heads:])
                            nc.vector.tensor_tensor(s3, e3[:, :, 0:heads], X[:, mid.slot, :, D:D + heads],
                                                    ALU.add).then_inc(read_e, 1)
                            v.wait_ge(read_e, mid.no + 1)
                            nc.vector.scalar_tensor_tensor(out=score[:], in0=score[:], scalar=SLOPE, in1=score[:],
                                                           op0=ALU.mult, op1=ALU.max).then_inc(score_ok, 1)
                    if kind == CHAIN and mid:
                        next(steps, None)
                    if kind == EXP and mid:
                        for _ in steps:
                            pass
                        then_c.end()
                    if kind == OWN and mid and heads > 1:
                        v.wait_ge(exp_ok, mid.no + 1)
                        nc.vector.scalar_tensor_tensor(out=wts2[:], in0=gates[:, mid.slot, P:2 * P], scalar=0.0,
                                                       in1=raw2[:], op0=ALU.not_equal,
                                                       op1=ALU.mult).then_inc(wts_ok, 1)
                    if kind == COLUMNS and mid:
                        until(v, wt_ps, mid.no + 1)
                        v.nop(nofuse=True).then_inc(gates_free, 1)
                        columns = wtT[:, mid.slot, :].rearrange("p (a r) -> p a r", a=kinds)
                        turned = pT[:, 0, 0:kinds * P].rearrange("p (a r) -> p a r", a=kinds)[:, :, 0:R]
                        nc.vector.tensor_copy(columns, turned).then_inc(wtT_ok, 1)
                        until(v, wtT_ok, mid.no + 1)

            rounds(v, one_round)


CHAIN_STEPS = {1: 20, H: 22}
M_AHEAD = {1: 0, H: 3}
FIRST = {1: 2, H: 4}
CHAIN_END = {1: 26, H: 12}


PAIRS = NG // 2
BOTH = (0, 1)


def pair_loop(engine):
    return engine.Fori(0, PAIRS)


def group_rows(tensor, i, b):
    return tensor[bass.ds((i * 2 + b) * (GT * P), GT * P), :].rearrange("(t p) w -> p t w", p=P)


def load_groups(engine, loads):
    for b in BOTH:
        for buffer, tensor, arrived, _, _ in loads:
            engine.dma_start(buffer[:, b], tensor[b * GT * P:(b + 1) * GT * P, :]
                             .rearrange("(t p) w -> p t w", p=P)).then_inc(arrived[b], 16)
    with engine.Fori(0, PAIRS - 1) as i:
        for b in BOTH:
            for buffer, tensor, arrived, used, count in loads:
                until(engine, used, (i * 2 + b + 1) * count)
                engine.dma_start(buffer[:, b], group_rows(tensor, i + 1, b)).then_inc(arrived[b], 16)


CUTS = ((0, 512), (512, GT * P))


def table_phase(nc, K, x_d, wq, bq, wk_t, tab_d):
    with ExitStack() as ctx:
        T = Tools(nc, ctx, "tab")
        x = T.sb("x", [P, 2, GT, D])
        xT = T.sb("xT", [D, 2, GT * P])
        qT = T.sb("qT", [D, 2, GT * P])
        out = T.sb("out", [P, 2, GT, DA])
        pA = [T.ps(f"pA{b}", [P, 1024]) for b in BOTH]
        pB = [T.ps(f"pB{b}", [P, 1024]) for b in BOTH]
        stored = [T.sem(f"stored{b}") for b in BOTH]
        x_in = [T.sem(f"x_in{b}") for b in BOTH]
        xT_ps, xT_ok, q_ps, q_ok, t_ps, t_ok = (T.sem(n) for n in ("xT_ps", "xT_ok", "q_ps", "q_ok", "t_ps", "t_ok"))
        block = ctx.enter_context(nc.Block())

        @block.gpsimd
        def _(pool):
            load_groups(pool, [(x, x_d, x_in, xT_ps, 1)])

        @block.tensor
        def _(pe):
            with pair_loop(pe) as i:
                for b in BOTH:
                    until(pe, x_in[b], i * 16 + 16)
                    until(pe, t_ok, i * 2 + b + 1)
                    for t in range(GT):
                        mm = nc.tensor.transpose(pA[b][0:D, t * P:(t + 1) * P], x[:, b, t, :], K["ident"][:])
                    mm.then_inc(xT_ps, 1)
                for b in BOTH:
                    until(pe, xT_ok, i * 2 + b + 1)
                    for lo, hi in CUTS:
                        mm = nc.tensor.matmul(pB[b][0:D, lo:hi], wq, xT[:, b, lo:hi], start=True, stop=True)
                    mm.then_inc(q_ps, 1)
                for b in BOTH:
                    until(pe, q_ok, i * 2 + b + 1)
                    for t in range(GT):
                        mm = nc.tensor.matmul(pA[b][:, t * DA:(t + 1) * DA], qT[:, b, t * P:(t + 1) * P], wk_t,
                                              start=True, stop=True)
                    mm.then_inc(t_ps, 1)

        @block.scalar
        def _(sc):
            with pair_loop(sc) as i:
                for b in BOTH:
                    sc.wait_ge(xT_ps, i * 2 + b + 1)
                    nc.scalar.copy(xT[:, b, :], pA[b][0:D, 0:GT * P]).then_inc(xT_ok, 1)
                for b in BOTH:
                    sc.wait_ge(q_ps, i * 2 + b + 1)
                    nc.scalar.activation(qT[:, b, :], pB[b][0:D, 0:GT * P], ACT.Identity, bias=bq).then_inc(q_ok, 1)

        @block.vector
        def _(v):
            for s in stored:
                v.nop(nofuse=True).then_inc(s, 16)
            v.nop(nofuse=True).then_inc(t_ok, 2)
            with pair_loop(v) as i:
                for b in BOTH:
                    v.wait_ge(t_ps, i * 2 + b + 1)
                    v.wait_ge(stored[b], i * 16 + 16)
                    nc.vector.tensor_scalar(out[:, b].rearrange("p t w -> p (t w)"), pA[b][:, 0:GT * DA],
                                            float(D) ** -0.5, None, ALU.mult).then_inc(t_ok, 1)

        @block.sync
        def _(sp):
            with pair_loop(sp) as i:
                for b in BOTH:
                    until(sp, t_ok, i * 2 + b + 1 + 2)
                    sp.dma_start(group_rows(tab_d, i, b), out[:, b]).then_inc(stored[b], 16)
            for s in stored:
                sp.wait_ge(s, 16 + 16 * PAIRS)


class Chain:

    def __init__(self, engine, sem, per_round):
        self.engine, self.sem, self.per_round, self.n, self.base = engine, sem, per_round, 0, 0
        self.before = None

    def start_round(self, i):
        if self.before is None:
            self.before = self.n
        self.n = self.before
        self.base = i * self.per_round

    def __call__(self, ins):
        self.n += 1
        ins.then_inc(self.sem, 1)
        self.engine.wait_ge(self.sem, self.base + self.n)

    def end_round(self):
        assert self.n - self.before == self.per_round, (self.n - self.before, self.per_round)


def spread_rows(x, shape):
    return x.unsqueeze(2).to_broadcast(shape)


def over_tiles(row):
    return row[:].unsqueeze(1).to_broadcast([P, GT, D])


def centre(v, then, x, sq, stat, var_ok):
    mean, var = stat[:, 0, :], stat[:, 1, :]
    then(v.tensor_reduce(mean, x, AX.X, ALU.add))
    then(v.tensor_scalar(mean, mean, -1.0 / D, None, ALU.mult))
    then(v.tensor_tensor(x, x, spread_rows(mean, [P, GT, D]), ALU.add))
    then(v.tensor_tensor(sq, x, x, ALU.mult))
    then(v.tensor_reduce(var, sq, AX.X, ALU.add))
    v.tensor_scalar(var, var, 1.0 / D, LN_EPS, ALU.mult, ALU.add).then_inc(var_ok, 1)


CENTRE_LINKS = 5


def divide(v, then, x, out, stat, std_ok, n):
    v.wait_ge(std_ok, n)
    then(v.reciprocal(stat[:, 3, :], stat[:, 2, :]))
    then(v.tensor_tensor(out, x, spread_rows(stat[:, 3, :], [P, GT, D]), ALU.mult))


DIVIDE_LINKS = 2


def normalise(v, nc, then, agg, rd, norm_ok):
    then(nc.vector.tensor_scalar(rd, agg[:, :, DA - 1], 0.5, None, ALU.max))
    then(nc.vector.reciprocal(rd, rd))
    nc.vector.tensor_tensor(agg, agg, spread_rows(rd, [P, GT, DA]), ALU.mult).then_inc(norm_ok, 1)


NORMALISE_LINKS = 2


def middle_phase(nc, K, W, sums_d, x_d, h_d, tab_d):
    with ExitStack() as ctx:
        T = Tools(nc, ctx, "mid")
        agg = T.sb("agg", [P, 2, GT, DA])
        x = T.sb("x", [P, 2, GT, D])
        rd = T.sb("rd", [P, 2, GT])
        aggT = T.sb("aggT", [DA, 2, GT * P])
        xT = T.sb("xT", [D, 2, GT * P])
        hT = T.sb("hT", [D, 2, GT * P])
        qT = T.sb("qT", [D, 2, GT * P])
        h = T.sb("h", [P, 2, GT, D])
        out = T.sb("out", [P, 2, GT, DA])
        pA = [T.ps(f"pA{b}", [P, 1024]) for b in BOTH]
        pB = [T.ps(f"pB{b}", [P, 1024]) for b in BOTH]
        stored = [T.sem(f"stored{b}") for b in BOTH]
        sums_in = [T.sem(f"sums_in{b}") for b in BOTH]
        x_in = [T.sem(f"x_in{b}") for b in BOTH]
        norm_ok, agg_ps, x_ps, aggT_ok, xT_ok, h_ps, h_ok, q_ps, q_ok, t_ps, t_ok, dve = (
            T.sem(n) for n in ("norm_ok", "agg_ps", "x_ps", "aggT_ok", "xT_ok", "h_ps", "h_ok", "q_ps",
                               "q_ok", "t_ps", "t_ok", "dve"))
        block = ctx.enter_context(nc.Block())

        @block.gpsimd
        def _(pool):
            load_groups(pool, [(agg, sums_d, sums_in, agg_ps, 1), (x, x_d, x_in, x_ps, 1)])

        @block.sync
        def _(sp):
            with pair_loop(sp) as i:
                for b in BOTH:
                    until(sp, t_ok, i * 2 + b + 1 + 2)
                    sp.dma_start(group_rows(tab_d, i, b), out[:, b]).then_inc(stored[b], 16)
                    sp.dma_start(group_rows(h_d, i, b), h[:, b]).then_inc(stored[b], 16)
            for s in stored:
                sp.wait_ge(s, 32 + 32 * PAIRS)

        @block.tensor
        def _(pe):
            with pair_loop(pe) as i:
                for b in BOTH:
                    until(pe, x_in[b], i * 16 + 16)
                    until(pe, t_ok, i * 2 + b + 1)
                    for t in range(GT):
                        mm = nc.tensor.transpose(pB[b][0:D, t * P:(t + 1) * P], x[:, b, t, :], K["ident"][:])
                    mm.then_inc(x_ps, 1)
                    until(pe, norm_ok, i * 2 + b + 1)
                    for t in range(GT):
                        mm = nc.tensor.transpose(pA[b][0:DA, t * P:(t + 1) * P], agg[:, b, t, :], K["ident"][:])
                    mm.then_inc(agg_ps, 1)
                for b in BOTH:
                    until(pe, xT_ok, i * 2 + b + 1)
                    until(pe, aggT_ok, i * 2 + b + 1)
                    for lo, hi in CUTS:
                        nc.tensor.matmul(pA[b][0:D, lo:hi], W["wva1"][:], aggT[:, b, lo:hi], start=True, stop=False)
                        mm = nc.tensor.matmul(pA[b][0:D, lo:hi], W["ws1"][:], xT[:, b, lo:hi], start=False, stop=True)
                    mm.then_inc(h_ps, 1)
                for b in BOTH:
                    until(pe, h_ok, i * 2 + b + 1)
                    for lo, hi in CUTS:
                        mm = nc.tensor.matmul(pB[b][0:D, lo:hi], W["wq2"][:], hT[:, b, lo:hi], start=True, stop=True)
                    mm.then_inc(q_ps, 1)
                    for t in range(GT):
                        nc.tensor.transpose(pA[b][:, t * D:(t + 1) * D], hT[:, b, t * P:(t + 1) * P],
                                            K["ident"][0:D, 0:D])
                for b in BOTH:
                    until(pe, q_ok, i * 2 + b + 1)
                    for t in range(GT):
                        mm = nc.tensor.matmul(pB[b][:, t * DA:(t + 1) * DA], qT[:, b, t * P:(t + 1) * P],
                                              W["wk_t2"][:], start=True, stop=True)
                    mm.then_inc(t_ps, 1)

        @block.scalar
        def _(sc):
            with pair_loop(sc) as i:
                for b in BOTH:
                    sc.wait_ge(x_ps, i * 2 + b + 1)
                    nc.scalar.copy(xT[:, b, :], pB[b][0:D, 0:GT * P]).then_inc(xT_ok, 1)
                for b in BOTH:
                    sc.wait_ge(h_ps, i * 2 + b + 1)
                    nc.scalar.activation(hT[:, b, :], pA[b][0:D, 0:GT * P], ACT.Relu,
                                         bias=W["bs1"][:]).then_inc(h_ok, 1)
                for b in BOTH:
                    sc.wait_ge(q_ps, i * 2 + b + 1)
                    nc.scalar.activation(qT[:, b, :], pB[b][0:D, 0:GT * P], ACT.Identity,
                                         bias=W["bq2"][:]).then_inc(q_ok, 1)

        @block.vector
        def _(v):
            for s in stored:
                v.nop(nofuse=True).then_inc(s, 32)
            v.nop(nofuse=True).then_inc(t_ok, 2)
            then = Chain(v, dve, 2 * NORMALISE_LINKS)
            with pair_loop(v) as i:
                then.start_round(i)
                for b in BOTH:
                    v.wait_ge(sums_in[b], i * 16 + 16)
                    normalise(v, nc, then, agg[:, b], rd[:, b], norm_ok)
                for b in BOTH:
                    v.wait_ge(agg_ps, i * 2 + b + 1)
                    nc.vector.tensor_copy(aggT[:, b, :], pA[b][0:DA, 0:GT * P]).then_inc(aggT_ok, 1)
                for b in BOTH:
                    v.wait_ge(t_ps, i * 2 + b + 1)
                    v.wait_ge(stored[b], i * 32 + 32)
                    nc.vector.tensor_copy(h[:, b].rearrange("p t w -> p (t w)"), pA[b][:, 0:GT * D])
                    nc.vector.tensor_scalar(out[:, b].rearrange("p t w -> p (t w)"), pB[b][:, 0:GT * DA],
                                            float(D) ** -0.5, None, ALU.mult).then_inc(t_ok, 1)
                then.end_round()


def second_phase(nc, K, W, sums_d, h_d, x_d, x1_d, tab_d):
    with ExitStack() as ctx:
        T = Tools(nc, ctx, "sec")
        agg = T.sb("agg", [P, 2, GT, DA])
        x = T.sb("x", [P, 2, GT, D])
        xb = T.sb("xb", [P, 2, GT, D])
        h = T.sb("h", [P, 2, GT, D])
        rd = T.sb("rd", [P, 2, GT])
        aggT = T.sb("aggT", [DA, 2, GT * P])
        hT = T.sb("hT", [D, 2, GT * P])
        y = T.sb("y", [P, 2, GT, D])
        sq = T.sb("sq", [P, 2, GT, D])
        stat = T.sb("stat", [P, 2, 4, GT])
        x1 = T.sb("x1", [P, 2, GT, D + H])
        x1T = T.sb("x1T", [D, 2, GT * P])
        out = T.sb("out", [P, 2, GT, 2 * H])
        pA = [T.ps(f"pA{b}", [P, 1024]) for b in BOTH]
        pB = [T.ps(f"pB{b}", [P, 1024]) for b in BOTH]
        stored = [T.sem(f"stored{b}") for b in BOTH]
        sums_in = [T.sem(f"sums_in{b}") for b in BOTH]
        x_in = [T.sem(f"x_in{b}") for b in BOTH]
        h_in = [T.sem(f"h_in{b}") for b in BOTH]
        norm_ok, agg_ps, h_ps, aggT_ok, hT_ok, xb_ok, y_ps, y_ok, x1_ok, x1_ps, x1T_ok, a_ps, t_ok, dve, var_ok, std_ok = (
            T.sem(n) for n in ("norm_ok", "agg_ps", "h_ps", "aggT_ok", "hT_ok", "xb_ok", "y_ps", "y_ok", "x1_ok",
                               "x1_ps", "x1T_ok", "a_ps", "t_ok", "dve", "var_ok", "std_ok"))
        block = ctx.enter_context(nc.Block())

        @block.gpsimd
        def _(pool):
            with pair_loop(pool) as i:
                for b in BOTH:
                    until(pool, y_ok, i * 2 + b + 1)
                    until(pool, x_in[b], i * 16 + 16)
                    nc.gpsimd.tensor_tensor(xb[:, b], x[:, b], over_tiles(W["bs2"]), ALU.add).then_inc(xb_ok, 1)

        @block.sync
        def _(sp):
            load_groups(sp, [(agg, sums_d, sums_in, agg_ps, 1), (h, h_d, h_in, h_ps, 1), (x, x_d, x_in, xb_ok, 1)])
            for s in stored:
                sp.wait_ge(s, 32 + 32 * PAIRS)

        @block.tensor
        def _(pe):
            with pair_loop(pe) as i:
                for b in BOTH:
                    until(pe, h_in[b], i * 16 + 16)
                    until(pe, t_ok, i * 2 + b + 1)
                    for t in range(GT):
                        mm = nc.tensor.transpose(pB[b][0:D, t * P:(t + 1) * P], h[:, b, t, :], K["ident"][:])
                    mm.then_inc(h_ps, 1)
                    until(pe, norm_ok, i * 2 + b + 1)
                    for t in range(GT):
                        mm = nc.tensor.transpose(pA[b][0:DA, t * P:(t + 1) * P], agg[:, b, t, :], K["ident"][:])
                    mm.then_inc(agg_ps, 1)
                for b in BOTH:
                    until(pe, hT_ok, i * 2 + b + 1)
                    until(pe, aggT_ok, i * 2 + b + 1)
                    for t in range(GT):
                        nc.tensor.matmul(pA[b][:, t * D:(t + 1) * D], aggT[:, b, t * P:(t + 1) * P], W["wva2"][:],
                                         start=True, stop=False)
                        mm = nc.tensor.matmul(pA[b][:, t * D:(t + 1) * D], hT[:, b, t * P:(t + 1) * P], W["ws2"][:],
                                              start=False, stop=True)
                    mm.then_inc(y_ps, 1)
                for b in BOTH:
                    until(pe, x1_ok, i * 2 + b + 1)
                    for t in range(GT):
                        mm = nc.tensor.transpose(pB[b][0:D, t * P:(t + 1) * P], x1[:, b, t, 0:D], K["ident"][:])
                    mm.then_inc(x1_ps, 1)
                for b in BOTH:
                    until(pe, x1T_ok, i * 2 + b + 1)
                    for t in range(GT):
                        mm = nc.tensor.matmul(pA[b][:, t * 2 * H:(t + 1) * 2 * H], x1T[:, b, t * P:(t + 1) * P],
                                              W["a_sd"][:], start=True, stop=True)
                    mm.then_inc(a_ps, 1)

        @block.scalar
        def _(sc):
            with pair_loop(sc) as i:
                for b in BOTH:
                    sc.wait_ge(h_ps, i * 2 + b + 1)
                    nc.scalar.copy(hT[:, b, :], pB[b][0:D, 0:GT * P]).then_inc(hT_ok, 1)
                for b in BOTH:
                    sc.wait_ge(var_ok, i * 2 + b + 1)
                    nc.scalar.activation(stat[:, b, 2, :], stat[:, b, 1, :], ACT.Sqrt).then_inc(std_ok, 1)
                for b in BOTH:
                    sc.wait_ge(x1_ps, i * 2 + b + 1)
                    nc.scalar.copy(x1T[:, b, :], pB[b][0:D, 0:GT * P]).then_inc(x1T_ok, 1)
                for b in BOTH:
                    until(sc, t_ok, i * 2 + b + 1 + 2)
                    sc.dma_start(group_rows(tab_d, i, b), out[:, b]).then_inc(stored[b], 16)
                    sc.dma_start(group_rows(x1_d, i, b), x1[:, b]).then_inc(stored[b], 16)

        @block.vector
        def _(v):
            for s in stored:
                v.nop(nofuse=True).then_inc(s, 32)
            v.nop(nofuse=True).then_inc(t_ok, 2)
            v.nop(nofuse=True).then_inc(y_ok, 2)
            then = Chain(v, dve, 2 * (NORMALISE_LINKS + CENTRE_LINKS + DIVIDE_LINKS + 3))
            with pair_loop(v) as i:
                then.start_round(i)
                for b in BOTH:
                    v.wait_ge(sums_in[b], i * 16 + 16)
                    normalise(v, nc, then, agg[:, b], rd[:, b], norm_ok)
                for b in BOTH:
                    v.wait_ge(agg_ps, i * 2 + b + 1)
                    nc.vector.tensor_copy(aggT[:, b, :], pA[b][0:DA, 0:GT * P]).then_inc(aggT_ok, 1)
                for b in BOTH:
                    v.wait_ge(y_ps, i * 2 + b + 1)
                    v.wait_ge(xb_ok, i * 2 + b + 1)
                    p3 = pA[b][:, 0:GT * D].rearrange("p (t w) -> p t w", w=D)
                    nc.vector.tensor_tensor(y[:, b], p3, xb[:, b], ALU.add).then_inc(y_ok, 1)
                    v.wait_ge(y_ok, i * 2 + b + 1 + 2)
                    centre(nc.vector, then, y[:, b], sq[:, b], stat[:, b], var_ok)
                for b in BOTH:
                    v.wait_ge(stored[b], i * 32 + 32)
                    divide(nc.vector, then, y[:, b], x1[:, b, :, 0:D], stat[:, b], std_ok, i * 2 + b + 1)
                    v.nop(nofuse=True).then_inc(x1_ok, 1)
                for b in BOTH:
                    v.wait_ge(a_ps, i * 2 + b + 1)
                    a3 = pA[b][:, 0:GT * 2 * H].rearrange("p (t w) -> p t w", w=2 * H)
                    then(nc.vector.tensor_copy(x1[:, b, :, D:], a3[:, :, 0:H]))
                    nc.vector.tensor_copy(out[:, b, :, 0:H], a3[:, :, H:])
                    then(nc.vector.tensor_tensor(out[:, b, :, H:], x1[:, b, :, D:], a3[:, :, H:], ALU.add))
                    then(nc.vector.scalar_tensor_tensor(out=out[:, b, :, H:], in0=out[:, b, :, H:], scalar=SLOPE,
                                                        in1=out[:, b, :, H:], op0=ALU.mult, op1=ALU.max))
                    v.nop(nofuse=True).then_inc(t_ok, 1)
                then.end_round()


def last_phase(nc, K, W, sums_d, x1_d, out_d):
    with ExitStack() as ctx:
        T = Tools(nc, ctx, "fin")
        agg = T.sb("agg", [P, 2, GT, WC])
        x1 = T.sb("x1", [P, 2, GT, D + H])
        x1_kept = T.sb("x1_kept", [P, 2, GT, D])
        x1b = T.sb("x1b", [P, 2, GT, D])
        own = T.sb("own", [P, 2, GT, H])
        den = T.sb("den", [P, 2, GT, H])
        ox = T.sb("ox", [P, 2, H, D])
        aggT = T.sb("aggT", [P, 2, GT, 4 * P])
        y = T.sb("y", [P, 2, GT, D])
        sq = T.sb("sq", [P, 2, GT, D])
        stat = T.sb("stat", [P, 2, 4, GT])
        z = T.sb("z", [P, 2, GT, D])
        zb = T.sb("zb", [P, 2, GT, D])
        zT = T.sb("zT", [D, 2, GT * P])
        hid = T.sb("hid", [P, 2, GT * P])
        out = T.sb("out", [P, 2, GT, D])
        pA = [T.ps(f"pA{b}", [P, 1024]) for b in BOTH]
        pB = [T.ps(f"pB{b}", [P, 1024]) for b in BOTH]
        stored = [T.sem(f"stored{b}") for b in BOTH]
        sums_in = [T.sem(f"sums_in{b}") for b in BOTH]
        x1_in = [T.sem(f"x1_in{b}") for b in BOTH]
        own_ok, ox_ok, loop_ok, prep_ok, norm_ok, agg_ps, aggT_ok, y_ps, y_ok, z_ok, zb_ok, z_ps, zT_ok, hid_ps = (
            T.sem(n) for n in ("own_ok", "ox_ok", "loop_ok", "prep_ok", "norm_ok", "agg_ps", "aggT_ok",
                               "y_ps", "y_ok", "z_ok", "zb_ok", "z_ps", "zT_ok", "hid_ps"))
        hid_ok, f_ps, f_ok, x1_done, o_ok, dve, var_ok, std_ok = (
            T.sem(n) for n in ("hid_ok", "f_ps", "f_ok", "x1_done", "o_ok", "dve", "var_ok", "std_ok"))
        block = ctx.enter_context(nc.Block())
        HD = H * D

        def groups_before(i, b):
            return i * 2 + b

        @block.gpsimd
        def _(pool):
            with pair_loop(pool) as i:
                for b in BOTH:
                    n = groups_before(i, b)
                    until(pool, x1_in[b], i * 16 + 16)
                    until(pool, own_ok, n + 1)
                    for t in range(GT):
                        nc.gpsimd.tensor_tensor(ox[:, t % 2], x1[:, b, t, 0:D].unsqueeze(1).to_broadcast([P, H, D]),
                                                own[:, b, t, :].unsqueeze(2).to_broadcast([P, H, D]),
                                                ALU.mult).then_inc(ox_ok, 1)
                        until(pool, ox_ok, n * GT + t + 1)
                        a3 = agg[:, b, t, 0:HD].rearrange("p (h d) -> p h d", d=D)
                        nc.gpsimd.tensor_tensor(a3, a3, ox[:, t % 2], ALU.add).then_inc(loop_ok, 1)
                    until(pool, loop_ok, n * GT + GT)
                for b in BOTH:
                    until(pool, x1_done, groups_before(i, b) + 1)
                    nc.gpsimd.tensor_tensor(x1b[:, b], x1[:, b, :, 0:D], over_tiles(W["bias_att"]), ALU.add)
                    nc.gpsimd.tensor_copy(x1_kept[:, b], x1[:, b, :, 0:D]).then_inc(prep_ok, 1)

        @block.sync
        def _(sp):
            load_groups(sp, [(x1, x1_d, x1_in, prep_ok, 1), (agg, sums_d, sums_in, agg_ps, GT)])
            for s in stored:
                sp.wait_ge(s, 16 + 16 * PAIRS)

        @block.tensor
        def _(pe):
            with pair_loop(pe) as i:
                for b in BOTH:
                    n = groups_before(i, b)
                    t0 = n * GT
                    until(pe, f_ok, n + 1)
                    for t in range(GT + 1):
                        if t < GT:
                            until(pe, norm_ok, t0 + t + 1)
                            if t >= 2:
                                until(pe, aggT_ok, t0 + t - 1)
                            for q in range(4):
                                mm = nc.tensor.transpose(pA[b][:, (t % 2) * 512 + q * P:(t % 2) * 512 + (q + 1) * P],
                                                         agg[:, b, t, q * P:(q + 1) * P], K["ident"][:])
                            mm.then_inc(agg_ps, 1)
                        if t:
                            until(pe, aggT_ok, t0 + t)
                            for q in range(4):
                                mm = nc.tensor.matmul(pB[b][:, (t - 1) * D:t * D], aggT[:, b, t - 1, q * P:(q + 1) * P],
                                                      W["watt2"][:, q, :], start=(q == 0), stop=(q == 3))
                    mm.then_inc(y_ps, 1)
                for b in BOTH:
                    until(pe, z_ok, groups_before(i, b) + 1)
                    for t in range(GT):
                        mm = nc.tensor.transpose(pA[b][0:D, t * P:(t + 1) * P], z[:, b, t, :], K["ident"][:])
                    mm.then_inc(z_ps, 1)
                for b in BOTH:
                    until(pe, zT_ok, groups_before(i, b) + 1)
                    for lo, hi in CUTS:
                        mm = nc.tensor.matmul(pB[b][:, lo:hi], W["w1"][:], zT[:, b, lo:hi], start=True, stop=True)
                    mm.then_inc(hid_ps, 1)
                for b in BOTH:
                    until(pe, hid_ok, groups_before(i, b) + 1)
                    for t in range(GT):
                        mm = nc.tensor.matmul(pA[b][:, t * D:(t + 1) * D], hid[:, b, t * P:(t + 1) * P], W["w2"][:],
                                              start=True, stop=True)
                    mm.then_inc(f_ps, 1)

        @block.scalar
        def _(sc):
            def root(b, n):
                sc.wait_ge(var_ok, n)
                nc.scalar.activation(stat[:, b, 2, :], stat[:, b, 1, :], ACT.Sqrt).then_inc(std_ok, 1)

            with pair_loop(sc) as i:
                for b in BOTH:
                    for t in range(GT):
                        sc.wait_ge(agg_ps, groups_before(i, b) * GT + t + 1)
                        nc.scalar.copy(aggT[:, b, t, :], pA[b][:, (t % 2) * 512:(t % 2) * 512 + 4 * P]).then_inc(aggT_ok, 1)
                for b in BOTH:
                    root(b, i * 6 + b + 1)
                for b in BOTH:
                    sc.wait_ge(z_ps, groups_before(i, b) + 1)
                    nc.scalar.copy(zT[:, b, :], pA[b][0:D, 0:GT * P]).then_inc(zT_ok, 1)
                for b in BOTH:
                    sc.wait_ge(hid_ps, groups_before(i, b) + 1)
                    nc.scalar.activation(hid[:, b, :], pB[b][:, 0:GT * P], ACT.Relu, bias=W["b1"][:]).then_inc(hid_ok, 1)
                for b in BOTH:
                    root(b, i * 6 + 2 + b + 1)
                for b in BOTH:
                    root(b, i * 6 + 4 + b + 1)
                for b in BOTH:
                    until(sc, o_ok, groups_before(i, b) + 1)
                    sc.dma_start(group_rows(out_d, i, b), out[:, b]).then_inc(stored[b], 16)

        @block.vector
        def _(v):
            for s in stored:
                v.nop(nofuse=True).then_inc(s, 16)
            v.nop(nofuse=True).then_inc(f_ok, 2)
            v.nop(nofuse=True).then_inc(x1_done, 2)
            then = Chain(v, dve, 2 * (5 + 3 * CENTRE_LINKS + 3 * DIVIDE_LINKS + 3))

            def denominators(use, b):
                v.wait_ge(sums_in[b], use * 16 + 16)
                sums = agg[:, b, :, HD:HD + H]
                d, o = den[:, b], own[:, b]
                then(nc.vector.tensor_tensor(d, sums, agg[:, b, :, HD + H:], ALU.add))
                then(nc.vector.scalar_tensor_tensor(out=o, in0=d, scalar=0.5, in1=agg[:, b, :, HD + H:],
                                                    op0=ALU.is_lt, op1=ALU.add))
                v.nop(nofuse=True).then_inc(own_ok, 1)
                then(nc.vector.tensor_tensor(d, sums, o, ALU.add))
                then(nc.vector.tensor_scalar(d, d, SM_EPS, float(H), ALU.add, ALU.mult))
                then(nc.vector.reciprocal(d, d))

            def pair(i, more):
                for b in BOTH:
                    for t in range(GT):
                        v.wait_ge(loop_ok, groups_before(i, b) * GT + t + 1)
                        a3 = agg[:, b, t, 0:HD].rearrange("p (h d) -> p h d", d=D)
                        nc.vector.tensor_tensor(a3, a3, den[:, b, t, :].unsqueeze(2).to_broadcast([P, H, D]),
                                                ALU.mult).then_inc(norm_ok, 1)
                for b in BOTH:
                    v.wait_ge(y_ps, groups_before(i, b) + 1)
                    v.wait_ge(prep_ok, groups_before(i, b) + 1)
                    y3 = pB[b][:, 0:GT * D].rearrange("p (t w) -> p t w", w=D)
                    nc.vector.tensor_tensor(y[:, b], y3, x1b[:, b], ALU.add).then_inc(y_ok, 1)
                    v.wait_ge(y_ok, groups_before(i, b) + 1)
                    centre(nc.vector, then, y[:, b], sq[:, b], stat[:, b], var_ok)
                for b in BOTH:
                    divide(nc.vector, then, y[:, b], z[:, b], stat[:, b], std_ok, i * 6 + b + 1)
                    then(nc.vector.tensor_tensor(z[:, b], z[:, b], over_tiles(W["ln1_g"]), ALU.mult))
                    nc.vector.tensor_tensor(z[:, b], z[:, b], over_tiles(W["ln1_b"]), ALU.add).then_inc(z_ok, 1)
                if more:
                    for b in BOTH:
                        denominators(i + 1, b)
                for b in BOTH:
                    v.wait_ge(z_ok, groups_before(i, b) + 1)
                    nc.vector.tensor_tensor(zb[:, b], z[:, b], over_tiles(W["b2"]), ALU.add).then_inc(zb_ok, 1)
                for b in BOTH:
                    v.wait_ge(f_ps, groups_before(i, b) + 1)
                    v.wait_ge(zb_ok, groups_before(i, b) + 1)
                    f3 = pA[b][:, 0:GT * D].rearrange("p (t w) -> p t w", w=D)
                    nc.vector.tensor_tensor(y[:, b], f3, zb[:, b], ALU.add).then_inc(f_ok, 1)
                    v.wait_ge(f_ok, groups_before(i, b) + 1 + 2)
                    centre(nc.vector, then, y[:, b], sq[:, b], stat[:, b], var_ok)
                for b in BOTH:
                    divide(nc.vector, then, y[:, b], y[:, b], stat[:, b], std_ok, i * 6 + 2 + b + 1)
                    then(nc.vector.tensor_tensor(y[:, b], y[:, b], over_tiles(W["ln2_g"]), ALU.mult))
                    then(nc.vector.tensor_tensor(y[:, b], y[:, b], over_tiles(W["ln2_b"]), ALU.add))
                    nc.vector.tensor_tensor(y[:, b], y[:, b], x1_kept[:, b], ALU.add).then_inc(x1_done, 1)
                    v.wait_ge(x1_done, groups_before(i, b) + 1 + 2)
                    centre(nc.vector, then, y[:, b], sq[:, b], stat[:, b], var_ok)
                for b in BOTH:
                    v.wait_ge(stored[b], i * 16 + 16)
                    divide(nc.vector, then, y[:, b], out[:, b], stat[:, b], std_ok, i * 6 + 4 + b + 1)
                    v.nop(nofuse=True).then_inc(o_ok, 1)

            for b in BOTH:
                denominators(0, b)
            with v.Fori(0, PAIRS - 1) as i:
                then.start_round(i)
                pair(i, True)
                then.end_round()
            then.start_round(PAIRS - 1)
            pair(PAIRS - 1, False)


def load_weights(nc, K, W, w):
    with ExitStack() as ctx:
        T = Tools(nc, ctx, "wgt")
        att = T.sb("att", [D, H, D])
        vec = T.sb("vec", [D, 2, H, D])
        prod = T.sb("prod", [D, H, D])
        stack = [T.sb(f"stack{n}", [DA, D]) for n in (0, 1)]
        turned = T.ps("turned", [D, 2, 512])
        loads = T.sem("loads")
        dve = T.sem("dve")
        turned_ok = T.sem("turned_ok")
        block = ctx.enter_context(nc.Block())
        row = lambda a: a.rearrange("(a d) -> a d", a=1)
        col = lambda a: a.rearrange("(d a) -> d a", a=1)
        copies = [(att[:], w["W_att"].rearrange("d (h c) -> d h c", h=H)),
                  (vec[:, 0], w["att_src"].partition_broadcast(D)), (vec[:, 1], w["att_dst"].partition_broadcast(D)),
                  (W["w1"][:], w["W1"]), (W["b1"][:], col(w["b1"])), (W["w2"][:], w["W2"])]
        for n in (1, 2):
            s = stack[n - 1]
            copies += [(s[0:D, :], w[f"Wk{n}"]), (s[D:D + 1, :], w[f"We{n}"]), (s[D + 1:DA, :], row(w[f"bk{n}"])),
                       (W[f"wva{n}"][0:D, :], w[f"Wv{n}"]), (W[f"wva{n}"][D:D + 1, :], w[f"We{n}"]),
                       (W[f"wva{n}"][D + 1:DA, :], row(w[f"bv{n}"])), (W[f"wq{n}"][:], w[f"Wq{n}"]),
                       (W[f"bq{n}"][:], col(w[f"bq{n}"])), (W[f"ws{n}"][:], w[f"Ws{n}"])]
        copies += [(W["bs1"][:], col(w["bs1"])), (W["bs2"][:], w["bs2"].partition_broadcast(P))]
        copies += [(W[n][:], w[n].partition_broadcast(P)) for n in ("bias_att", "b2", "ln1_g", "ln1_b", "ln2_g",
                                                                    "ln2_b")]
        by_pair = w["W_att"].rearrange("d (q a o) -> a d q o", a=2, o=D)
        copies += [(W["watt2"][a * D:(a + 1) * D, :, :], by_pair[a]) for a in (0, 1)]

        @block.sync
        def _(sp):
            for dst, src in copies:
                sp.dma_start(dst, src).then_inc(loads, 16)
            sp.wait_ge(loads, 16 * len(copies))

        @block.tensor
        def _(pe):
            until(pe, loads, 16 * len(copies))
            for n in (0, 1):
                mm = nc.tensor.transpose(turned[:, n, 0:DA], stack[n][:], K["ident"][0:DA, 0:DA])
            mm.then_inc(turned_ok, 1)

        @block.vector
        def _(v):
            v.wait_ge(loads, 16 * len(copies))
            for n in (0, 1):
                nc.vector.tensor_tensor(prod[:], att[:], vec[:, n], ALU.mult).then_inc(dve, 1)
                v.wait_ge(dve, 2 * n + 1)
                nc.vector.tensor_reduce(W["a_sd"][:, n * H:(n + 1) * H], prod[:], AX.X, ALU.add).then_inc(dve, 1)
                v.wait_ge(dve, 2 * n + 2)
            v.wait_ge(turned_ok, 1)
            for n in (1, 2):
                nc.vector.tensor_copy(W[f"wk_t{n}"][:], turned[:, n - 1, 0:DA])


WEIGHTS = ["Wq1", "bq1", "Wk1", "bk1", "Wv1", "bv1", "We1", "Ws1", "bs1", "Wq2", "bq2", "Wk2", "bk2", "Wv2", "bv2",
           "We2", "Ws2", "bs2"]
WEIGHTS_L1 = ["W_att", "att_src", "att_dst", "bias_att", "W1", "b1", "W2", "b2", "ln1_g", "ln1_b", "ln2_g", "ln2_b"]


def build(nc, x, src, dst, ew, w, out):
    def scratch(name, shape):
        return nc.dram_tensor(f"scratch_{name}", shape, F32, kind="Internal").ap()

    dram = {"dst_flat": scratch("dst_flat", (STEPS * P + P,)), "gates": scratch("gates", (STEPS, GATE_W))}
    tab1, tab2 = scratch("tab1", (N_PAD, DA)), scratch("tab2", (N_PAD, DA))
    tab3 = scratch("tab3", (N_PAD, 2 * H))
    sums1, sums2 = (scratch(f"sums{n}", (N_PAD, DA)) for n in (1, 2))
    sums3 = scratch("sums3", (N_PAD, WC))
    h, x1 = scratch("h", (N_PAD, D)), scratch("x1", (N_PAD, D + H))
    with ExitStack() as ctx:
        T = Tools(nc, ctx, "all")
        K = {"ident": T.sb("ident", [P, P]), "ones": T.sb("ones", [P, P]), "node_no": T.sb("node_no", [P, P]),
             "keep": T.sb("keep", [P, STEPS]), "j_int": T.sb("j_int", [1, STEPS], I32),
             "last_int": T.sb("last_int", [1, STEPS], I32),
             "src_idx": T.sb("src_idx", [P, STEPS], I32), "rel": T.sb("rel", [P, STEPS]), "w": T.sb("w", [P, STEPS])}
        W = {"w1": T.sb("w1", [D, 2 * D]), "b1": T.sb("b1", [2 * D, 1]), "w2": T.sb("w2", [2 * D, D]),
             "a_sd": T.sb("a_sd", [D, 2 * H]), "watt2": T.sb("watt2", [P, H // 2, D]), "bs1": T.sb("bs1", [D, 1])}
        for n in (1, 2):
            W |= {f"wk_t{n}": T.sb(f"wk_t{n}", [D, DA]), f"wva{n}": T.sb(f"wva{n}", [DA, D]),
                  f"wq{n}": T.sb(f"wq{n}", [D, D]), f"bq{n}": T.sb(f"bq{n}", [D, 1]), f"ws{n}": T.sb(f"ws{n}", [D, D])}
        for n in ("bs2", "bias_att", "b2", "ln1_g", "ln1_b", "ln2_g", "ln2_b"):
            W[n] = T.sb(n, [P, D])
        build_schedule(nc, K, src, dst, ew, dram)
        load_weights(nc, K, W, w)
        table_phase(nc, K, x, W["wq1"][:], W["bq1"][:], W["wk_t1"][:], tab1)
        edge_phase(nc, K, "e1", 1, x, D, tab1, DA, dram, sums1)
        middle_phase(nc, K, W, sums1, x, h, tab2)
        edge_phase(nc, K, "e2", 1, h, D, tab2, DA, dram, sums2)
        second_phase(nc, K, W, sums2, h, x, x1, tab3)
        edge_phase(nc, K, "e3", H, x1, D + H, tab3, 2 * H, dram, sums3)
        last_phase(nc, K, W, sums3, x1, out)


def lay_out(inputs):
    import numpy as np

    def edges(a, fill):
        a = np.ascontiguousarray(a).reshape(-1)
        return np.concatenate([a, np.full(E_PAD - E, fill, a.dtype)]).reshape(-1, P)

    x = np.ascontiguousarray(inputs["x"])
    arrays = {"x": np.concatenate([x, np.zeros((N_PAD - N, D), x.dtype)]), "src": edges(inputs["src"], 0),
              "dst": edges(inputs["dst"], NODE_PAD), "ew": edges(inputs["edge_weight1"], 0)}
    for n in WEIGHTS:
        arrays["w_" + n] = np.ascontiguousarray(inputs["L0_gnn_" + n])
    for n in WEIGHTS_L1:
        arrays["w_" + n] = np.ascontiguousarray(inputs["L1_gnn_" + n])
    return arrays


def kernel(**inputs):
    import concourse.bacc as bacc
    from concourse.bass_utils import run_bass_kernel_spmd

    arrays = lay_out(inputs)
    nc = bacc.Bacc("TRN2", target_bir_lowering=False, num_devices=1)
    t = {n: nc.dram_tensor(n, a.shape, mybir.dt.from_np(a.dtype), kind="ExternalInput").ap()
         for n, a in arrays.items()}
    out = nc.dram_tensor("out", (N_PAD, D), F32, kind="ExternalOutput").ap()
    build(nc, t["x"], t["src"], t["dst"], t["ew"], {n: t["w_" + n] for n in WEIGHTS + WEIGHTS_L1}, out)
    r = run_bass_kernel_spmd(nc, [arrays], core_ids=[0])
    return r.results[0]["out"][:N]
```
